# Optimizing a Trainium2 kernel written in Bass

```python
import numpy as np
import jax
import jax.numpy as jnp

def _softmax(x, axis=-1):
    return jax.nn.softmax(x, axis=axis)

def _gelu(x):
    return jax.nn.gelu(x, approximate=True)

def _silu(x):
    return jax.nn.silu(x)

def _sigmoid(x):
    return jax.nn.sigmoid(x)

def _layernorm(x, axis=-1, eps=1e-05):
    m = jnp.mean(x, axis=axis, keepdims=True)
    v = jnp.var(x, axis=axis, keepdims=True)
    return (x - m) / jnp.sqrt(v + eps)

def _scatter_add(tgt, idx, src, axis=0):
    return tgt.at[idx].add(src)

def _segment_sum(src, seg, n):
    return jax.ops.segment_sum(src, seg, n)
kernel_name = 'mk_perceiver_d2_seqx_r4_c846f5'

def setup_inputs(seed: int=0):
    np.random.seed(seed)
    _w = jnp.asarray

    def _rec_inputs():
        import jax
        import jax.numpy as jnp
        _rk = jax.random.key(seed)
        x = -0.0002928 + 1 * jax.random.normal(jax.random.fold_in(_rk, 1), (4, 256, 256), jnp.float32)
        _lenS = 256 - jax.random.randint(jax.random.fold_in(_rk, 7), (4,), 0, max(1, 256 // 4) + 1, jnp.int32)
        _lenS2 = 4096 - jax.random.randint(jax.random.fold_in(_rk, 8), (4,), 0, max(1, 4096 // 4) + 1, jnp.int32)
        _ctx_1024P = jax.random.normal(jax.random.fold_in(_rk, 11), (4, 16, 256), jnp.float32)
        _ctx_1024c = jax.random.dirichlet(jax.random.fold_in(_rk, 511), 0.3 * jnp.ones((16,), jnp.float32), (4, 4096))
        _ctx_1024t = jnp.einsum('bsk,bkd->bsd', _ctx_1024c, _ctx_1024P)
        _ctx_1024t = _ctx_1024t * jax.lax.rsqrt(jnp.mean(jnp.square(_ctx_1024t)) + 1e-12) * 0.953939
        ctx_1024 = -1.39393e-06 + 0.999914 * (_ctx_1024t + 0.3 * jax.random.normal(jax.random.fold_in(_rk, 611), (4, 4096, 256), jnp.float32))
        return (x, ctx_1024)
    x, ctx_1024 = _rec_inputs()

    def _L0_xattn_setup():
        import jax, jax.numpy as jnp
        import numpy as np
        D_MODEL = 256
        NUM_HEADS = 16
        D_K = D_MODEL // NUM_HEADS

        def _split_heads(x):
            B, S, _ = x.shape
            return x.reshape(B, S, NUM_HEADS, D_K).transpose(0, 2, 1, 3)
        key = jax.random.key(seed)
        ks = jax.random.split(key, 11)
        B, S, D = (2, 512, D_MODEL)
        scale = 1.0 / np.sqrt(D)
        inp = {'queries': jax.random.normal(ks[0], (B, S, D), jnp.float32), 'keys': jax.random.normal(ks[1], (B, S, D), jnp.float32), 'values': jax.random.normal(ks[2], (B, S, D), jnp.float32), 'w_q': jax.random.normal(ks[3], (D, D), jnp.float32) * scale, 'b_q': jnp.zeros((D,), jnp.float32), 'w_k': jax.random.normal(ks[4], (D, D), jnp.float32) * scale, 'b_k': jnp.zeros((D,), jnp.float32), 'w_v': jax.random.normal(ks[5], (D, D), jnp.float32) * scale, 'b_v': jnp.zeros((D,), jnp.float32), 'w_o': jax.random.normal(ks[6], (D, D), jnp.float32) * scale, 'b_o': jnp.zeros((D,), jnp.float32)}
        return inp
    _L0_xattn_all = _L0_xattn_setup()
    _L0_xattn_in = {k: v for k, v in _L0_xattn_all.items() if k in ('w_q', 'b_q', 'w_k', 'b_k', 'w_v', 'b_v', 'w_o', 'b_o')}
    del _L0_xattn_all

    def _L0_attn_setup():
        import jax, jax.numpy as jnp
        import numpy as np
        import math
        D_MODEL = 256
        NUM_HEADS = 16
        HEAD_DIM = D_MODEL // NUM_HEADS
        B, S = (2, 512)

        def _causal_attn(q, k, v):
            scale = 1.0 / math.sqrt(q.shape[-1])
            scores = jnp.einsum('bthd,bshd->bhts', q, k) * scale
            t = q.shape[1]
            mask = jnp.tril(jnp.ones((t, t), dtype=bool))
            scores = jnp.where(mask, scores, -jnp.inf)
            attn = jax.nn.softmax(scores, axis=-1)
            return jnp.einsum('bhts,bshd->bthd', attn, v)
        key = jax.random.key(seed)
        ks = jax.random.split(key, 7)
        sc = 0.02
        return {'x': jax.random.normal(ks[0], (B, S, D_MODEL), dtype=jnp.float32), 'Wqkv_w': jax.random.normal(ks[1], (3 * D_MODEL, D_MODEL), dtype=jnp.float32) * sc, 'Wqkv_b': jnp.zeros((3 * D_MODEL,), dtype=jnp.float32), 'conv_w': jax.random.normal(ks[2], (D_MODEL, D_MODEL, 3), dtype=jnp.float32) * sc, 'conv_b': jnp.zeros((D_MODEL,), dtype=jnp.float32), 'out_w': jax.random.normal(ks[3], (D_MODEL, D_MODEL), dtype=jnp.float32) * sc, 'out_b': jnp.zeros((D_MODEL,), dtype=jnp.float32)}
    _L0_attn_all = _L0_attn_setup()
    _L0_attn_in = {k: v for k, v in _L0_attn_all.items() if k in ('Wqkv_w', 'Wqkv_b', 'conv_w', 'conv_b', 'out_w', 'out_b')}
    del _L0_attn_all

    def _L0_ffn_setup():
        import jax, jax.numpy as jnp
        import numpy as np
        DIM = 256
        DEPTH = 6
        HEADS = 16
        DIM_HEAD = 64
        WINDOW = 64
        INNER = HEADS * DIM_HEAD
        DIM_INNER = int(DIM * 4 * 2 / 3)
        QK_SCALE = 8.0

        def shift_tokens(t):
            a, s = jnp.split(t, 2, -1)
            s = jnp.pad(s, ((0, 0), (1, 0), (0, 0)))[:, :-1]
            return jnp.concatenate([a, s], -1)

        def l2norm(t):
            return t / jnp.maximum(jnp.linalg.norm(t, axis=-1, keepdims=True), 1e-12)

        def rotate_half(x):
            x1, x2 = jnp.split(x, 2, -1)
            return jnp.concatenate([-x2, x1], -1)

        def rotary_tables(n):
            half = jnp.arange(0, DIM_HEAD, 2, dtype=jnp.float32)
            inv_freq = 1.0 / 10000.0 ** (half / DIM_HEAD)
            t = jnp.arange(n, dtype=jnp.float32)
            freqs = t[:, None] * inv_freq[None, :]
            freqs = jnp.concatenate([freqs, freqs], -1)
            base_scale = (half + 0.4 * DIM_HEAD) / (1.4 * DIM_HEAD)
            power = (t - n // 2) / (WINDOW // 2)
            scale = base_scale[None, :] ** power[:, None]
            scale = jnp.concatenate([scale, scale], -1)
            return (freqs, scale)

        def local_attention(q, k, v):
            b, h, n, d = q.shape
            w = WINDOW
            nw = n // w
            bq = q.reshape(b, h, nw, w, d)
            bk = k.reshape(b, h, nw, w, d)
            bv = v.reshape(b, h, nw, w, d)

            def look(t):
                p = jnp.pad(t, ((0, 0), (0, 0), (1, 0), (0, 0), (0, 0)))
                return jnp.concatenate([p[:, :, :nw], p[:, :, 1:]], axis=3)
            bk2, bv2 = (look(bk), look(bv))
            seq = jnp.arange(n).reshape(nw, w)
            seq_p = jnp.pad(seq, ((1, 0), (0, 0)), constant_values=-1)
            jt = jnp.concatenate([seq_p[:nw], seq_p[1:]], axis=1)
            it = seq[:, :, None]
            jb = jt[:, None, :]
            mask = (it < jb) | (it > jb + w) | (jb == -1)
            sim = jnp.einsum('bhwie,bhwje->bhwij', bq, bk2) * QK_SCALE
            sim = jnp.where(mask, -jnp.finfo(sim.dtype).max, sim)
            attn = jax.nn.softmax(sim, -1)
            out = jnp.einsum('bhwij,bhwje->bhwie', attn, bv2)
            return out.reshape(b, h, n, d)

        def attn_layer(x, Wqkv, qs, ksc, Wo):
            b, n, _ = x.shape
            qkv = x @ Wqkv
            q, k, v = jnp.split(qkv, 3, -1)
            sh = lambda t: t.reshape(b, n, HEADS, DIM_HEAD).transpose(0, 2, 1, 3)
            q, k, v = (sh(q), sh(k), sh(v))
            q = l2norm(q) * qs
            k = l2norm(k) * ksc
            freqs, scale = rotary_tables(n)
            cos, sin = (jnp.cos(freqs), jnp.sin(freqs))
            q = q * cos * scale + rotate_half(q) * sin * scale
            inv = 1.0 / scale
            k = k * cos * inv + rotate_half(k) * sin * inv
            out = local_attention(q, k, v)
            out = out.transpose(0, 2, 1, 3).reshape(b, n, INNER)
            return out @ Wo

        def ffn_layer(x, g, bln, W1, b1, W2, b2):
            mu = x.mean(-1, keepdims=True)
            var = ((x - mu) ** 2).mean(-1, keepdims=True)
            xn = (x - mu) / jnp.sqrt(var + 1e-05) * g + bln
            hg = xn @ W1 + b1
            a, gate = jnp.split(hg, 2, -1)
            return a * jax.nn.gelu(gate, approximate=False) @ W2 + b2
        key = jax.random.key(seed)
        ks = jax.random.split(key, 8)
        B, N = (2, 512)
        init = lambda k, shape: jax.random.normal(k, shape, jnp.float32) * 0.02
        return {'x': jax.random.normal(ks[0], (B, N, DIM), jnp.float32), 'Wqkv': init(ks[1], (DEPTH, DIM, 3 * INNER)), 'q_scale': jnp.ones((DEPTH, DIM_HEAD), jnp.float32), 'k_scale': jnp.ones((DEPTH, DIM_HEAD), jnp.float32), 'Wo': init(ks[2], (DEPTH, INNER, DIM)), 'ln_g': jnp.ones((DEPTH, DIM), jnp.float32), 'ln_b': jnp.zeros((DEPTH, DIM), jnp.float32), 'W1': init(ks[3], (DEPTH, DIM, 2 * DIM_INNER)), 'b1': jnp.zeros((DEPTH, 2 * DIM_INNER), jnp.float32), 'W2': init(ks[4], (DEPTH, DIM_INNER, DIM)), 'b2': jnp.zeros((DEPTH, DIM), jnp.float32)}
    _L0_ffn_all = _L0_ffn_setup()
    _L0_ffn_in = {k: v for k, v in _L0_ffn_all.items() if k in ('Wqkv', 'q_scale', 'k_scale', 'Wo', 'ln_g', 'ln_b', 'W1', 'b1', 'W2', 'b2')}
    del _L0_ffn_all

    def _L1_xattn_setup():
        import jax, jax.numpy as jnp
        import numpy as np
        D_MODEL = 256
        NUM_HEADS = 16
        HEAD_DIM = D_MODEL // NUM_HEADS
        SCALE = HEAD_DIM ** (-0.5)
        key = jax.random.key(seed)
        ks = jax.random.split(key, 8)
        B, Nq, Nk = (2, 512, 512)
        s = D_MODEL ** (-0.5)
        return {'query': jax.random.normal(ks[0], (B, Nq, D_MODEL), jnp.float32), 'key': jax.random.normal(ks[1], (B, Nk, D_MODEL), jnp.float32), 'value': jax.random.normal(ks[2], (B, Nk, D_MODEL), jnp.float32), 'Wq': jax.random.normal(ks[3], (D_MODEL, D_MODEL), jnp.float32) * s, 'Wk': jax.random.normal(ks[4], (D_MODEL, D_MODEL), jnp.float32) * s, 'Wv': jax.random.normal(ks[5], (D_MODEL, D_MODEL), jnp.float32) * s, 'Wo': jax.random.normal(ks[6], (D_MODEL, D_MODEL), jnp.float32) * s, 'bo': jnp.zeros((D_MODEL,), jnp.float32)}
    _L1_xattn_all = _L1_xattn_setup()
    _L1_xattn_in = {k: v for k, v in _L1_xattn_all.items() if k in ('Wq', 'Wk', 'Wv', 'Wo', 'bo')}
    del _L1_xattn_all

    def _L1_attn_setup():
        import jax, jax.numpy as jnp
        import numpy as np
        from jax import lax
        H = 16
        D_CONV = 4
        NORMALIZER = 16.0
        EPS = 1e-05

        def _causal_conv_silu(x, w):
            B, L, D = x.shape
            xp = jnp.pad(x, ((0, 0), (D_CONV - 1, 0), (0, 0)))
            y = sum((xp[:, k:k + L, :] * w[:, k] for k in range(D_CONV)))
            return jax.nn.silu(y)

        def _gla_scan(q, k, v, gk):
            B, h, L, dk = q.shape
            dv = v.shape[-1]
            qT = jnp.moveaxis(q, 2, 0)
            kT = jnp.moveaxis(k, 2, 0)
            vT = jnp.moveaxis(v, 2, 0)
            gT = jnp.moveaxis(gk, 2, 0)

            def step(S, inp):
                qt, kt, vt, gt = inp
                S = S * jnp.exp(gt)[..., None] + kt[..., None] * vt[..., None, :]
                ot = jnp.einsum('bhk,bhkv->bhv', qt, S)
                return (S, ot)
            S0 = jnp.zeros((B, h, dk, dv), q.dtype)
            S, o = lax.scan(step, S0, (qT, kT, vT, gT))
            return (jnp.moveaxis(o, 0, 2), S)

        def _reference_tuple_inner(x, conv_w, Wq, Wkg, Wv, Wg, bg, Wout, aug_balance):
            xb = jnp.swapaxes(x, 0, 1)
            xb = _causal_conv_silu(xb, conv_w)
            q = xb @ Wq
            k_gate = xb @ Wkg
            v = xb @ Wv
            g = xb @ Wg + bg
            gk = jax.nn.log_sigmoid(k_gate) / NORMALIZER
            k = 1.0 - jnp.exp(gk)
            B, L, _ = q.shape
            split = lambda t: t.reshape(B, L, H, -1).transpose(0, 2, 1, 3)
            qh, kh, gkh, vh = (split(q), split(k), split(gk), split(v))
            dk = qh.shape[-1]
            o, new_state = _gla_scan(qh * dk ** (-0.5), kh, vh, gkh)
            aug = aug_balance.reshape(H, dk)
            aug_w = jnp.einsum('bhlk,hk,bhlk->bhl', qh, aug, kh)
            o = o + jax.nn.sigmoid(aug_w[..., None] * vh)
            mu = o.mean(-1, keepdims=True)
            var = o.var(-1, keepdims=True)
            o = (o - mu) * lax.rsqrt(var + EPS)
            o = o.transpose(0, 2, 1, 3).reshape(B, L, -1)
            out = jax.nn.silu(g) * o @ Wout
            return (jnp.swapaxes(out, 0, 1), new_state)
        key = jax.random.key(seed)
        ks = jax.random.split(key, 9)
        L, B, D = (2048, 8, 256)
        s = lambda fan: 1.0 / np.sqrt(fan)
        return {'x': jax.random.normal(ks[0], (L, B, D), jnp.float32), 'conv_w': jax.random.normal(ks[1], (D, D_CONV), jnp.float32) * s(D_CONV), 'Wq': jax.random.normal(ks[2], (D, D // 2), jnp.float32) * s(D), 'Wkg': jax.random.normal(ks[3], (D, D // 2), jnp.float32) * s(D), 'Wv': jax.random.normal(ks[4], (D, D), jnp.float32) * s(D), 'Wg': jax.random.normal(ks[5], (D, D), jnp.float32) * s(D), 'bg': jax.random.normal(ks[6], (D,), jnp.float32) * 0.02, 'Wout': jax.random.normal(ks[7], (D, D), jnp.float32) * s(D), 'aug_balance': jnp.zeros((D // 2,), jnp.float32)}
    _L1_attn_all = _L1_attn_setup()
    _L1_attn_in = {k: v for k, v in _L1_attn_all.items() if k in ('conv_w', 'Wq', 'Wkg', 'Wv', 'Wg', 'bg', 'Wout', 'aug_balance')}
    del _L1_attn_all

    def _L1_ffn_setup():
        import jax, jax.numpy as jnp
        import numpy as np
        B, S, H, I = (2, 512, 256, 128)
        E, K, G, TG = (64, 8, 8, 4)
        SCALE = 2.5
        CAP = 256
        key = jax.random.key(seed)
        ks = jax.random.split(key, 6)
        hidden_states = jax.random.normal(ks[0], (B, S, H), jnp.float32)
        gate_w = jax.random.normal(ks[1], (E, H), jnp.float32) * 0.02
        gate_bias = jax.random.normal(ks[2], (E,), jnp.float32) * 0.02
        w_gate = jax.random.normal(ks[3], (E, H, I), jnp.float32) * (1.0 / np.sqrt(H))
        w_up = jax.random.normal(ks[4], (E, H, I), jnp.float32) * (1.0 / np.sqrt(H))
        w_down = jax.random.normal(ks[5], (E, I, H), jnp.float32) * (1.0 / np.sqrt(I))
        return {'hidden_states': hidden_states, 'gate_w': gate_w, 'gate_bias': gate_bias, 'w_gate': w_gate, 'w_up': w_up, 'w_down': w_down}
    _L1_ffn_all = _L1_ffn_setup()
    _L1_ffn_in = {k: v for k, v in _L1_ffn_all.items() if k in ('gate_w', 'gate_bias', 'w_gate', 'w_up', 'w_down')}
    del _L1_ffn_all
    return {'x': x, 'ctx_1024': ctx_1024, 'L0_xattn_w_q': _L0_xattn_in['w_q'], 'L0_xattn_b_q': _L0_xattn_in['b_q'], 'L0_xattn_w_k': _L0_xattn_in['w_k'], 'L0_xattn_b_k': _L0_xattn_in['b_k'], 'L0_xattn_w_v': _L0_xattn_in['w_v'], 'L0_xattn_b_v': _L0_xattn_in['b_v'], 'L0_xattn_w_o': _L0_xattn_in['w_o'], 'L0_xattn_b_o': _L0_xattn_in['b_o'], 'L0_attn_Wqkv_w': _L0_attn_in['Wqkv_w'], 'L0_attn_Wqkv_b': _L0_attn_in['Wqkv_b'], 'L0_attn_conv_w': _L0_attn_in['conv_w'], 'L0_attn_conv_b': _L0_attn_in['conv_b'], 'L0_attn_out_w': _L0_attn_in['out_w'], 'L0_attn_out_b': _L0_attn_in['out_b'], 'L0_ffn_Wqkv': _L0_ffn_in['Wqkv'], 'L0_ffn_q_scale': _L0_ffn_in['q_scale'], 'L0_ffn_k_scale': _L0_ffn_in['k_scale'], 'L0_ffn_Wo': _L0_ffn_in['Wo'], 'L0_ffn_ln_g': _L0_ffn_in['ln_g'], 'L0_ffn_ln_b': _L0_ffn_in['ln_b'], 'L0_ffn_W1': _L0_ffn_in['W1'], 'L0_ffn_b1': _L0_ffn_in['b1'], 'L0_ffn_W2': _L0_ffn_in['W2'], 'L0_ffn_b2': _L0_ffn_in['b2'], 'L1_xattn_Wq': _L1_xattn_in['Wq'], 'L1_xattn_Wk': _L1_xattn_in['Wk'], 'L1_xattn_Wv': _L1_xattn_in['Wv'], 'L1_xattn_Wo': _L1_xattn_in['Wo'], 'L1_xattn_bo': _L1_xattn_in['bo'], 'L1_attn_conv_w': _L1_attn_in['conv_w'], 'L1_attn_Wq': _L1_attn_in['Wq'], 'L1_attn_Wkg': _L1_attn_in['Wkg'], 'L1_attn_Wv': _L1_attn_in['Wv'], 'L1_attn_Wg': _L1_attn_in['Wg'], 'L1_attn_bg': _L1_attn_in['bg'], 'L1_attn_Wout': _L1_attn_in['Wout'], 'L1_attn_aug_balance': _L1_attn_in['aug_balance'], 'L1_ffn_gate_w': _L1_ffn_in['gate_w'], 'L1_ffn_gate_bias': _L1_ffn_in['gate_bias'], 'L1_ffn_w_gate': _L1_ffn_in['w_gate'], 'L1_ffn_w_up': _L1_ffn_in['w_up'], 'L1_ffn_w_down': _L1_ffn_in['w_down']}

def reference(x, ctx_1024, L0_xattn_w_q, L0_xattn_b_q, L0_xattn_w_k, L0_xattn_b_k, L0_xattn_w_v, L0_xattn_b_v, L0_xattn_w_o, L0_xattn_b_o, L0_attn_Wqkv_w, L0_attn_Wqkv_b, L0_attn_conv_w, L0_attn_conv_b, L0_attn_out_w, L0_attn_out_b, L0_ffn_Wqkv, L0_ffn_q_scale, L0_ffn_k_scale, L0_ffn_Wo, L0_ffn_ln_g, L0_ffn_ln_b, L0_ffn_W1, L0_ffn_b1, L0_ffn_W2, L0_ffn_b2, L1_xattn_Wq, L1_xattn_Wk, L1_xattn_Wv, L1_xattn_Wo, L1_xattn_bo, L1_attn_conv_w, L1_attn_Wq, L1_attn_Wkg, L1_attn_Wv, L1_attn_Wg, L1_attn_bg, L1_attn_Wout, L1_attn_aug_balance, L1_ffn_gate_w, L1_ffn_gate_bias, L1_ffn_w_gate, L1_ffn_w_up, L1_ffn_w_down):
    import jax
    import jax.numpy as jnp

    def _L0_xattn_ref(queries, keys, values, w_q, b_q, w_k, b_k, w_v, b_v, w_o, b_o):
        import jax, jax.numpy as jnp
        import numpy as np
        D_MODEL = 256
        NUM_HEADS = 16
        D_K = D_MODEL // NUM_HEADS

        def _split_heads(x):
            B, S, _ = x.shape
            return x.reshape(B, S, NUM_HEADS, D_K).transpose(0, 2, 1, 3)
        q = _split_heads(queries @ w_q.T + b_q)
        k = _split_heads(keys @ w_k.T + b_k)
        v = _split_heads(values @ w_v.T + b_v)
        scores = jnp.einsum('bhqd,bhkd->bhqk', q, k) / jnp.sqrt(jnp.asarray(D_K, q.dtype))
        weights = jax.nn.softmax(scores, axis=-1)
        attn = jnp.einsum('bhqk,bhkd->bhqd', weights, v)
        B, H, S, dk = attn.shape
        merged = attn.transpose(0, 2, 1, 3).reshape(B, S, H * dk)
        return merged @ w_o.T + b_o

    def _L0_attn_ref(x, Wqkv_w, Wqkv_b, conv_w, conv_b, out_w, out_b):
        import jax, jax.numpy as jnp
        import numpy as np
        import math
        D_MODEL = 256
        NUM_HEADS = 16
        HEAD_DIM = D_MODEL // NUM_HEADS
        B, S = (2, 512)

        def _causal_attn(q, k, v):
            scale = 1.0 / math.sqrt(q.shape[-1])
            scores = jnp.einsum('bthd,bshd->bhts', q, k) * scale
            t = q.shape[1]
            mask = jnp.tril(jnp.ones((t, t), dtype=bool))
            scores = jnp.where(mask, scores, -jnp.inf)
            attn = jax.nn.softmax(scores, axis=-1)
            return jnp.einsum('bhts,bshd->bthd', attn, v)
        b, s, d = x.shape
        qkv = x @ Wqkv_w.T + Wqkv_b
        qkv = qkv.reshape(b, s, 3, NUM_HEADS, HEAD_DIM)
        q, k, v = (qkv[:, :, 0], qkv[:, :, 1], qkv[:, :, 2])
        ctx = _causal_attn(q, k, v)
        ctx_c = ctx.reshape(b, s, d).transpose(0, 2, 1)
        conv_out = jax.lax.conv_general_dilated(ctx_c, conv_w, window_strides=(1,), padding=[(1, 1)], dimension_numbers=('NCH', 'OIH', 'NCH')) + conv_b[None, :, None]
        q2 = conv_out.transpose(0, 2, 1).reshape(b, s, NUM_HEADS, HEAD_DIM)
        ctx2 = _causal_attn(q2, k, v)
        out = ctx2.reshape(b, s, d) @ out_w.T + out_b
        return out

    def _L0_ffn_ref(x, Wqkv, q_scale, k_scale, Wo, ln_g, ln_b, W1, b1, W2, b2):
        import jax, jax.numpy as jnp
        import numpy as np
        DIM = 256
        DEPTH = 6
        HEADS = 16
        DIM_HEAD = 64
        WINDOW = 64
        INNER = HEADS * DIM_HEAD
        DIM_INNER = int(DIM * 4 * 2 / 3)
        QK_SCALE = 8.0

        def shift_tokens(t):
            a, s = jnp.split(t, 2, -1)
            s = jnp.pad(s, ((0, 0), (1, 0), (0, 0)))[:, :-1]
            return jnp.concatenate([a, s], -1)

        def l2norm(t):
            return t / jnp.maximum(jnp.linalg.norm(t, axis=-1, keepdims=True), 1e-12)

        def rotate_half(x):
            x1, x2 = jnp.split(x, 2, -1)
            return jnp.concatenate([-x2, x1], -1)

        def rotary_tables(n):
            half = jnp.arange(0, DIM_HEAD, 2, dtype=jnp.float32)
            inv_freq = 1.0 / 10000.0 ** (half / DIM_HEAD)
            t = jnp.arange(n, dtype=jnp.float32)
            freqs = t[:, None] * inv_freq[None, :]
            freqs = jnp.concatenate([freqs, freqs], -1)
            base_scale = (half + 0.4 * DIM_HEAD) / (1.4 * DIM_HEAD)
            power = (t - n // 2) / (WINDOW // 2)
            scale = base_scale[None, :] ** power[:, None]
            scale = jnp.concatenate([scale, scale], -1)
            return (freqs, scale)

        def local_attention(q, k, v):
            b, h, n, d = q.shape
            w = WINDOW
            nw = n // w
            bq = q.reshape(b, h, nw, w, d)
            bk = k.reshape(b, h, nw, w, d)
            bv = v.reshape(b, h, nw, w, d)

            def look(t):
                p = jnp.pad(t, ((0, 0), (0, 0), (1, 0), (0, 0), (0, 0)))
                return jnp.concatenate([p[:, :, :nw], p[:, :, 1:]], axis=3)
            bk2, bv2 = (look(bk), look(bv))
            seq = jnp.arange(n).reshape(nw, w)
            seq_p = jnp.pad(seq, ((1, 0), (0, 0)), constant_values=-1)
            jt = jnp.concatenate([seq_p[:nw], seq_p[1:]], axis=1)
            it = seq[:, :, None]
            jb = jt[:, None, :]
            mask = (it < jb) | (it > jb + w) | (jb == -1)
            sim = jnp.einsum('bhwie,bhwje->bhwij', bq, bk2) * QK_SCALE
            sim = jnp.where(mask, -jnp.finfo(sim.dtype).max, sim)
            attn = jax.nn.softmax(sim, -1)
            out = jnp.einsum('bhwij,bhwje->bhwie', attn, bv2)
            return out.reshape(b, h, n, d)

        def attn_layer(x, Wqkv, qs, ksc, Wo):
            b, n, _ = x.shape
            qkv = x @ Wqkv
            q, k, v = jnp.split(qkv, 3, -1)
            sh = lambda t: t.reshape(b, n, HEADS, DIM_HEAD).transpose(0, 2, 1, 3)
            q, k, v = (sh(q), sh(k), sh(v))
            q = l2norm(q) * qs
            k = l2norm(k) * ksc
            freqs, scale = rotary_tables(n)
            cos, sin = (jnp.cos(freqs), jnp.sin(freqs))
            q = q * cos * scale + rotate_half(q) * sin * scale
            inv = 1.0 / scale
            k = k * cos * inv + rotate_half(k) * sin * inv
            out = local_attention(q, k, v)
            out = out.transpose(0, 2, 1, 3).reshape(b, n, INNER)
            return out @ Wo

        def ffn_layer(x, g, bln, W1, b1, W2, b2):
            mu = x.mean(-1, keepdims=True)
            var = ((x - mu) ** 2).mean(-1, keepdims=True)
            xn = (x - mu) / jnp.sqrt(var + 1e-05) * g + bln
            hg = xn @ W1 + b1
            a, gate = jnp.split(hg, 2, -1)
            return a * jax.nn.gelu(gate, approximate=False) @ W2 + b2
        for i in range(DEPTH):
            x = attn_layer(shift_tokens(x), Wqkv[i], q_scale[i], k_scale[i], Wo[i]) + x
            x = ffn_layer(shift_tokens(x), ln_g[i], ln_b[i], W1[i], b1[i], W2[i], b2[i]) + x
        return x

    def _L1_xattn_ref(query, key, value, Wq, Wk, Wv, Wo, bo):
        import jax, jax.numpy as jnp
        import numpy as np
        D_MODEL = 256
        NUM_HEADS = 16
        HEAD_DIM = D_MODEL // NUM_HEADS
        SCALE = HEAD_DIM ** (-0.5)
        B, Nq, C = query.shape
        Nk = key.shape[1]
        H, Dh = (NUM_HEADS, HEAD_DIM)
        q = (query @ Wq.T).reshape(B, Nq, H, Dh).transpose(0, 2, 1, 3)
        k = (key @ Wk.T).reshape(B, Nk, H, Dh).transpose(0, 2, 1, 3)
        v = (value @ Wv.T).reshape(B, Nk, H, Dh).transpose(0, 2, 1, 3)
        sim = jnp.einsum('bhqd,bhkd->bhqk', q, k) * SCALE
        attn = jax.nn.softmax(sim, axis=-1)
        out = jnp.einsum('bhqk,bhkd->bhqd', attn, v)
        out = out.transpose(0, 2, 1, 3).reshape(B, Nq, C)
        return out @ Wo.T + bo

    def _L1_attn_ref(x, conv_w, Wq, Wkg, Wv, Wg, bg, Wout, aug_balance):
        import jax, jax.numpy as jnp
        import numpy as np
        from jax import lax
        H = 16
        D_CONV = 4
        NORMALIZER = 16.0
        EPS = 1e-05

        def _causal_conv_silu(x, w):
            B, L, D = x.shape
            xp = jnp.pad(x, ((0, 0), (D_CONV - 1, 0), (0, 0)))
            y = sum((xp[:, k:k + L, :] * w[:, k] for k in range(D_CONV)))
            return jax.nn.silu(y)

        def _gla_scan(q, k, v, gk):
            B, h, L, dk = q.shape
            dv = v.shape[-1]
            qT = jnp.moveaxis(q, 2, 0)
            kT = jnp.moveaxis(k, 2, 0)
            vT = jnp.moveaxis(v, 2, 0)
            gT = jnp.moveaxis(gk, 2, 0)

            def step(S, inp):
                qt, kt, vt, gt = inp
                S = S * jnp.exp(gt)[..., None] + kt[..., None] * vt[..., None, :]
                ot = jnp.einsum('bhk,bhkv->bhv', qt, S)
                return (S, ot)
            S0 = jnp.zeros((B, h, dk, dv), q.dtype)
            S, o = lax.scan(step, S0, (qT, kT, vT, gT))
            return (jnp.moveaxis(o, 0, 2), S)

        def _reference_tuple_inner(x, conv_w, Wq, Wkg, Wv, Wg, bg, Wout, aug_balance):
            xb = jnp.swapaxes(x, 0, 1)
            xb = _causal_conv_silu(xb, conv_w)
            q = xb @ Wq
            k_gate = xb @ Wkg
            v = xb @ Wv
            g = xb @ Wg + bg
            gk = jax.nn.log_sigmoid(k_gate) / NORMALIZER
            k = 1.0 - jnp.exp(gk)
            B, L, _ = q.shape
            split = lambda t: t.reshape(B, L, H, -1).transpose(0, 2, 1, 3)
            qh, kh, gkh, vh = (split(q), split(k), split(gk), split(v))
            dk = qh.shape[-1]
            o, new_state = _gla_scan(qh * dk ** (-0.5), kh, vh, gkh)
            aug = aug_balance.reshape(H, dk)
            aug_w = jnp.einsum('bhlk,hk,bhlk->bhl', qh, aug, kh)
            o = o + jax.nn.sigmoid(aug_w[..., None] * vh)
            mu = o.mean(-1, keepdims=True)
            var = o.var(-1, keepdims=True)
            o = (o - mu) * lax.rsqrt(var + EPS)
            o = o.transpose(0, 2, 1, 3).reshape(B, L, -1)
            out = jax.nn.silu(g) * o @ Wout
            return (jnp.swapaxes(out, 0, 1), new_state)
        return _reference_tuple_inner(x, conv_w, Wq, Wkg, Wv, Wg, bg, Wout, aug_balance)[0]

    def _L1_ffn_ref(hidden_states, gate_w, gate_bias, w_gate, w_up, w_down):
        import jax, jax.numpy as jnp
        import numpy as np
        B, S, H, I = (2, 512, 256, 128)
        E, K, G, TG = (64, 8, 8, 4)
        SCALE = 2.5
        CAP = 256
        b, s, h = hidden_states.shape
        x = hidden_states.reshape(-1, h)
        n = x.shape[0]
        logits = x.astype(jnp.float32) @ gate_w.astype(jnp.float32).T
        scores = jax.nn.sigmoid(logits)
        sfc = scores + gate_bias[None, :]
        group_scores = jax.lax.top_k(sfc.reshape(n, G, E // G), 2)[0].sum(-1)
        gidx = jax.lax.top_k(group_scores, TG)[1]
        gmask = jnp.zeros((n, G), bool).at[jnp.arange(n)[:, None], gidx].set(True)
        smask = jnp.repeat(gmask, E // G, axis=1)
        tmp = jnp.where(smask, sfc, -jnp.inf)
        topk_idx = jax.lax.top_k(tmp, K)[1]
        topk_w = jnp.take_along_axis(scores, topk_idx, axis=1)
        topk_w = topk_w / (topk_w.sum(-1, keepdims=True) + 1e-20)
        topk_w = topk_w * SCALE
        e = topk_idx.reshape(-1)
        token = jnp.repeat(jnp.arange(n), K)
        oh = jax.nn.one_hot(e, E, dtype=jnp.int32)
        pos = jnp.take_along_axis(jnp.cumsum(oh, 0) - 1, e[:, None], 1)[:, 0]
        valid = pos < CAP
        pos_c = jnp.where(valid, pos, CAP)
        buf = jnp.zeros((E, CAP + 1, h), x.dtype).at[e, pos_c].set(x[token])[:, :CAP]
        g = jnp.einsum('ech,ehi->eci', buf, w_gate)
        u = jnp.einsum('ech,ehi->eci', buf, w_up)
        y = jnp.einsum('eci,eih->ech', jax.nn.silu(g) * u, w_down)
        y_slots = y[e, jnp.minimum(pos, CAP - 1)]
        w_slot = topk_w.reshape(-1) * valid.astype(topk_w.dtype)
        out = jnp.zeros((n, h), jnp.float32).at[token].add(y_slots * w_slot[:, None])
        return out.reshape(b, s, h)
    x = x + _L0_xattn_ref(_layernorm(x, axis=-1), ctx_1024, ctx_1024, L0_xattn_w_q, L0_xattn_b_q, L0_xattn_w_k, L0_xattn_b_k, L0_xattn_w_v, L0_xattn_b_v, L0_xattn_w_o, L0_xattn_b_o)
    x = x + _L0_attn_ref(_layernorm(x, axis=-1), L0_attn_Wqkv_w, L0_attn_Wqkv_b, L0_attn_conv_w, L0_attn_conv_b, L0_attn_out_w, L0_attn_out_b)
    x = x + _L0_ffn_ref(_layernorm(x, axis=-1), L0_ffn_Wqkv, L0_ffn_q_scale, L0_ffn_k_scale, L0_ffn_Wo, L0_ffn_ln_g, L0_ffn_ln_b, L0_ffn_W1, L0_ffn_b1, L0_ffn_W2, L0_ffn_b2)
    x = x + _L1_xattn_ref(_layernorm(x, axis=-1), ctx_1024, ctx_1024, L1_xattn_Wq, L1_xattn_Wk, L1_xattn_Wv, L1_xattn_Wo, L1_xattn_bo)
    x = x + _L1_attn_ref(_layernorm(x, axis=-1), L1_attn_conv_w, L1_attn_Wq, L1_attn_Wkg, L1_attn_Wv, L1_attn_Wg, L1_attn_bg, L1_attn_Wout, L1_attn_aug_balance)
    x = x + _L1_ffn_ref(_layernorm(x, axis=-1), L1_ffn_gate_w, L1_ffn_gate_bias, L1_ffn_w_gate, L1_ffn_w_up, L1_ffn_w_down)
    return x

_drawn_inputs = setup_inputs


def setup_inputs(seed=0):
    import zlib

    import numpy as np

    out = dict(_drawn_inputs(seed))
    spreads = {'L0_xattn_b_q': (0.0, 0.1),
     'L0_xattn_b_k': (0.0, 2.0),
     'L0_xattn_b_v': (0.0, 0.1),
     'L0_xattn_b_o': (0.0, 0.1),
     'L0_attn_Wqkv_b': (0.0, 0.1),
     'L0_attn_conv_b': (0.0, 2.0),
     'L0_attn_out_b': (0.0, 0.1),
     'L0_ffn_q_scale': (1.0, 0.6),
     'L0_ffn_k_scale': (1.0, 0.6),
     'L0_ffn_ln_g': (1.0, 0.564),
     'L0_ffn_ln_b': (0.0, 0.415),
     'L0_ffn_b1': (0.0, 0.1),
     'L0_ffn_b2': (0.0, 0.1),
     'L1_xattn_bo': (0.0, 0.1),
     'L1_attn_aug_balance': (0.0, 0.392)}
    factors = {'L0_attn_conv_w': 29.193, 'L1_attn_bg': 4.411}
    for name, (base, spread) in spreads.items():
        noise = np.random.default_rng([zlib.crc32(name.encode()), seed]).standard_normal(out[name].shape)
        drawn = base * np.exp(spread * noise) if base else spread * noise
        out[name] = jnp.asarray(drawn.astype(out[name].dtype))
    for name, factor in factors.items():
        out[name] = (out[name] * factor).astype(out[name].dtype)
    return out
```

```python
from contextlib import ExitStack

import numpy as np

import concourse.bass as bass
from concourse import mybir

F32 = mybir.dt.float32
BF16 = mybir.dt.bfloat16
ALU = mybir.AluOpType
ACT = mybir.ActivationFunctionType
AX = mybir.AxisListType

P = 128
B, S, D = 4, 256, 256
N = B * S
NT = N // P
KC = D // P
H = 16
SK = 4096
LN_EPS = 1e-5
NEG = -1e30


class Mark:

    def __init__(self, sem, value):
        self.sem, self.value = sem, value


def flat(marks):
    for m in marks:
        if m is None:
            continue
        if isinstance(m, Mark):
            yield m
        else:
            yield from flat(m)


class Lane:

    def __init__(self, name):
        self.name, self.queue, self.sem, self.count = name, [], None, 0

    def use(self, sem):
        self.sem, self.count = sem, 0

    def do(self, build, *waits, count=True):
        self.queue.append((list(flat(waits)), build, self.sem if count else None, 1))
        if not count:
            return None
        self.count += 1
        return Mark(self.sem, self.count)

    def dma(self, slot, dst, src, *waits):
        self.queue.append((list(flat(waits)), lambda e: e.dma_start(dst, src), slot.sem, 16))
        slot.count += 16
        return Mark(slot.sem, slot.count)

    def hold(self, *waits):
        self.queue.append((list(flat(waits)), None, None, 0))

    def last(self):
        return Mark(self.sem, self.count) if self.count else None

    def replay(self, engine):
        reached = {}
        for waits, build, sem, step in self.queue:
            for m in waits:
                if reached.get(m.sem.name, 0) < m.value:
                    engine.wait_ge(m.sem, m.value)
                    reached[m.sem.name] = m.value
            if build is not None:
                ins = build(engine)
                if sem is not None:
                    ins.then_inc(sem, step)


class Slot:

    def __init__(self, sem):
        self.sem, self.count = sem, 0


class Ring:

    def __init__(self, n):
        self.users, self.at = [[] for _ in range(n)], -1

    def take(self):
        self.at = (self.at + 1) % len(self.users)
        users, self.users[self.at] = self.users[self.at], []
        return self.at, users

    def used(self, i, *marks):
        self.users[i] += list(flat(marks))


class Core:

    def __init__(self, nc, ctx):
        self.nc, self.ctx = nc, ctx
        self.pe, self.act, self.dve, self.pool, self.sp = (
            Lane(n) for n in ("pe", "act", "dve", "pool", "sp"))
        self.lanes = (self.pe, self.act, self.dve, self.pool, self.sp)
        self.nsem = 0
        self.slots = []

    def sem(self, name):
        self.nsem += 1
        return self.ctx.enter_context(self.nc.semaphore(f"{name}_{self.nsem}"))

    def slot(self, name):
        s = Slot(self.sem(name))
        self.slots.append(s)
        return s

    def stage(self, name):
        ends = [l.last() for l in self.lanes if l.sem is not None]
        ends += [Mark(s.sem, s.count) for s in self.slots if s.count]
        for lane in self.lanes:
            lane.hold(ends)
            lane.use(self.sem(f"{name}_{lane.name}"))


def rsqrt(c, out, src, n, *waits):
    return c.pool.do(lambda e: e.tensor_tensor(out, src, c.minus_half[:, 0:n], ALU.pow), *waits)


def layernorm(c, src, dst, st, ready):
    stats, mv, rs = st
    for t in range(NT):
        a = c.dve.do(lambda e, t=t: e.bn_stats(stats[:, t, :], src[:, t, :]), ready)
        last = c.dve.do(lambda e, t=t: e.bn_aggr(mv[:, t, :], stats[:, t, :]), a)
    a = c.dve.do(lambda e: e.tensor_scalar(rs[:, 0, :], mv[:, :, 1], LN_EPS, None, ALU.add), last)
    a = rsqrt(c, rs[:, 2, :], rs[:, 0, :], NT, a)
    out = []
    for t in range(NT):
        out.append(c.dve.do(lambda e, t=t: e.tensor_scalar(
            dst[:, t, :], src[:, t, :], mv[:, t, 0:1], rs[:, 2, t:t + 1],
            ALU.subtract, ALU.mult), a))
    return out


def to_features(c, src, dst, ready, banks, ring, affine=None, tiles=NT, lanes=None):
    width = src.shape[2] if len(src.shape) == 3 else D
    out = []
    for g in range(tiles // 4):
        group = []
        for k in range(width // P):
            b, users = ring.take()
            for j in range(4):
                t = 4 * g + j
                tr = c.pe.do(lambda e, t=t, k=k, j=j, b=b: e.transpose(
                    banks[b][:, j * P:(j + 1) * P], src[:, t, k * P:(k + 1) * P], c.ident[:, :]),
                    ready[t], users, c.ident_ready, count=(j == 3))
            o = dst[:, k, g * 512:(g + 1) * 512]
            if affine is not None:
                gain, bias = affine
                ev = c.dve.do(lambda e, o=o, b=b, k=k: e.tensor_scalar(
                    o, banks[b][:, :], gain[:, k:k + 1], bias[:, k:k + 1], ALU.mult, ALU.add), tr)
            elif k % 2:
                ev = c.act.do(lambda e, o=o, b=b: e.activation(o, banks[b][:, :], ACT.Copy), tr)
            else:
                ev = c.dve.do(lambda e, o=o, b=b: e.tensor_copy(o, banks[b][:, :]), tr)
            ring.used(b, ev)
            group.append(ev)
        out.append(group)
    return out


def matmuls(c, out, pairs, *waits):
    n = len(pairs)
    for i, (l, r) in enumerate(pairs):
        m = c.pe.do(lambda e, i=i, l=l, r=r: e.matmul(out, l, r, start=(i == 0), stop=(i == n - 1)),
                    waits if i == 0 else [], count=(i == n - 1))
    return m


def cross_attention(c, name, ctx_t, wq, wk, wv, wo, bq, bk, bv, bo, kscratch):
    nc = c.nc
    KB = 1024
    NKB = SK // KB
    ITEMS = B * NKB
    DH = D // H
    STACK = 6 * DH
    ROWS = STACK + 3
    Q_PART = (0, 1, 0, 1, 2, 0)
    K_PART = (0, 0, 1, 1, 0, 2)
    KT = KB // P
    QUADS = H // 4
    SLOTS = QUADS * KT
    VW = DH + 1
    NU = 5
    NV = 3
    c.stage(name)
    pe, act, dve, pool, sp = c.lanes
    outer = ExitStack()
    att = outer.enter_context(nc.sbuf_tensor(f"{name}_att", [P, NT, D], F32))
    with ExitStack() as long:
        def sb(n, shape, dt=F32, ctx=long):
            return ctx.enter_context(nc.sbuf_tensor(f"{name}_{n}", shape, dt))

        def ps(n, shape, dt=F32, ctx=long):
            return ctx.enter_context(nc.psum_tensor(f"{name}_{n}", shape, dt))

        q_base = sb("q_base", [P, H, N], BF16)
        wk_sb, wv_sb = sb("wk", [P, KC, D]), sb("wv", [P, KC, D])
        w_slot = c.slot(f"{name}_w")
        w_mark = sp.dma(w_slot, wk_sb[:, :, :], wk.rearrange("(k p) n -> p k n", p=P))
        w_mark = sp.dma(w_slot, wv_sb[:, :, :], wv.rearrange("(k p) n -> p k n", p=P))
        if bk is not None:
            bk_sb = sb("bk", [P, KC])
            w_mark = sp.dma(w_slot, bk_sb[:, :], bk)
        with ExitStack() as short:
            xn = sb("xn", [P, NT, D], ctx=short)
            xt = sb("xt", [P, KC, N], ctx=short)
            wq_sb = sb("wq", [P, KC, D], ctx=short)
            st = (sb("st", [P, NT, 6], ctx=short), sb("mv", [P, NT, 2], ctx=short),
                  sb("rs", [P, 3, NT], ctx=short))
            qf = sb("qf", [P, 2, D], ctx=short)
            qr = sb("qr", [P, 2, D], ctx=short)
            qtm = sb("qtm", [P, 2, H, STACK], BF16, ctx=short)
            bq_sb = sb("bq", [P, D], ctx=short)
            banks = [ps(f"bank{i}", [P, 512], ctx=short) for i in range(4)]
            tbank = [ps(f"tbank{i}", [P, 8, P], BF16, ctx=short) for i in range(2)]
            ring, tring, qring = Ring(4), Ring(2), Ring(2)
            q_slot = c.slot(f"{name}_wq")
            wq_mark = sp.dma(q_slot, wq_sb[:, :, :], wq.rearrange("(k p) n -> p k n", p=P))
            if bq is not None:
                wq_mark = sp.dma(q_slot, bq_sb[:, :], bq)
            normed = layernorm(c, c.x, xn, st, c.x_ready)
            xt_ready = to_features(c, xn, xt, normed, banks, ring)
            for t in range(NT):
                b, users = ring.take()
                mm = matmuls(c, banks[b][:, 0:D],
                             [(xt[:, k, t * P:(t + 1) * P], wq_sb[:, k, :]) for k in range(KC)],
                             xt_ready[t // 4], wq_mark, users)
                i, qusers = qring.take()
                f, r = qf[:, i, :], qr[:, i, :]
                if bq is not None:
                    a = dve.do(lambda e, f=f, b=b: e.tensor_tensor(
                        f, banks[b][:, 0:D], bq_sb[:, :], ALU.add), mm, qusers)
                else:
                    a = dve.do(lambda e, f=f, b=b: e.tensor_copy(f, banks[b][:, 0:D]), mm, qusers)
                ring.used(b, a)

                def part(j, i=i):
                    return qtm[:, i, :, j * DH:(j + 1) * DH]
                f3 = f.rearrange("p (h d) -> p h d", d=DH)
                r3 = r.rearrange("p (h d) -> p h d", d=DH)
                a = act.do(lambda e, o=part(0), f3=f3: e.activation(o, f3, ACT.Copy, scale=0.25), a, qusers)
                a0 = a
                a = dve.do(lambda e, r3=r3, f3=f3, o=part(0): e.scalar_tensor_tensor(
                    r3, f3, 0.25, o, ALU.mult, ALU.subtract), a)
                a = act.do(lambda e, o=part(1), r3=r3: e.activation(o, r3, ACT.Copy), a)
                a1 = a
                a = dve.do(lambda e, r3=r3, o=part(4), s=part(1): e.tensor_tensor(
                    o, r3, s, ALU.subtract), a)
                a2 = a
                done = [a2]
                done.append(dve.do(lambda e, o=part(2), s=part(0): e.tensor_copy(o, s), a0))
                done.append(dve.do(lambda e, o=part(5), s=part(0): e.tensor_copy(o, s), a0))
                done.append(dve.do(lambda e, o=part(3), s=part(1): e.tensor_copy(o, s), a1))
                for g in range(2):
                    tb, tusers = tring.take()
                    for j in range(8):
                        h = 8 * g + j
                        tr = pe.do(lambda e, tb=tb, j=j, h=h, i=i: e.transpose(
                            tbank[tb][0:STACK, j, :], qtm[:, i, h, :], c.ident_bf[:, :]),
                            done, tusers, c.ident_ready, count=(j == 7))
                    ev = dve.do(lambda e, tb=tb, g=g, t=t: e.tensor_copy(
                        q_base[0:STACK, 8 * g:8 * g + 8, t * P:(t + 1) * P],
                        tbank[tb][0:STACK, :, :]), tr)
                    tring.used(tb, ev)
                    qring.used(i, tr)
        c.stage(f"{name}_blocks")
        ks = sb("ks", [P, NU, 8, KB], BF16)
        vs = sb("vs", [P, NV, KT, H, VW])
        cx = sb("cx", [P, 2, KC, KB])
        ex = sb("ex", [P, 2, 4, S])
        kp = sb("kp", [P, 2, 3, 512], BF16)
        kr = sb("kr", [P, 512])
        o_sb = sb("o_sb", [P, 2, S])
        o_all = sb("o_all", [P, NKB, 2, H, VW])
        m_part = sb("m_part", [P, 2, 2, H, 2])
        m_blk2 = sb("m_blk", [P, 2, 2, H, NKB])
        m_spl = sb("m_spl", [P, 2, 8, 4])
        mt_bf = sb("mt_bf", [P, 2, 8, 3], BF16)
        w_blk = sb("w_blk", [P, 2, H, NKB])
        m_all = sb("m_all", [P, 2, H])
        acc = sb("acc", [P, 2, H, VW])
        sc = [ps(f"sc{i}", [P, 4, S]) for i in range(2)]
        mx = [ps(f"mx{i}", [P, 512]) for i in range(2)]
        pv = ps("pv", [P, S])
        pj = ps("pj", [P, 512])
        pj_bf = pj[:, :].bitcast(BF16)
        sc_ring, mx_ring, pv_ring, pj_ring = Ring(2), Ring(2), Ring(1), Ring(1)
        ks_ring, vs_ring, cx_ring, ex_ring, kp_ring, o_ring = (
            Ring(NU), Ring(NV), Ring(2), Ring(2), Ring(2), Ring(2))
        mp_ring, ms_ring = Ring(2), Ring(2)
        ks_slot = [c.slot(f"{name}_ks{i}") for i in range(NU)]
        cx_slot = [c.slot(f"{name}_cx{i}") for i in range(2)]
        kd_slot = [c.slot(f"{name}_kd{i}") for i in range(4)]
        ones_k = pool.do(lambda e: e.memset(ks[96:128, :, :, :], 1.0))
        init = [pool.do(lambda e: e.memset(vs[:, :, :, :, DH:VW], 1.0), ones_k),
                dve.do(lambda e: e.memset(pv[:, :], 0.0))]
        ctx_r = ctx_t.rearrange("b (k p) s -> b p k s", p=P)

        item = [dict() for _ in range(ITEMS)]
        q_m_users = [[] for _ in range(QUADS)]
        blk_users = []
        m_blk_users = [[], []]
        att_ready = []

        def load_ctx(i):
            b, kb = divmod(i, NKB)
            s, users = cx_ring.take()
            item[i]["cx"] = s
            item[i]["cx_ready"] = sp.dma(cx_slot[s], cx[:, s, :, :],
                                         ctx_r[b, :, :, kb * KB:(kb + 1) * KB], users)

        def project_keys(i, mt, ch):
            b, kb = divmod(i, NKB)
            s = item[i]["cx"]
            _, users = pj_ring.take()
            mm = matmuls(c, pj[:, :],
                         [(wk_sb[:, k, mt * P:(mt + 1) * P], cx[:, s, k, ch * 512:(ch + 1) * 512])
                          for k in range(KC)], item[i]["cx_ready"], w_mark, users)
            cx_ring.used(s, mm)
            p, pusers = kp_ring.take()
            bias = bk_sb[:, mt:mt + 1] if bk is not None else 0.0
            if bk is not None:
                a = act.do(lambda e: e.activation(kp[:, p, 0, :], pj[:, :], ACT.Identity, bias=bias),
                           mm, pusers)
            else:
                a = act.do(lambda e: e.activation(kp[:, p, 0, :], pj[:, :], ACT.Copy), mm, pusers)
            r = dve.do(lambda e: e.scalar_tensor_tensor(
                kr[:, :], pj[:, :], bias, kp[:, p, 0, :], ALU.add, ALU.subtract),
                a, item[i].get("kr_users"), c.kr_users)
            pj_ring.used(0, a, r)
            a2 = pool.do(lambda e: e.tensor_copy(kp[:, p, 1, :], kr[:, :]), r, pusers)
            a3 = pool.do(lambda e: e.tensor_tensor(
                kp[:, p, 2, :], kr[:, :], kp[:, p, 1, :], ALU.subtract), a2)
            c.kr_users = [a3]
            d = (2 * i + mt) % 2
            out = sp.dma(kd_slot[2 * d + ch], kscratch[2 * i + mt, :, :, ch * 512:(ch + 1) * 512]
                         .rearrange("c p n -> p c n"), kp[:, p, :, :], a, a2, a3)
            kp_ring.used(p, out)
            item[i].setdefault(("k", mt), []).append(out)

        def stack_keys(i, mt):
            u, users = ks_ring.take()
            item[i][("unit", mt)] = u
            for j, part in enumerate(K_PART):
                m = sp.dma(ks_slot[u], ks[DH * j:DH * (j + 1), u, :, :],
                           kscratch[2 * i + mt, part, :, :].rearrange("(h d) n -> d h n", d=DH),
                           users, item[i][("k", mt)])
            item[i][("ready", mt)] = m

        def project_values(i, t):
            s = item[i]["cx"]
            if t == 0:
                item[i]["vs"], item[i]["vs_users"] = vs_ring.take()
                item[i]["v_ready"] = []
            v = item[i]["vs"]
            _, users = pj_ring.take()
            mm = matmuls(c, pj[:, 0:D],
                         [(cx[:, s, k, t * P:(t + 1) * P], wv_sb[:, k, :]) for k in range(KC)],
                         item[i]["cx_ready"], w_mark, users)
            cx_ring.used(s, mm)
            a = act.do(lambda e: e.activation(
                vs[:, v, t, :, 0:DH], pj[:, 0:D].rearrange("p (h d) -> p h d", d=DH), ACT.Copy),
                mm, item[i]["vs_users"], init)
            pj_ring.used(0, a)
            item[i]["v_ready"].append(a)

        def block_max(i, h, qt):
            b, kb = divmod(i, NKB)
            mt, hl = divmod(h, 8)
            u = item[i][("unit", mt)]
            par = i % 2
            if h == 0 and qt == 0:
                item[i]["mx"] = []
            for ch in range(2):
                s, users = mx_ring.take()
                mm = pe.do(lambda e, s=s, ch=ch: e.matmul(
                    mx[s][:, :], q_base[0:STACK, h, b * S + qt * P:b * S + (qt + 1) * P],
                    ks[0:STACK, u, hl, ch * 512:(ch + 1) * 512], start=True, stop=True),
                    item[i][("ready", mt)], users)
                r = dve.do(lambda e, s=s, ch=ch: e.tensor_reduce(
                    m_part[:, par, qt, h, ch:ch + 1], mx[s][:, :], AX.X, ALU.max), mm,
                    c.m_part_users.get((par, h)))
                mx_ring.used(s, r)
                item[i]["mx"].append(r)

        def place_max(i, g):
            b, kb = divmod(i, NKB)
            par = i % 2
            hs = slice(4 * g, 4 * g + 4)
            s, users = ms_ring.take()
            m_blk = m_blk2[:, b % 2, :, :, :]
            a = dve.do(lambda e: e.tensor_reduce(m_blk[:, :, hs, kb:kb + 1], m_part[:, par, :, hs, :],
                                                 AX.X, ALU.max), item[i]["mx"], m_blk_users[b % 2])
            c.m_part_users.update({(par, h): [a] for h in range(4 * g, 4 * g + 4)})
            item[i].setdefault("blk", []).append(a)
            m8 = m_spl[:, s, :, :]
            neg = m8[:, :, 0].rearrange("p (q h) -> p q h", q=2)
            a = dve.do(lambda e: e.tensor_scalar(neg, m_blk[:, :, hs, kb], -1.0, None, ALU.mult), a, users)
            a = dve.do(lambda e: e.tensor_copy(mt_bf[:, s, :, 0], m8[:, :, 0]), a)
            a = dve.do(lambda e: e.tensor_tensor(m8[:, :, 1], m8[:, :, 0], mt_bf[:, s, :, 0],
                                                 ALU.subtract), a)
            a = dve.do(lambda e: e.tensor_copy(mt_bf[:, s, :, 1], m8[:, :, 1]), a)
            a = dve.do(lambda e: e.tensor_tensor(mt_bf[:, s, :, 2], m8[:, :, 1], mt_bf[:, s, :, 1],
                                                 ALU.subtract), a)
            _, pusers = pj_ring.take()
            for j in range(8):
                tr = pe.do(lambda e, j=j: e.transpose(
                    pj_bf[96:99, j * P:(j + 1) * P], mt_bf[:, s, j, :], c.ident_bf[:, :]),
                    a, pusers, count=(j == 7))
            ms_ring.used(s, tr)
            a = act.do(lambda e: e.activation(
                q_base[96:99, hs, b * S:(b + 1) * S].rearrange("p h (q t) -> p q h t", q=2),
                pj_bf[96:99, :].rearrange("p (q h t) -> p q h t", q=2, h=4), ACT.Copy),
                tr, q_m_users[g])
            q_m_users[g] = []
            pj_ring.used(0, a)
            item[i][("m", g)] = a

        def scores(i, g, kt):
            b = i // NKB
            s, users = sc_ring.take()
            for j in range(4):
                h = 4 * g + j
                mt, hl = divmod(h, 8)
                u = item[i][("unit", mt)]
                mm = pe.do(lambda e, s=s, j=j, h=h, u=u, hl=hl: e.matmul(
                    sc[s][:, j, :], ks[0:ROWS, u, hl, kt * P:(kt + 1) * P],
                    q_base[0:ROWS, h, b * S:(b + 1) * S], start=True, stop=True),
                    users, item[i][("m", g)], item[i][("ready", mt)], init, count=(j == 3))
            ks_ring.used(u, mm)
            q_m_users[g].append(mm)
            x, xusers = ex_ring.take()
            a = act.do(lambda e: e.activation(ex[:, x, :, :], sc[s][:, :, :], ACT.Exp), mm, xusers)
            sc_ring.used(s, a)
            return (i, g, kt, x, a)

        def weigh(unit):
            i, g, kt, x, a = unit
            v = item[i]["vs"]
            if kt == 0:
                _, c.pv_users = pv_ring.take()
            for j in range(4):
                mm = pe.do(lambda e, j=j: e.matmul(
                    pv[32 * j:32 * j + VW, :], vs[:, v, kt, 4 * g + j, :], ex[:, x, j, :],
                    start=(kt == 0), stop=(kt == KT - 1)),
                    a, item[i]["v_ready"], c.pv_users, init, count=(j == 3))
            ex_ring.used(x, mm)
            vs_ring.used(v, mm)
            if kt < KT - 1:
                return
            o, ousers = o_ring.take()
            ev = dve.do(lambda e: e.tensor_copy(o_sb[:, o, :], pv[:, :]), mm, ousers)
            pv_ring.used(0, ev)
            item[i][("o", g)] = (o, ev)

        def gather(i, g):
            kb = i % NKB
            o, ev = item[i][("o", g)]
            _, users = pj_ring.take()
            for q in range(2):
                tr = pe.do(lambda e, q=q: e.transpose(pj[:, q * P:(q + 1) * P],
                                                      o_sb[:, o, q * P:(q + 1) * P], c.ident[:, :]),
                           ev, users, count=(q == 1))
            o_ring.used(o, tr)
            a = dve.do(lambda e: e.tensor_copy(
                o_all[:, kb, :, 4 * g:4 * g + 4, :],
                pj[:, 0:S].rearrange("p (q h v) -> p q h v", q=2, h=4)[:, :, :, 0:VW]), tr, blk_users)
            pj_ring.used(0, a)
            item[i].setdefault("o", []).append(a)

        def combine(b):
            m_blk = m_blk2[:, b % 2, :, :, :]
            marks = [item[i][k] for i in range(b * NKB, (b + 1) * NKB) for k in ("o", "blk")]
            a = dve.do(lambda e: e.tensor_reduce(m_all[:, :, :].rearrange("p q (h o) -> p q h o", o=1),
                                                 m_blk[:, :, :, :], AX.X, ALU.max), marks)
            for kb in range(NKB):
                a2 = dve.do(lambda e, kb=kb: e.tensor_tensor(w_blk[:, :, :, kb], m_blk[:, :, :, kb],
                                                             m_all[:, :, :], ALU.subtract), a)
            a = act.do(lambda e: e.activation(w_blk[:, :, :, :], w_blk[:, :, :, :], ACT.Exp), a2)
            for kb in range(NKB):
                ob = o_all[:, kb, :, :, :].rearrange("p q h v -> p (q h) v")
                wb = (w_blk[:, :, :, kb:kb + 1].rearrange("p q h o -> p (q h) o")
                      .to_broadcast([P, 2 * H, VW]))
                a3 = dve.do(lambda e, ob=ob, wb=wb: e.tensor_tensor(ob, ob, wb, ALU.mult), a)
                ac = acc[:, :, :, :].rearrange("p q h v -> p (q h) v")
                if kb == 0:
                    a4 = dve.do(lambda e, ob=ob, ac=ac: e.tensor_copy(ac, ob), a3)
                else:
                    a4 = dve.do(lambda e, ob=ob, ac=ac: e.tensor_tensor(ac, ac, ob, ALU.add), a3, a4)
            blk_users[:] = [a4]
            m_blk_users[b % 2] = [a2]
            a = dve.do(lambda e: e.reciprocal(m_all[:, :, :], acc[:, :, :, DH]), a4)
            rb = m_all[:, :, :].rearrange("p q (h o) -> p (q h) o", o=1).to_broadcast([P, 2 * H, DH])
            av = acc[:, :, :, 0:DH].rearrange("p q h v -> p (q h) v")
            ov = att[:, 2 * b:2 * b + 2, :].rearrange("p q (h v) -> p (q h) v", v=DH)
            a = dve.do(lambda e: e.tensor_tensor(ov, av, rb, ALU.mult), a)
            att_ready.extend([a, a])

        c.kr_users, c.m_part_users, c.pv_users = [], {}, []
        for w in range(-2, ITEMS):
            fill, top, run = w + 2, w + 1, w
            if fill < ITEMS:
                if fill == 0:
                    load_ctx(0)
                if fill + 1 < ITEMS:
                    load_next = fill + 1
                else:
                    load_next = None
            pending = None
            for s in range(SLOTS):
                g, kt = divmod(s, KT)
                unit = None
                if run >= 0:
                    unit = scores(run, g, kt)
                if 0 <= top < ITEMS:
                    block_max(top, s // 2, s % 2)
                if fill < ITEMS:
                    if s in (0, 2):
                        project_keys(fill, 0, s // 2)
                    elif s == 4:
                        stack_keys(fill, 0)
                    elif s in (16, 18):
                        project_keys(fill, 1, (s - 16) // 2)
                    elif s == 20:
                        stack_keys(fill, 1)
                    elif s % 2 == 0 and s // 2 in (3, 4, 5, 6, 7, 11, 12, 13):
                        project_values(fill, (3, 4, 5, 6, 7, 11, 12, 13).index(s // 2))
                    if s == 1 and load_next is not None:
                        load_ctx(load_next)
                if run >= 0 and pending is not None:
                    weigh(pending)
                    if pending[2] == KT - 1:
                        gather(run, pending[1])
                pending = unit
                if 0 <= top < ITEMS and kt == KT - 1:
                    if g < QUADS - 1 or run < 0:
                        place_max(top, g)
            if run >= 0:
                weigh(pending)
                gather(run, QUADS - 1)
                if top < ITEMS:
                    place_max(top, QUADS - 1)
                if run % NKB == NKB - 1:
                    combine(run // NKB)
    c.stage(f"{name}_out")
    with ExitStack() as short:
        def sb(n, shape, dt=F32):
            return short.enter_context(nc.sbuf_tensor(f"{name}_{n}", shape, dt))
        wo_sb, bo_sb, bv_sb = sb("wo", [P, KC, D]), sb("bo", [P, D]), sb("bv", [P, D])
        at = sb("at", [P, KC, N])
        out_banks = [short.enter_context(nc.psum_tensor(f"{name}_ob{i}", [P, 512], F32)) for i in range(8)]
        ring = Ring(8)
        slot = c.slot(f"{name}_wo")
        m = sp.dma(slot, wo_sb[:, :, :], wo.rearrange("(k p) n -> p k n", p=P))
        m = sp.dma(slot, bo_sb[:, :], bo)
        if bv is not None:
            m = sp.dma(slot, bv_sb[:, :], bv)
            ready = [dve.do(lambda e, t=t: e.tensor_tensor(att[:, t, :], att[:, t, :], bv_sb[:, :],
                                                           ALU.add), m) for t in range(NT)]
        else:
            ready = [None] * NT
        at_ready = to_features(c, att, at, ready, out_banks, ring)
        c.x_ready = project_residual(c, at, wo_sb, KC, bo_sb, out_banks, ring, at_ready, m)
    outer.close()


def project_residual(c, src, w_sb, chunks, bias_sb, banks, ring, ready, w_mark):
    for t in range(NT):
        b, users = ring.take()
        mm = matmuls(c, banks[b][:, 0:D],
                     [(src[:, k, t * P:(t + 1) * P], w_sb[:, k, :]) for k in range(chunks)],
                     ready[t // 4], w_mark, users)
        a = c.dve.do(lambda e, t=t, b=b: e.tensor_tensor(c.x[:, t, :], c.x[:, t, :],
                                                         banks[b][:, 0:D], ALU.add), mm)
        ring.used(b, a)
        last = c.dve.do(lambda e, t=t: e.tensor_tensor(c.x[:, t, :], c.x[:, t, :],
                                                       bias_sb[:, :], ALU.add), a)
    return last


def self_attention(c, name, sb, ps_s, ps_t, ps_o, rings, q_of, k_of, v_of, mask, scale, heads_per_out,
                   emit, ready, v_ready, extra, batches=range(B), scale_of=None):
    pe, act, dve, pool, sp = c.lanes
    s_ring, t_ring, o_ring, p_ring, pt_ring, st_ring = rings
    p_sb, pt_sb, stat = sb
    KEYS = (P, 2 * P)
    OFF = (0, P)
    step = P // heads_per_out

    def front(b, h):
        p, pusers = p_ring.take()
        st, stusers = st_ring.take()
        t3 = stat[:, st, :, :]
        s, susers = s_ring.take()
        for q in range(2):
            ql, qt = q_of(b, h, q)
            kr = k_of(b, h, KEYS[q])
            mm = pe.do(lambda e, q=q, ql=ql, kr=kr: e.matmul(
                ps_s[s][:, OFF[q]:OFF[q] + KEYS[q]], ql, kr, start=True, stop=True),
                ready, susers, count=(q == 1))
        sv = p_sb[:, p, :]
        a = dve.do(lambda e: e.tensor_tensor(sv, ps_s[s][:, 0:3 * P], mask[:, :], ALU.add), mm,
                   pusers, extra)
        s_ring.used(s, a)
        for q in range(2):
            m = dve.do(lambda e, q=q: e.tensor_reduce(
                t3[:, 0, q:q + 1], sv[:, OFF[q]:OFF[q] + KEYS[q]], AX.X, ALU.max), a, stusers)
        if scale_of is not None:
            for q in range(2):
                m2 = dve.do(lambda e, q=q: e.tensor_scalar(
                    t3[:, 4, q:q + 1], scale_of(b, h, q), scale, None, ALU.mult), m)
            m = dve.do(lambda e: e.scalar_tensor_tensor(
                t3[:, 1, :], t3[:, 0, :], -1.0, t3[:, 4, :], ALU.mult, ALU.mult), m2)
        else:
            m = dve.do(lambda e: e.tensor_scalar(t3[:, 1, :], t3[:, 0, :], -scale, None, ALU.mult), m)
        for q in range(2):
            x = act.do(lambda e, q=q: e.activation(
                sv[:, OFF[q]:OFF[q] + KEYS[q]], sv[:, OFF[q]:OFF[q] + KEYS[q]], ACT.Exp,
                bias=t3[:, 1, q:q + 1],
                scale=scale if scale_of is None else t3[:, 4, q:q + 1], accum_out=t3[:, 2, q:q + 1]), m)
        m = dve.do(lambda e: e.reciprocal(t3[:, 3, :], t3[:, 2, :]), x)
        for q in range(2):
            n = pool.do(lambda e, q=q: e.tensor_scalar(
                sv[:, OFF[q]:OFF[q] + KEYS[q]], sv[:, OFF[q]:OFF[q] + KEYS[q]],
                t3[:, 3, q:q + 1], None, ALU.mult), m)
        st_ring.used(st, n)
        return p, n

    def back(b, h, p, n):
        t, tusers = t_ring.take()
        for j in range(3):
            tr = pe.do(lambda e, j=j: e.transpose(
                ps_t[t][:, j * P:(j + 1) * P], p_sb[:, p, j * P:(j + 1) * P], c.ident[:, :]),
                n, tusers, count=(j == 2))
        p_ring.used(p, tr)
        pt, ptusers = pt_ring.take()
        if h % 2:
            ev = act.do(lambda e: e.activation(pt_sb[:, pt, :], ps_t[t][:, 0:3 * P], ACT.Copy),
                        tr, ptusers)
        else:
            ev = dve.do(lambda e: e.tensor_copy(pt_sb[:, pt, :], ps_t[t][:, 0:3 * P]), tr, ptusers)
        t_ring.used(t, ev)
        return pt, ev

    def apply(b, h, pt, ev):
        g, j = divmod(h, heads_per_out)
        if j == 0:
            open_bank["at"], open_bank["users"] = o_ring.take()
        o = open_bank["at"]
        rows = slice(step * j, step * j + step)
        pe.do(lambda e: e.matmul(ps_o[o][rows, 0:2 * P], v_of(b, 0, h), pt_sb[:, pt, 0:2 * P],
                                 start=True, stop=False), ev, v_ready, open_bank["users"], count=False)
        mm = pe.do(lambda e: e.matmul(ps_o[o][rows, P:2 * P], v_of(b, 1, h), pt_sb[:, pt, 2 * P:3 * P],
                                      start=False, stop=True))
        pt_ring.used(pt, mm)
        if j == heads_per_out - 1:
            o_ring.used(o, emit(b, g, ps_o[o], mm))

    todo = [(b, h) for b in batches for h in range(H)]
    fronts, backs, open_bank = {}, {}, {}
    LAG1, LAG2 = 3, 4
    for i in range(len(todo) + LAG2):
        if i < len(todo):
            fronts[i] = front(*todo[i])
        if 0 <= i - LAG1 < len(todo):
            backs[i - LAG1] = back(*todo[i - LAG1], *fronts[i - LAG1])
        if 0 <= i - LAG2 < len(todo):
            apply(*todo[i - LAG2], *backs[i - LAG2])
        yield


def run(*jobs):
    jobs = list(jobs)
    while jobs:
        jobs = [j for j in jobs if next(j, "end") != "end"]


def attention_buffers(c, name, ctx):
    nc = c.nc
    sb = (ctx.enter_context(nc.sbuf_tensor(f"{name}_p", [P, 5, 3 * P], F32)),
          ctx.enter_context(nc.sbuf_tensor(f"{name}_pt", [P, 3, 3 * P], F32)),
          ctx.enter_context(nc.sbuf_tensor(f"{name}_stat", [P, 5, 5, 2], F32)))
    return sb


def conv_attention(c, name, g):
    nc = c.nc
    c.stage(name)
    pe, act, dve, pool, sp = c.lanes
    G = 4
    HW = P // G
    DH = D // H
    with ExitStack() as ctx:
        def sb(n, shape, dt=F32):
            return ctx.enter_context(nc.sbuf_tensor(f"{name}_{n}", shape, dt))
        wq, wk = sb("wq", [P, KC, G * P]), sb("wk", [P, KC, G * P])
        wv = sb("wv", [P, KC, G * P])
        wo = sb("wo", [P, G, D])
        cw = sb("cw", [P, 3, G, G * P])
        cols = sb("cols", [P, 3, G])
        bv, bo = sb("bv", [P, G * P]), sb("bo", [P, D])
        mask = sb("mask", [P, 3 * P])
        xn, xt = sb("xn", [P, NT, D]), sb("xt", [P, KC, N])
        q, k = sb("q", [P, G, N]), sb("k", [P, G, N])
        v = sb("v", [P, NT, G * P])
        cc = sb("cc", [P, G, B, S + 2])
        st = (sb("st", [P, NT, 6]), sb("mv", [P, NT, 2]), sb("rs", [P, 3, NT]))
        asb = attention_buffers(c, name, ctx)
        banks = [ctx.enter_context(nc.psum_tensor(f"{name}_bank{i}", [P, 512], F32)) for i in range(8)]
        slot = c.slot(f"{name}_w")
        for dst, src in ((wq, "ca_wq"), (wk, "ca_wk"), (wv, "ca_wv"), (wo, "ca_wo")):
            w = sp.dma(slot, dst[:, :, :], g(src).rearrange("(k p) n -> p k n", p=P))
        for dst, src in ((cols, "ca_cols"),):
            w = sp.dma(slot, dst[:, :, :], g(src).rearrange("p (a b) -> p a b", a=3))
        for dst, src in ((bv, "ca_bv"), (bo, "ca_bo"), (mask, "causal")):
            w = sp.dma(slot, dst[:, :], g(src))
        slot2 = c.slot(f"{name}_cw")
        cw_mark = sp.dma(slot2, cw[:, :, :, :], g("ca_cw").rearrange("t (k p) n -> p t k n", p=P))
        zero = [pool.do(lambda e, b=b: e.memset(cc[:, :, :, b:b + 1], 0.0)) for b in (0, S + 1)]
        ring = Ring(8)
        normed = layernorm(c, c.x, xn, st, c.x_ready)
        xr = to_features(c, xn, xt, normed, banks, ring)

        def project(dst, w_sb, bias_col, src_of, chunks, marks, n_of=2):
            out = []
            for gr in range(G):
                for half in range(2):
                    b, users = ring.take()
                    mm = matmuls(c, banks[b][:, :], [
                        (w_sb(i, gr), src_of(i, half)) for i in range(chunks)], marks, users)
                    o = dst[:, gr, half * 512:(half + 1) * 512]
                    bias = cols[:, bias_col, gr:gr + 1]
                    if half:
                        a = act.do(lambda e, o=o, b=b, bias=bias: e.activation(
                            o, banks[b][:, :], ACT.Identity, bias=bias), mm)
                    else:
                        a = dve.do(lambda e, o=o, b=b, bias=bias: e.tensor_scalar(
                            o, banks[b][:, :], bias, None, ALU.add), mm)
                    ring.used(b, a)
                    out.append(a)
            return out

        def xsrc(i, half):
            return xt[:, i, half * 512:(half + 1) * 512]
        qk = project(q, lambda i, gr: wq[:, i, gr * P:(gr + 1) * P], 0, xsrc, KC, [xr, w])
        qk += project(k, lambda i, gr: wk[:, i, gr * P:(gr + 1) * P], 1, xsrc, KC, [xr, w])
        v_ready = []
        for t in range(NT):
            b, users = ring.take()
            mm = matmuls(c, banks[b][:, :], [(xt[:, i, t * P:(t + 1) * P], wv[:, i, :])
                                             for i in range(KC)], users)
            a = dve.do(lambda e, t=t, b=b: e.tensor_tensor(v[:, t, :], banks[b][:, :], bv[:, :],
                                                           ALU.add), mm)
            ring.used(b, a)
            v_ready.append(a)

        free = [Ring(2), Ring(2), Ring(2), Ring(5), Ring(3), Ring(5)]
        for r, b0 in ((free[0], 0), (free[1], 2), (free[2], 4)):
            for i in range(2):
                r.used(i, ring.users[b0 + i])
        ring.users[0:6] = [[] for _ in range(6)]

        def q_of(b, h, qt):
            gr, j = divmod(h, G)
            rows = slice(HW * j, HW * j + DH)
            return q[rows, gr, b * S + qt * P:b * S + (qt + 1) * P], None

        def k_of(b, h, n):
            gr, j = divmod(h, G)
            return k[HW * j:HW * j + DH, gr, b * S:b * S + n]

        def v_of(b, kt, h):
            return v[:, 2 * b + kt, HW * h:HW * (h + 1)]
        conv_in = []

        def keep(b, gr, bank, mm):
            a = act.do(lambda e: e.activation(cc[:, gr, b, 1:S + 1], bank[:, 0:S], ACT.Copy), mm)
            conv_in.append(a)
            return a
        run(self_attention(c, name, asb, banks[0:2], banks[2:4], banks[4:6], free, q_of, k_of, v_of,
                       mask, 1.0 / float(np.sqrt(DH)), G, keep, qk, v_ready, w))
        q2 = []
        for gr in range(G):
            for half in range(2):
                for bb in range(2):
                    b = 2 * half + bb
                    i = 6 + (bb % 2)
                    users, ring.users[i] = ring.users[i], []
                    pairs = [(cw[:, t, kk, gr * P:(gr + 1) * P], cc[:, kk, b, t:t + S])
                             for t in range(3) for kk in range(G)]
                    mm = matmuls(c, banks[i][:, 0:S], pairs, conv_in, zero, cw_mark, users)
                    a = dve.do(lambda e, gr=gr, b=b, i=i: e.tensor_scalar(
                        q[:, gr, b * S:(b + 1) * S], banks[i][:, 0:S], cols[:, 2, gr:gr + 1], None,
                        ALU.add), mm)
                    ring.users[i] = [a]
                    q2.append(a)
        ctx2 = []

        def keep2(b, gr, bank, mm):
            a = act.do(lambda e: e.activation(cc[:, gr, b, 1:S + 1], bank[:, 0:S], ACT.Copy), mm, q2)
            ctx2.append(a)
            return a
        run(self_attention(c, name, asb, banks[0:2], banks[2:4], banks[4:6], free, q_of, k_of, v_of,
                       mask, 1.0 / float(np.sqrt(DH)), G, keep2, [q2, qk], v_ready, w))
        for t in range(NT):
            b, qt = divmod(t, 2)
            i = 6 + t % 2
            users, ring.users[i] = ring.users[i], []
            mm = matmuls(c, banks[i][:, 0:D],
                         [(cc[:, kk, b, 1 + qt * P:1 + (qt + 1) * P], wo[:, kk, :]) for kk in range(G)],
                         ctx2, users)
            a = dve.do(lambda e, t=t, i=i: e.tensor_tensor(c.x[:, t, :], c.x[:, t, :],
                                                           banks[i][:, 0:D], ALU.add), mm)
            ring.users[i] = [a]
            last = dve.do(lambda e, t=t: e.tensor_tensor(c.x[:, t, :], c.x[:, t, :], bo[:, :],
                                                         ALU.add), a)
        c.x_ready = last


DEPTH = 6
LH = 64
INNER = H * LH
FF = int(D * 4 * 2 / 3)
FC = -(-FF // P)
FFP = FC * P


def local_transformer(c, name, g):
    nc = c.nc
    c.stage(name)
    pe, act, dve, pool, sp = c.lanes
    HP = H // 2
    with ExitStack() as ctx:
        def sb(n, shape, dt=F32):
            return ctx.enter_context(nc.sbuf_tensor(f"{name}_{n}", shape, dt))
        park = c.slot(f"{name}_park")
        y = c.x
        parked = sp.dma(park, c.parked, c.x[:, :, :], c.x_ready)
        wqk = sb("wqk", [P, 2, KC, 2 * INNER])
        wval = sb("wval", [P, KC, INNER])
        wo, w1, w2 = sb("wo", [P, HP, D]), sb("w1", [P, KC, 2 * FFP]), sb("w2", [P, FC, D])
        scl = sb("scl", [P, 2, 4, LH])
        rot = sb("rot", [P, 4, 2, LH])
        tab = sb("tab", [P, 2, 4, 2, LH])
        b2, ffc, lnc = sb("b2", [P, 2, D]), sb("ffc", [P, DEPTH, 2, FC]), sb("lnc", [P, DEPTH, 2, KC])
        mask = sb("mask", [P, 3 * P])
        xs, xt = sb("xs", [P, 2, 2, P]), sb("xt", [P, 2, KC, S])
        r_qk = sb("r_qk", [P, 2, INNER])
        t_sq = sb("t_sq", [P, 2, 512])
        t_rot = sb("t_rot", [P, 2, 512])
        nrm = sb("nrm", [P, 2, 3, H])
        rq = sb("rq", [P, 2, 2, H])
        q_even, q_odd = sb("q_even", [P, 2, HP, S]), sb("q_odd", [P, 2, HP, S])
        kt = sb("kt", [P, 2, HP, S])
        v = sb("v", [P, 2, 2, INNER])
        ot = sb("ot", [P, HP, S])
        fs, ft = sb("fs", [P, 2, D]), sb("ft", [P, KC, S])
        fst, fmv, frs = sb("fst", [P, 2, 6]), sb("fmv", [P, 2, 2]), sb("frs", [P, 2, 2])
        gl, u = sb("gl", [P, 2, S]), sb("u", [P, FC, S])
        st = (sb("st", [P, NT, 6]), sb("mv", [P, NT, 2]), sb("rs", [P, 3, NT]))
        asb = attention_buffers(c, name, ctx)
        banks = [ctx.enter_context(nc.psum_tensor(f"{name}_bank{i}", [P, 512], F32)) for i in range(8)]
        arings = [Ring(2), Ring(2), Ring(2), Ring(5), Ring(3), Ring(5)]
        gen = Ring(2)
        r_ring, t_ring, n_ring = Ring(2), Ring(2), Ring(2)
        gl_ring = Ring(2)

        slot = c.slot(f"{name}_small")
        small = sp.dma(slot, rot[:, :, :, :], g("lt_rot").rearrange("p (a b c) -> p a b c", a=4, b=2))
        small = sp.dma(slot, ffc[:, :, :, :], g("lt_ffc").rearrange("p (a b c) -> p a b c", a=DEPTH, b=2))
        small = sp.dma(slot, lnc[:, :, :, :], g("lt_lnc").rearrange("p (a b c) -> p a b c", a=DEPTH, b=2))
        small = sp.dma(slot, mask[:, :], g("band"))
        zeros = [dve.do(lambda e: e.memset(q_even[64:128, :, :, :], 0.0)),
                 dve.do(lambda e: e.memset(q_odd[0:64, :, :, :], 0.0)),
                 dve.do(lambda e: e.memset(xs[0:1, :, 0, :], 0.0))]
        normed = layernorm(c, c.x, y, st, [c.x_ready, parked])
        y_ready = {b: [normed[2 * b], normed[2 * b + 1]] for b in range(B)}

        wq_slot = [c.slot(f"{name}_wqkv{i}") for i in range(2)]
        wb_slot = [c.slot(f"{name}_w{n}") for n in ("o", "1", "2")]
        xs_slot = [c.slot(f"{name}_xs{i}") for i in range(2)]
        fs_slot = c.slot(f"{name}_fs")
        wv_slot = c.slot(f"{name}_wval")
        wval_ready, wval_users = {}, {l: [] for l in range(-1, DEPTH)}
        wqkv_ready, wqkv_users = {}, {l: [] for l in range(-2, DEPTH)}
        wb_ready, wb_users = {}, {l: [[], [], []] for l in range(-1, DEPTH)}
        tab_ready, tab_users = {}, {l: [] for l in range(-2, DEPTH)}
        b2_users = {l: [] for l in range(-2, DEPTH)}
        par_users = {}
        ot_users, fs_users, ft_users, u_users = [[]], [[]], [[]], [[]]

        def load_front(l):
            i = l % 2
            w = g("lt_wqkv")[l].rearrange("(k p) n -> p k n", p=P)
            sp.dma(wq_slot[i], wqk[:, i, :, :], w[:, :, 0:2 * INNER], wqkv_users[l - 2])
            wval_ready[l] = sp.dma(wv_slot, wval[:, :, :], w[:, :, 2 * INNER:], wval_users[l - 1])
            sp.dma(wq_slot[i], b2[:, i, :], g("lt_b2")[l], b2_users[l - 2])
            m = sp.dma(wq_slot[i], scl[:, i, :, :], g("lt_scl")[l].rearrange("p (a b) -> p a b", a=4),
                       tab_users[l - 2])
            wqkv_ready[l] = m
            for tile in range(2):
                a = dve.do(lambda e, tile=tile: e.tensor_tensor(
                    tab[:, i, :, tile, :], rot[:, :, tile, :], scl[:, i, :, :], ALU.mult),
                    m, small, tab_users[l - 2])
            tab_ready[l] = a

        def load_back(l, n):
            dst = (wo, w1, w2)[n]
            src = (g("lt_wo"), g("lt_w1"), g("lt_w2"))[n]
            wb_ready[l, n] = sp.dma(wb_slot[n], dst[:, :, :], src[l].rearrange("(k p) n -> p k n", p=P),
                                    wb_users[l - 1][n])

        def shift(dst, slot_, b, cols, *waits):
            sp.dma(slot_, dst[1:P, :, cols], y[0:P - 1, 2 * b:2 * b + 2, P:D], waits)
            return sp.dma(slot_, dst[0:1, 1, cols], y[P - 1:P, 2 * b, P:D])

        def front(l, b):
            par, lp = (l * B + b) % 2, l % 2
            prev = par_users.get((l * B + b) - 2, [])
            m = shift(xs[:, par, :, :], xs_slot[par], b, slice(0, P), y_ready[b], zeros, prev)
            if b == 0:
                load_front(l)
            yield
            i, users = gen.take()
            for k in range(KC):
                for q in range(2):
                    src = y[:, 2 * b + q, 0:P] if k == 0 else xs[:, par, q, :]
                    tr = pe.do(lambda e, k=k, q=q, src=src, i=i: e.transpose(
                        banks[6 + i][:, (2 * k + q) * P:(2 * k + q + 1) * P], src, c.ident[:, :]),
                        m, y_ready[b], users, count=(k + q == 2))
            a = act.do(lambda e, i=i: e.activation(
                xt[:, par, :, :], banks[6 + i][:, :].rearrange("p (k s) -> p k s", k=KC), ACT.Copy),
                tr, prev)
            gen.used(i, a)
            x_mark = a
            done_k, done_q, done_v = [], [], []
            yield
            for tile in range(2):
                for sec in (0, 1):
                    r, rusers = r_ring.take()
                    n, nusers = n_ring.take()
                    parts = []
                    for half in range(2):
                        i, users = gen.take()
                        col = sec * INNER + half * 512
                        mm = matmuls(c, banks[6 + i][:, :], [
                            (xt[:, par, k, tile * P:(tile + 1) * P], wqk[:, lp, k, col:col + 512])
                            for k in range(KC)], x_mark, wqkv_ready[l], users)
                        wqkv_users[l].append(mm)
                        t, tusers = t_ring.take()
                        p3 = banks[6 + i][:, :].rearrange("p (h d) -> p h d", d=LH)
                        sq3 = t_sq[:, t, :].rearrange("p (h d) -> p h d", d=LH)
                        ro3 = t_rot[:, t, :].rearrange("p (h d) -> p h d", d=LH)
                        out3 = r_qk[:, r, half * 512:(half + 1) * 512].rearrange("p (h d) -> p h d", d=LH)

                        def table(j, lo, hi, tile=tile, sec=sec):
                            return (tab[:, lp, 2 * sec + j, tile:tile + 1, lo:hi]
                                    .to_broadcast([P, 8, hi - lo]))
                        a = act.do(lambda e, sq3=sq3, p3=p3: e.activation(sq3, p3, ACT.Square), mm, tusers)
                        s_ = dve.do(lambda e, n=n, half=half, sq3=sq3: e.tensor_reduce(
                            nrm[:, n, 0, half * 8:half * 8 + 8], sq3, AX.X, ALU.add), a, nusers)
                        c1 = dve.do(lambda e, out3=out3, p3=p3, tb=table(0, 0, LH): e.tensor_tensor(
                            out3, p3, tb, ALU.mult), mm, rusers, tab_ready[l])
                        dve.do(lambda e, ro3=ro3, p3=p3, tb=table(1, 0, 32): e.tensor_tensor(
                            ro3[:, :, 0:32], p3[:, :, 32:64], tb, ALU.mult), tusers)
                        c2 = dve.do(lambda e, ro3=ro3, p3=p3, tb=table(1, 32, 64): e.tensor_tensor(
                            ro3[:, :, 32:64], p3[:, :, 0:32], tb, ALU.mult))
                        gen.used(i, a, c2)
                        c3 = dve.do(lambda e, out3=out3, ro3=ro3: e.tensor_tensor(
                            out3, out3, ro3, ALU.add), c1, c2)
                        t_ring.used(t, s_, c3)
                        parts += [s_, c3]
                        yield
                    f = dve.do(lambda e, n=n: e.tensor_scalar(nrm[:, n, 1, :], nrm[:, n, 0, :], 1e-24,
                                                         None, ALU.max), parts)
                    if sec == 0:
                        f = rsqrt(c, rq[:, par, tile, :], nrm[:, n, 1, :], H, f, prev)
                        done_q.append(f)
                        n_ring.used(n, f)
                    else:
                        f = rsqrt(c, nrm[:, n, 2, :], nrm[:, n, 1, :], H, f)
                        full = r_qk[:, r, :].rearrange("p (h d) -> p h d", d=LH)
                        nb = (nrm[:, n, 2, :].rearrange("p (h o) -> p h o", o=1)
                              .to_broadcast([P, H, LH]))
                        f = dve.do(lambda e, full=full, nb=nb: e.tensor_tensor(full, full, nb, ALU.mult), f)
                        n_ring.used(n, f)
                    yield
                    for half in range(2):
                        i, users = gen.take()
                        for j in range(4):
                            hp = 4 * half + j
                            tr = pe.do(lambda e, r=r, i=i, j=j, hp=hp: e.transpose(
                                banks[6 + i][:, j * P:(j + 1) * P], r_qk[:, r, hp * P:(hp + 1) * P],
                                c.ident[:, :]), f, parts, users, count=(j == 3))
                        src = banks[6 + i][:, :].rearrange("p (j t) -> p j t", j=4)
                        hs, ts = slice(4 * half, 4 * half + 4), slice(tile * P, (tile + 1) * P)
                        if sec == 0:
                            a = act.do(lambda e, src=src, hs=hs, ts=ts: e.activation(
                                q_even[0:64, par, hs, ts], src[0:64, :, :], ACT.Copy), tr, prev)
                            a2 = dve.do(lambda e, src=src, hs=hs, ts=ts: e.tensor_copy(
                                q_odd[64:128, par, hs, ts], src[64:128, :, :]), tr, prev)
                            done_q += [a, a2]
                            gen.used(i, a, a2)
                        else:
                            a = act.do(lambda e, src=src, hs=hs, ts=ts: e.activation(
                                kt[:, par, hs, ts], src, ACT.Copy), tr, prev)
                            done_k.append(a)
                            gen.used(i, a)
                        r_ring.used(r, tr)
                        yield
                for half in range(2):
                    i, users = gen.take()
                    col = half * 512
                    mm = matmuls(c, banks[6 + i][:, :], [
                        (xt[:, par, k, tile * P:(tile + 1) * P], wval[:, k, col:col + 512])
                        for k in range(KC)], x_mark, wval_ready[l], users)
                    wval_users[l].append(mm)
                    a = act.do(lambda e, i=i, tile=tile, half=half: e.activation(
                        v[:, par, tile, half * 512:(half + 1) * 512], banks[6 + i][:, :], ACT.Copy),
                        mm, prev)
                    gen.used(i, a)
                    done_v.append(a)
                    yield
            tab_users[l].append(done_k[-1])
            tab_users[l] += parts
            ready[l * B + b] = ([done_q, done_k], done_v)

        def back(l, b):
            par = (l * B + b) % 2
            qk_ready, v_ready = ready[l * B + b]
            emitted = []

            def keep(b_, gr, bank, mm):
                a = act.do(lambda e: e.activation(ot[:, gr, :], bank[:, 0:S], ACT.Copy), mm, ot_users[0])
                emitted.append(a)
                return a

            def q_of(b_, h, qt):
                q = q_odd if h % 2 else q_even
                return q[:, par, h // 2, qt * P:(qt + 1) * P], None
            yield from self_attention(
                c, name, asb, banks[0:2], banks[2:4], banks[4:6], arings, q_of,
                lambda b_, h, n: kt[:, par, h // 2, 0:n],
                lambda b_, t, h: v[:, par, t, h * LH:(h + 1) * LH],
                mask, 8.0, 2, keep, [qk_ready, zeros], v_ready, small, batches=[b],
                scale_of=lambda b_, h, q: rq[:, par, q, h:h + 1])
            par_users[l * B + b] = [emitted, pe.last(), dve.last(), act.last()]
            m = []
            for tile in range(2):
                t = 2 * b + tile
                i, users = gen.take()
                mm = matmuls(c, banks[6 + i][:, 0:D], [
                    (ot[:, k, tile * P:(tile + 1) * P], wo[:, k, :]) for k in range(HP)],
                    emitted, wb_ready[l, 0], users)
                a = dve.do(lambda e, t=t, i=i: e.tensor_tensor(y[:, t, :], y[:, t, :],
                                                               banks[6 + i][:, 0:D], ALU.add), mm)
                gen.used(i, a)
                m.append(a)
                yield
            ot_users[0] = [mm]
            wb_users[l][0] = [mm]
            if b == B - 1 and l + 1 < DEPTH:
                load_back(l + 1, 0)
            sp.dma(fs_slot, fs[:, :, 0:P], y[:, 2 * b:2 * b + 2, 0:P], m, fs_users[0])
            f = [shift(fs, fs_slot, b, slice(P, D)),
                 dve.do(lambda e: e.memset(fs[0:1, 0, P:D], 0.0), fs_users[0])]
            yield
            for q in range(2):
                a = dve.do(lambda e, q=q: e.bn_stats(fst[:, q, :], fs[:, q, :]), f)
                a = dve.do(lambda e, q=q: e.bn_aggr(fmv[:, q, :], fst[:, q, :]), a)
            a = dve.do(lambda e: e.tensor_scalar(frs[:, 0, :], fmv[:, :, 1], LN_EPS, None, ALU.add), a)
            a = rsqrt(c, frs[:, 1, :], frs[:, 0, :], 2, a)
            n = []
            for q in range(2):
                n.append(dve.do(lambda e, q=q: e.tensor_scalar(
                    fs[:, q, :], fs[:, q, :], fmv[:, q, 0:1], frs[:, 1, q:q + 1],
                    ALU.subtract, ALU.mult), a))
            yield
            i, users = gen.take()
            for k in range(KC):
                for q in range(2):
                    tr = pe.do(lambda e, k=k, q=q, i=i: e.transpose(
                        banks[6 + i][:, (2 * k + q) * P:(2 * k + q + 1) * P],
                        fs[:, q, k * P:(k + 1) * P], c.ident[:, :]), n, users, count=(k + q == 2))
            fs_users[0] = [tr]
            fx = []
            for k in range(KC):
                fx.append(dve.do(lambda e, k=k, i=i: e.tensor_scalar(
                    ft[:, k, :], banks[6 + i][:, k * S:(k + 1) * S], lnc[:, l, 0, k:k + 1],
                    lnc[:, l, 1, k:k + 1], ALU.mult, ALU.add), tr, small, ft_users[0]))
            gen.used(i, fx)
            yield
            ud = []
            for mc in range(FC):
                i, users = gen.take()
                matmuls(c, banks[6 + i][:, S:2 * S], [
                    (w1[:, k, FFP + mc * P:FFP + (mc + 1) * P], ft[:, k, :]) for k in range(KC)],
                    fx, wb_ready[l, 1], users)
                mm = matmuls(c, banks[6 + i][:, 0:S], [
                    (w1[:, k, mc * P:(mc + 1) * P], ft[:, k, :]) for k in range(KC)])
                j, jusers = gl_ring.take()
                a = act.do(lambda e, i=i, j=j, mc=mc: e.activation(
                    gl[:, j, :], banks[6 + i][:, S:2 * S], ACT.Gelu, bias=ffc[:, l, 1, mc:mc + 1]),
                    mm, jusers)
                a = dve.do(lambda e, i=i, j=j, mc=mc: e.scalar_tensor_tensor(
                    u[:, mc, :], banks[6 + i][:, 0:S], ffc[:, l, 0, mc:mc + 1], gl[:, j, :],
                    ALU.add, ALU.mult), a, u_users[0])
                gen.used(i, a)
                gl_ring.used(j, a)
                ud.append(a)
                yield
            ft_users[0] = [mm]
            wb_users[l][1] = [mm]
            if b == B - 1 and l + 1 < DEPTH:
                load_back(l + 1, 1)
            fin = []
            for tile in range(2):
                t = 2 * b + tile
                i, users = gen.take()
                mm = matmuls(c, banks[6 + i][:, 0:D], [
                    (u[:, k, tile * P:(tile + 1) * P], w2[:, k, :]) for k in range(FC)],
                    ud, wb_ready[l, 2], users)
                a = dve.do(lambda e, t=t, i=i: e.tensor_tensor(y[:, t, :], y[:, t, :],
                                                               banks[6 + i][:, 0:D], ALU.add), mm)
                gen.used(i, a)
                a = dve.do(lambda e, t=t: e.tensor_tensor(y[:, t, :], y[:, t, :], b2[:, l % 2, :],
                                                          ALU.add), a)
                fin.append(a)
                yield
            b2_users[l] = fin
            u_users[0] = [mm]
            wb_users[l][2] = [mm]
            if b == B - 1 and l + 1 < DEPTH:
                load_back(l + 1, 2)
            y_ready[b] = fin

        ready = {}
        ot_all = ot[:, :, :]
        jobs = [(l, b) for l in range(DEPTH) for b in range(B)]
        for n in range(3):
            load_back(0, n)
        for n in range(len(jobs) + 1):
            pair = []
            if n < len(jobs):
                pair.append(front(*jobs[n]))
            if n > 0:
                pair.append(back(*jobs[n - 1]))
            run(*pair)
        back_in = sp.dma(park, ot_all, c.parked, par_users[len(jobs) - 1], parked, ot_users[0])
        for t in range(NT):
            last = dve.do(lambda e, t=t: e.tensor_tensor(y[:, t, :], y[:, t, :], ot_all[:, t, :],
                                                         ALU.add), y_ready[t // 2], back_in)
        c.x_ready = last


DK = D // 2 // H
DV = D // H
TAPS = 4


def gated_linear_attention(c, name, g):
    nc = c.nc
    c.stage(name)
    pe, act, dve, pool, sp = c.lanes
    with ExitStack() as ctx:
        def sb(n, shape, dt=F32):
            return ctx.enter_context(nc.sbuf_tensor(f"{name}_{n}", shape, dt))
        taps = sb("taps", [P, KC, TAPS])
        w_in, w_out = sb("w_in", [P, KC, 3 * D]), sb("w_out", [P, KC, D])
        bg, aug = sb("bg", [P, D]), sb("aug", [P, P])
        xn, xt = sb("xn", [P, NT, D]), sb("xt", [P, KC, N])
        yc = sb("yc", [P, KC, N])
        q, kg, eg, kk = (sb(n, [P, NT, P]) for n in ("q", "kg", "eg", "kk"))
        v, gt = sb("v", [P, NT, D]), sb("gt", [P, NT, D])
        t1, t2 = sb("t1", [P, NT, P]), sb("t2", [P, NT, P])
        kd = sb("kd", [P, NT, P])
        cf = sb("cf", [P, NT, H])
        tv = sb("tv", [P, NT, D])
        o = sb("o", [P, NT, D])
        mu, var = sb("mu", [P, NT * H]), sb("var", [P, NT * H])
        ot = sb("ot", [P, KC, N])
        st = (sb("st", [P, NT, 6]), sb("mv", [P, NT, 2]), sb("rs", [P, 3, NT]))
        banks = [ctx.enter_context(nc.psum_tensor(f"{name}_bank{i}", [P, 512], F32)) for i in range(8)]
        ring = Ring(8)
        slot = c.slot(f"{name}_w")
        sp.dma(slot, taps[:, :, :], g("gla_taps").rearrange("p (k t) -> p k t", k=KC))
        sp.dma(slot, w_in[:, :, :], g("gla_win").rearrange("(k p) n -> p k n", p=P))
        sp.dma(slot, w_out[:, :, :], g("gla_wout").rearrange("(k p) n -> p k n", p=P))
        sp.dma(slot, bg[:, :], g("gla_bg"))
        w = sp.dma(slot, aug[:, :], g("gla_aug"))
        normed = layernorm(c, c.x, xn, st, c.x_ready)
        xr = to_features(c, xn, xt, normed, banks, ring)

        yr = []
        for k in range(KC):
            a = dve.do(lambda e, k=k: e.tensor_scalar(yc[:, k, :], xt[:, k, :],
                                                      taps[:, k, TAPS - 1:TAPS], None, ALU.mult), xr, w)
            for back in range(1, TAPS):
                a = dve.do(lambda e, k=k, back=back: e.scalar_tensor_tensor(
                    yc[:, k, back * S:N], xt[:, k, 0:N - back * S], taps[:, k, TAPS - 1 - back:TAPS - back],
                    yc[:, k, back * S:N], ALU.mult, ALU.add), a)
            yr.append(act.do(lambda e, k=k: e.activation(xt[:, k, :], yc[:, k, :], ACT.Silu), a))

        qr, kr, vr, gr = [], [], [], []
        for t in range(NT):
            b, users = ring.take()
            mm = matmuls(c, banks[b][:, :], [(xt[:, k, t * P:(t + 1) * P], w_in[:, k, 0:512])
                                             for k in range(KC)], yr, users)
            a1 = dve.do(lambda e, t=t, b=b: e.tensor_copy(q[:, t, :], banks[b][:, 0:P]), mm)
            a2 = dve.do(lambda e, t=t, b=b: e.tensor_copy(kg[:, t, :], banks[b][:, P:2 * P]), mm)
            a3 = act.do(lambda e, t=t, b=b: e.activation(v[:, t, :], banks[b][:, 2 * P:], ACT.Copy), a2)
            ring.used(b, a1, a2, a3)
            b, users = ring.take()
            mm = matmuls(c, banks[b][:, 0:D], [(xt[:, k, t * P:(t + 1) * P], w_in[:, k, 512:768])
                                               for k in range(KC)], users)
            a4 = dve.do(lambda e, t=t, b=b: e.tensor_tensor(gt[:, t, :], banks[b][:, 0:D], bg[:, :],
                                                            ALU.add), mm)
            ring.used(b, a4)
            qr.append(a1), kr.append(a2), vr.append(a3), gr.append(a4)

        sg = act.do(lambda e: e.activation(gt[:, :, :], gt[:, :, :], ACT.Silu), gr)
        a = act.do(lambda e: e.activation(t1[:, :, :], kg[:, :, :], ACT.Abs), kr)
        a = act.do(lambda e: e.activation(t1[:, :, :], t1[:, :, :], ACT.Exp, scale=-1.0), a)
        a = dve.do(lambda e: e.tensor_scalar(t1[:, :, :], t1[:, :, :], 1.0, None, ALU.add), a)
        a = act.do(lambda e: e.activation(t2[:, :, :], t1[:, :, :], ACT.Ln), a)
        a = dve.do(lambda e: e.scalar_tensor_tensor(t1[:, :, :], kg[:, :, :], 0.0, t2[:, :, :],
                                                    ALU.min, ALU.subtract), a)
        er = act.do(lambda e: e.activation(eg[:, :, :], t1[:, :, :], ACT.Exp, scale=1.0 / 16.0), a)
        kr = dve.do(lambda e: e.tensor_scalar(kk[:, :, :], eg[:, :, :], -1.0, 1.0, ALU.mult, ALU.add), er)

        def steps(x, s, n):
            return x[:, 2 * s:2 * (s + n), :]

        def heads(x, width):
            return x.rearrange("p t (h d) -> p (t h) d", d=width)

        a = dve.do(lambda e: e.tensor_tensor(t2[:, :, :], q[:, :, :], kk[:, :, :], ALU.mult), qr, kr)
        augb = aug[:, :].rearrange("p (o n) -> p o n", o=1).to_broadcast([P, NT, P])
        a = dve.do(lambda e: e.tensor_tensor(t2[:, :, :], t2[:, :, :], augb, ALU.mult), a)
        a = dve.do(lambda e: e.tensor_reduce(cf[:, :, :].rearrange("p t (h o) -> p (t h) o", o=1),
                                             heads(t2[:, :, :], DK), AX.X, ALU.add), a)
        cb = cf[:, :, :].rearrange("p t (h o) -> p (t h) o", o=1).to_broadcast([P, NT * H, DV])
        a = dve.do(lambda e: e.tensor_tensor(heads(o[:, :, :], DV), heads(v[:, :, :], DV), cb, ALU.mult),
                   a, vr)
        oa = act.do(lambda e: e.activation(o[:, :, :], o[:, :, :], ACT.Sigmoid), a)
        qs = dve.do(lambda e: e.tensor_scalar(q[:, :, :], q[:, :, :], float(DK) ** -0.5, None, ALU.mult), a)
        for s in range(B):
            if s:
                dec = (steps(eg, s, 1).rearrange("p t d -> p (t d)").rearrange("p (o n) -> p o n", o=1)
                       .to_broadcast([P, s, 2 * P]))
                kds = steps(kd, 0, s).rearrange("p (s t) d -> p s (t d)", t=2)
                a = dve.do(lambda e, kds=kds, dec=dec: e.tensor_tensor(kds, kds, dec, ALU.mult), a)
            a = dve.do(lambda e, s=s: e.tensor_copy(steps(kd, s, 1), steps(kk, s, 1)), a)
            qb = (steps(q, s, 1).rearrange("p t d -> p (t d)").rearrange("p (o n) -> p o n", o=1)
                  .to_broadcast([P, s + 1, 2 * P]))
            a = dve.do(lambda e, s=s, qb=qb: e.tensor_tensor(
                steps(t1, 0, s + 1).rearrange("p (s t) d -> p s (t d)", t=2),
                steps(kd, 0, s + 1).rearrange("p (s t) d -> p s (t d)", t=2), qb, ALU.mult), a, qs)
            a = dve.do(lambda e, s=s: e.tensor_reduce(
                steps(cf, 0, s + 1).rearrange("p t (h o) -> p (t h) o", o=1),
                heads(steps(t1, 0, s + 1), DK), AX.X, ALU.add), a)
            cbs = (steps(cf, 0, s + 1).rearrange("p t (h o) -> p (t h) o", o=1)
                   .to_broadcast([P, 2 * (s + 1) * H, DV]))
            a = dve.do(lambda e, s=s, cbs=cbs: e.tensor_tensor(
                heads(steps(tv, 0, s + 1), DV), heads(steps(v, 0, s + 1), DV), cbs, ALU.mult), a)
            for j in range(s + 1):
                a = dve.do(lambda e, s=s, j=j: e.tensor_tensor(
                    steps(o, s, 1), steps(o, s, 1), steps(tv, j, 1), ALU.add), a, oa)
        oh = heads(o[:, :, :], DV)
        th = heads(tv[:, :, :], DV)

        def col(x):
            return x[:, :].rearrange("p (n o) -> p n o", o=1)
        a = dve.do(lambda e: e.tensor_reduce(col(mu), oh, AX.X, ALU.add), a)
        a = dve.do(lambda e: e.tensor_scalar(mu[:, :], mu[:, :], 1.0 / DV, None, ALU.mult), a)
        a = dve.do(lambda e: e.tensor_tensor(oh, oh, col(mu).to_broadcast([P, NT * H, DV]), ALU.subtract), a)
        a2 = act.do(lambda e: e.activation(tv[:, :, :], o[:, :, :], ACT.Square), a)
        a = dve.do(lambda e: e.tensor_reduce(col(var), th, AX.X, ALU.add), a2)
        a = dve.do(lambda e: e.tensor_scalar(var[:, :], var[:, :], 1.0 / DV, LN_EPS, ALU.mult, ALU.add), a)
        a = act.do(lambda e: e.activation(mu[:, :], var[:, :], ACT.Sqrt), a)
        a = dve.do(lambda e: e.reciprocal(var[:, :], mu[:, :]), a)
        a = dve.do(lambda e: e.tensor_tensor(oh, oh, col(var).to_broadcast([P, NT * H, DV]), ALU.mult), a)
        fin = []
        for t in range(NT):
            fin.append(dve.do(lambda e, t=t: e.tensor_tensor(o[:, t, :], o[:, t, :], gt[:, t, :],
                                                             ALU.mult), a, sg))
        orr = to_features(c, o, ot, fin, banks, ring)
        for t in range(NT):
            b, users = ring.take()
            mm = matmuls(c, banks[b][:, 0:D], [(ot[:, k, t * P:(t + 1) * P], w_out[:, k, :])
                                               for k in range(KC)], orr[t // 4], users)
            last = dve.do(lambda e, t=t, b=b: e.tensor_tensor(c.x[:, t, :], c.x[:, t, :],
                                                              banks[b][:, 0:D], ALU.add), mm)
            ring.used(b, last)
        c.x_ready = last


EXPERTS, GROUPS, TOP_GROUPS, TOP = 64, 8, 4, 8
GE = EXPERTS // GROUPS
FI = 128
CAP = 256
ROUTE_SCALE = 2.5
OUT = -1e30
TAKEN = -3e38


def experts(c, name, g):
    nc = c.nc
    c.stage(name)
    pe, act, dve, pool, sp = c.lanes
    NW = 3
    with ExitStack() as ctx:
        def sb(n, shape, dt=F32):
            return ctx.enter_context(nc.sbuf_tensor(f"{name}_{n}", shape, dt))
        gw, gb = sb("gw", [P, KC, EXPERTS]), sb("gb", [P, EXPERTS])
        upper, ones = sb("upper", [P, P]), sb("ones", [P, P])
        xn, xt = sb("xn", [P, NT, D]), sb("xt", [P, KC, N])
        sc, sf, pick = (sb(n, [P, NT, EXPERTS]) for n in ("sc", "sf", "pick"))
        srt = sb("srt", [P, NT, GROUPS, 8])
        gs, gm, g8, v8 = (sb(n, [P, NT, 8]) for n in ("gs", "gm", "g8", "v8"))
        wt, den = sb("wt", [P, NT, EXPERTS]), sb("den", [P, 2, NT])
        wg, wu, wd = sb("wg", [P, NW, KC, FI]), sb("wu", [P, NW, KC, FI]), sb("wd", [P, NW, D])
        sg, hh = sb("sg", [P, 2, 512]), sb("hh", [P, 2, 512])
        st = (sb("st", [P, NT, 6]), sb("mv", [P, NT, 2]), sb("rs", [P, 3, NT]))
        banks = [ctx.enter_context(nc.psum_tensor(f"{name}_bank{i}", [P, 512], F32)) for i in range(8)]
        ring = Ring(8)
        slot = c.slot(f"{name}_w")
        w_slot = [c.slot(f"{name}_w{i}") for i in range(NW)]
        sp.dma(slot, gw[:, :, :], g("moe_gw").rearrange("(k p) n -> p k n", p=P))
        sp.dma(slot, gb[:, :], g("moe_gb"))
        w = sp.dma(slot, upper[:, :], g("upper"))
        w_ring = Ring(NW)

        def load(e_):
            i, users = w_ring.take()
            sp.dma(w_slot[i], wg[:, i, :, :], g("moe_wg")[e_].rearrange("(k p) n -> p k n", p=P), users)
            sp.dma(w_slot[i], wu[:, i, :, :], g("moe_wu")[e_].rearrange("(k p) n -> p k n", p=P))
            return i, sp.dma(w_slot[i], wd[:, i, :], g("moe_wd")[e_])
        loaded = {e_: load(e_) for e_ in range(NW - 1)}
        one = dve.do(lambda e: e.memset(ones[:, :], 1.0))
        normed = layernorm(c, c.x, xn, st, c.x_ready)
        xr = to_features(c, xn, xt, normed, banks, ring)
        sr = []
        for t in range(NT):
            b, users = ring.take()
            mm = matmuls(c, banks[b][:, 0:EXPERTS], [(xt[:, k, t * P:(t + 1) * P], gw[:, k, :])
                                                     for k in range(KC)], xr[t // 4], w, users)
            a = act.do(lambda e, t=t, b=b: e.activation(sc[:, t, :], banks[b][:, 0:EXPERTS],
                                                        ACT.Sigmoid), mm)
            ring.used(b, a)
            sr.append(dve.do(lambda e, t=t: e.tensor_tensor(sf[:, t, :], sc[:, t, :], gb[:, :], ALU.add), a))
        for t in range(NT):
            for gr in range(GROUPS):
                a = dve.do(lambda e, t=t, gr=gr: e.max(srt[:, t, gr, :], sf[:, t, gr * GE:(gr + 1) * GE]),
                           sr[t])
        a = dve.do(lambda e: e.tensor_tensor(gs[:, :, :], srt[:, :, :, 0], srt[:, :, :, 1], ALU.add), a)
        for t in range(NT):
            a1 = dve.do(lambda e, t=t: e.max(g8[:, t, :], gs[:, t, :]), a)
        a1 = dve.do(lambda e: e.memset(g8[:, :, TOP_GROUPS:], -OUT), a1)
        for t in range(NT):
            a2 = dve.do(lambda e, t=t: e.match_replace(gm[:, t, :], g8[:, t, :], gs[:, t, :], TAKEN), a1)
        a2 = dve.do(lambda e: e.tensor_scalar(gm[:, :, :], gm[:, :, :], TAKEN / 2, OUT, ALU.is_gt, ALU.mult), a2)
        gmb = gm[:, :, :].rearrange("p t (g o) -> p (t g) o", o=1).to_broadcast([P, NT * GROUPS, GE])
        a = dve.do(lambda e: e.tensor_tensor(
            sf[:, :, :].rearrange("p t (g j) -> p (t g) j", j=GE),
            sf[:, :, :].rearrange("p t (g j) -> p (t g) j", j=GE), gmb, ALU.add), a2)
        for t in range(NT):
            a1 = dve.do(lambda e, t=t: e.max(v8[:, t, :], sf[:, t, :]), a)
        for t in range(NT):
            a2 = dve.do(lambda e, t=t: e.match_replace(pick[:, t, :], v8[:, t, :], sf[:, t, :], TAKEN), a1)
        pr = dve.do(lambda e: e.tensor_scalar(pick[:, :, :], pick[:, :, :], TAKEN / 2, None, ALU.is_lt), a2)
        a = dve.do(lambda e: e.tensor_tensor(wt[:, :, :], sc[:, :, :], pick[:, :, :], ALU.mult), pr)
        a = dve.do(lambda e: e.tensor_reduce(den[:, 0, :].rearrange("p (t o) -> p t o", o=1),
                                             wt[:, :, :], AX.X, ALU.add), a)
        a = dve.do(lambda e: e.tensor_scalar(den[:, 0, :], den[:, 0, :], 1e-20, None, ALU.add), a)
        a = dve.do(lambda e: e.reciprocal(den[:, 1, :], den[:, 0, :]), a)
        for t in range(NT):
            wr = dve.do(lambda e, t=t: e.tensor_scalar(wt[:, t, :], wt[:, t, :], den[:, 1, t:t + 1],
                                                      ROUTE_SCALE, ALU.mult, ALU.mult), a)
        for t in range(NT):
            b, users = ring.take()
            mm = matmuls(c, banks[b][:, 0:EXPERTS],
                         [(ones[:, :], pick[:, j, :]) for j in range(t)] + [(upper[:, :], pick[:, t, :])],
                         pr, one, w, users)
            a = dve.do(lambda e, t=t, b=b: e.scalar_tensor_tensor(
                wt[:, t, :], banks[b][:, 0:EXPERTS], CAP + 0.5, wt[:, t, :], ALU.is_lt, ALU.mult),
                mm, wr)
            ring.used(b, a)
        w_done = a
        up_ring, y_ring, h_ring = Ring(2), Ring(4), Ring(2)
        for i in range(8):
            (up_ring.used(i // 2, ring.users[i]) if i < 4 else y_ring.used(i - 4, ring.users[i]))

        def up(e_, half):
            i, m = loaded[e_]
            b, users = up_ring.take()
            pairs = [(wg[:, i, k, :], xt[:, k, half * 512:(half + 1) * 512]) for k in range(KC)]
            m1 = matmuls(c, banks[2 * b][:, :], pairs, m, xr, users)
            pairs = [(wu[:, i, k, :], xt[:, k, half * 512:(half + 1) * 512]) for k in range(KC)]
            m2 = matmuls(c, banks[2 * b + 1][:, :], pairs)
            h, husers = h_ring.take()
            a = act.do(lambda e: e.activation(sg[:, h, :], banks[2 * b][:, :], ACT.Silu), m1, husers)
            a = dve.do(lambda e: e.tensor_tensor(hh[:, h, :], sg[:, h, :], banks[2 * b + 1][:, :],
                                                 ALU.mult), a, m2)
            up_ring.used(b, a)
            return e_, half, h, a

        def down(e_, half, h, a):
            i, _ = loaded[e_]
            for p in range(2):
                y, users = y_ring.take()
                for j in range(2):
                    t = 4 * half + 2 * p + j
                    mm = pe.do(lambda e, j=j, y=y, t=t: e.matmul(
                        banks[4 + y][:, j * D:(j + 1) * D], hh[:, h, (t % 4) * P:(t % 4 + 1) * P],
                        wd[:, i, :], start=True, stop=True), a, users, count=(j == 1))
                for j in range(2):
                    t = 4 * half + 2 * p + j
                    s = dve.do(lambda e, j=j, y=y, t=t: e.scalar_tensor_tensor(
                        c.x[:, t, :], banks[4 + y][:, j * D:(j + 1) * D], wt[:, t, e_:e_ + 1],
                        c.x[:, t, :], ALU.mult, ALU.add), mm, w_done, acc.get(t))
                    acc[t] = s
                y_ring.used(y, s)
            h_ring.used(h, mm)
            w_ring.used(i, mm)
            return s
        acc = {}
        pending = None
        for e_ in range(EXPERTS):
            for half in range(2):
                if half == 1 and e_ + NW - 1 < EXPERTS:
                    loaded[e_ + NW - 1] = load(e_ + NW - 1)
                unit = up(e_, half)
                if pending is not None:
                    down(*pending)
                pending = unit
        last = down(*pending)
        c.x_ready = last


def scratch_tensors(nc):
    return {"keys": nc.dram_tensor("keys", (2 * B * (SK // 1024), 3, P, 1024), BF16, kind="Internal").ap(),
            "parked": nc.dram_tensor("parked", (P, NT, D), F32, kind="Internal").ap()}


def head_rows(w):
    w = np.asarray(w)
    z = np.zeros(w.shape[:-1] + (H, 32), w.dtype)
    z[..., 0:16] = w.reshape(w.shape[:-1] + (H, 16))
    return np.ascontiguousarray(z.reshape(w.shape[:-1] + (2 * D,)))


def more_layout(a, o, rows, cols):
    w, b = a["L0_attn_Wqkv_w"], a["L0_attn_Wqkv_b"]
    for i, n in enumerate("qkv"):
        o[f"ca_w{n}"] = head_rows(w[i * D:(i + 1) * D].T)
    o["ca_bv"] = rows(head_rows(b[2 * D:]))
    o["ca_cols"] = np.ascontiguousarray(np.concatenate(
        [cols(head_rows(v)) for v in (b[0:D], b[D:2 * D], a["L0_attn_conv_b"])], 1))
    cw = a["L0_attn_conv_w"].transpose(2, 1, 0)
    cw = head_rows(cw)
    o["ca_cw"] = np.ascontiguousarray(head_rows(cw.transpose(0, 2, 1)).transpose(0, 2, 1))
    o["ca_wo"] = np.ascontiguousarray(head_rows(a["L0_attn_out_w"]).T)
    o["ca_bo"] = rows(a["L0_attn_out_b"])
    i, j = np.arange(P)[:, None], np.arange(2 * P)[None, :]
    o["causal"] = np.where(np.concatenate([j[:, :P] <= i, j <= i + P], 1), 0, NEG).astype(np.float32)
    f = np.float32
    o["lt_wqkv"] = a["L0_ffn_Wqkv"]
    o["lt_wo"] = a["L0_ffn_Wo"]
    w1 = np.zeros((DEPTH, D, 2, FFP), f)
    w1[..., :FF] = a["L0_ffn_W1"].reshape(DEPTH, D, 2, FF)
    o["lt_w1"] = w1.reshape(DEPTH, D, 2 * FFP)
    w2 = np.zeros((DEPTH, FFP, D), f)
    w2[:, :FF] = a["L0_ffn_W2"]
    o["lt_w2"] = w2
    b1 = np.zeros((DEPTH, 2, FFP), f)
    b1[..., :FF] = a["L0_ffn_b1"].reshape(DEPTH, 2, FF)
    o["lt_ffc"] = np.ascontiguousarray(b1.reshape(-1, P).T)
    ln = np.stack([a["L0_ffn_ln_g"], a["L0_ffn_ln_b"]], 1)
    o["lt_lnc"] = np.ascontiguousarray(ln.reshape(-1, P).T)
    o["lt_b2"] = np.ascontiguousarray(np.broadcast_to(a["L0_ffn_b2"][:, None], (DEPTH, P, D)))
    qs, ks = a["L0_ffn_q_scale"], a["L0_ffn_k_scale"]
    scl = np.stack([qs, np.roll(qs, 32, 1), ks, np.roll(ks, 32, 1)], 1).reshape(DEPTH, 1, 4 * LH)
    o["lt_scl"] = np.ascontiguousarray(np.broadcast_to(scl, (DEPTH, P, 4 * LH)))
    half = np.arange(0, LH, 2, dtype=f)
    t = np.arange(S, dtype=f)
    freqs = t[:, None] * (f(1) / f(10000) ** (half / f(LH)))[None, :]
    base = (half + f(0.4 * LH)) / f(1.4 * LH)
    scale = base[None, :] ** ((t - S // 2) / f(32))[:, None]
    cos, sin = np.cos(freqs), np.sin(freqs)
    two = lambda p, q: np.concatenate([p, q], 1)
    rot = np.stack([two(cos * scale, cos * scale), two(-sin * scale, sin * scale),
                    two(cos / scale, cos / scale), two(-sin / scale, sin / scale)])
    o["lt_rot"] = np.ascontiguousarray(
        rot.reshape(4, 2, P, LH).transpose(2, 0, 1, 3).reshape(P, -1).astype(f))
    band = np.concatenate([(j[:, :P] <= i) & (j[:, :P] >= i - 64),
                           (j <= i + P) & (j >= i + P - 64)], 1)
    o["band"] = np.where(band, 0, NEG).astype(f)
    o["gla_taps"] = np.ascontiguousarray(
        a["L1_attn_conv_w"].reshape(KC, P, TAPS).transpose(1, 0, 2).reshape(P, -1))
    o["gla_win"] = np.ascontiguousarray(np.concatenate(
        [a[f"L1_attn_W{n}"] for n in ("q", "kg", "v", "g")], 1))
    o["gla_wout"] = a["L1_attn_Wout"]
    o["gla_bg"] = rows(a["L1_attn_bg"])
    o["gla_aug"] = rows(a["L1_attn_aug_balance"])
    o["moe_gw"] = np.ascontiguousarray(a["L1_ffn_gate_w"].T)
    o["moe_gb"] = rows(a["L1_ffn_gate_bias"])
    o["moe_wg"], o["moe_wu"], o["moe_wd"] = (a[f"L1_ffn_w_{n}"] for n in ("gate", "up", "down"))
    o["upper"] = np.triu(np.ones((P, P), np.float32))


def build(nc, ins, out, scratch, first=0, last=5):
    with ExitStack() as ctx:
        c = Core(nc, ctx)
        sb = lambda n, shape, dt=F32: ctx.enter_context(nc.sbuf_tensor(n, shape, dt))
        c.x = sb("x_sb", [P, NT, D])
        c.parked = scratch["parked"]
        c.minus_half = sb("minus_half", [P, 64])
        c.ident = sb("ident", [P, P])
        c.ident_bf = sb("ident_bf", [P, P], BF16)
        c.stage("load")
        s = c.slot("load")
        c.sp.dma(s, c.x[:, :, :], ins["x"].rearrange("b (q p) d -> p (b q) d", p=P))
        m = c.sp.dma(s, c.ident[:, :], ins["ident"])
        half = c.dve.do(lambda e: e.memset(c.minus_half[:, :], -0.5))
        c.x_ready = [m, half]
        c.ident_ready = c.dve.do(lambda e: e.tensor_copy(c.ident_bf[:, :], c.ident[:, :]), m)
        g = ins.get
        for i in range(first, last + 1):
            STAGES[i](c, g, scratch)
        c.stage("store")
        s = c.slot("store")
        m = c.sp.dma(s, out.rearrange("b (q p) d -> p (b q) d", p=P), c.x[:, :, :])
        c.sp.hold(m)
        with nc.Block() as block:
            block.sync(lambda e: c.sp.replay(e))
            block.gpsimd(lambda e: c.pool.replay(e))
            block.scalar(lambda e: c.act.replay(e))
            block.vector(lambda e: c.dve.replay(e))
            block.tensor(lambda e: c.pe.replay(e))


STAGES = [
    lambda c, g, d: cross_attention(c, "xa0", g("ctx_t"), g("xa0_wq"), g("xa0_wk"), g("xa0_wv"), g("xa0_wo"),
                                 g("xa0_bq"), g("xa0_bk"), g("xa0_bv"), g("xa0_bo"), d["keys"]),
    lambda c, g, d: conv_attention(c, "ca", g),
    lambda c, g, d: local_transformer(c, "lt", g),
    lambda c, g, d: cross_attention(c, "xa1", g("ctx_t"), g("xa1_wq"), g("xa1_wk"), g("xa1_wv"), g("xa1_wo"),
                                 None, None, None, g("xa1_bo"), d["keys"]),
    lambda c, g, d: gated_linear_attention(c, "gla", g),
    lambda c, g, d: experts(c, "moe", g),
]


def layout(inputs):
    a = {k: np.asarray(v) for k, v in inputs.items()}

    def rows(v):
        return np.ascontiguousarray(np.broadcast_to(v, (P, v.shape[-1])))

    def cols(v):
        return np.ascontiguousarray(v.reshape(-1, P).T)

    o = {"x": a["x"], "ident": np.eye(P, dtype=np.float32)}
    o["ctx_t"] = np.ascontiguousarray(a["ctx_1024"].transpose(0, 2, 1))
    for n in "qkvo":
        o[f"xa0_w{n}"] = np.ascontiguousarray(a[f"L0_xattn_w_{n}"].T)
        o[f"xa1_w{n}"] = np.ascontiguousarray(a[f"L1_xattn_W{n}"].T)
    for n in "qvo":
        o[f"xa0_b{n}"] = rows(a[f"L0_xattn_b_{n}"])
    o["xa0_bk"] = cols(a["L0_xattn_b_k"])
    o["xa1_bo"] = rows(a["L1_xattn_bo"])
    more_layout(a, o, rows, cols)
    return o


def kernel(**inputs):
    import concourse.bacc as bacc
    from concourse.bass_utils import run_bass_kernel_spmd

    nc = bacc.Bacc("TRN2", target_bir_lowering=False, num_devices=1)
    arrays = layout(inputs)
    ins = {k: nc.dram_tensor(f"in_{k}", v.shape, mybir.dt.from_np(v.dtype), kind="ExternalInput").ap()
           for k, v in arrays.items()}
    out = nc.dram_tensor("result", (B, S, D), F32, kind="ExternalOutput").ap()
    build(nc, ins, out, scratch_tensors(nc))
    r = run_bass_kernel_spmd(nc, [{f"in_{k}": v for k, v in arrays.items()}], core_ids=[0])
    return r.results[0]["result"]
```

```python
from contextlib import ExitStack

import numpy as np

import concourse.bass as bass
from concourse import mybir

F32 = mybir.dt.float32
BF16 = mybir.dt.bfloat16
ALU = mybir.AluOpType
ACT = mybir.ActivationFunctionType
AX = mybir.AxisListType

P = 128
B, S, D = 4, 256, 256
N = B * S
NT = N // P
KC = D // P
H = 16
SK = 4096
LN_EPS = 1e-5
NEG = -1e30


class Mark:

    def __init__(self, sem, value):
        self.sem, self.value = sem, value


def flat(marks):
    for m in marks:
        if m is None:
            continue
        if isinstance(m, Mark):
            yield m
        else:
            yield from flat(m)


class Lane:

    def __init__(self, name):
        self.name, self.queue, self.sem, self.count = name, [], None, 0

    def use(self, sem):
        self.sem, self.count = sem, 0

    def do(self, build, *waits, count=True):
        self.queue.append((list(flat(waits)), build, self.sem if count else None, 1))
        if not count:
            return None
        self.count += 1
        return Mark(self.sem, self.count)

    def dma(self, slot, dst, src, *waits):
        self.queue.append((list(flat(waits)), lambda e: e.dma_start(dst, src), slot.sem, 16))
        slot.count += 16
        return Mark(slot.sem, slot.count)

    def hold(self, *waits):
        self.queue.append((list(flat(waits)), None, None, 0))

    def last(self):
        return Mark(self.sem, self.count) if self.count else None

    def replay(self, engine):
        reached = {}
        for waits, build, sem, step in self.queue:
            for m in waits:
                if reached.get(m.sem.name, 0) < m.value:
                    engine.wait_ge(m.sem, m.value)
                    reached[m.sem.name] = m.value
            if build is not None:
                ins = build(engine)
                if sem is not None:
                    ins.then_inc(sem, step)


class Slot:

    def __init__(self, sem):
        self.sem, self.count = sem, 0


class Ring:

    def __init__(self, n):
        self.users, self.at = [[] for _ in range(n)], -1

    def take(self):
        self.at = (self.at + 1) % len(self.users)
        users, self.users[self.at] = self.users[self.at], []
        return self.at, users

    def used(self, i, *marks):
        self.users[i] += list(flat(marks))


class Core:

    def __init__(self, nc, ctx):
        self.nc, self.ctx = nc, ctx
        self.pe, self.act, self.dve, self.pool, self.sp = (
            Lane(n) for n in ("pe", "act", "dve", "pool", "sp"))
        self.lanes = (self.pe, self.act, self.dve, self.pool, self.sp)
        self.nsem = 0
        self.slots = []

    def sem(self, name):
        self.nsem += 1
        return self.ctx.enter_context(self.nc.semaphore(f"{name}_{self.nsem}"))

    def slot(self, name):
        s = Slot(self.sem(name))
        self.slots.append(s)
        return s

    def stage(self, name):
        ends = [l.last() for l in self.lanes if l.sem is not None]
        ends += [Mark(s.sem, s.count) for s in self.slots if s.count]
        for lane in self.lanes:
            lane.hold(ends)
            lane.use(self.sem(f"{name}_{lane.name}"))


def rsqrt(c, out, src, n, *waits):
    return c.pool.do(lambda e: e.tensor_tensor(out, src, c.minus_half[:, 0:n], ALU.pow), *waits)


def layernorm(c, src, dst, st, ready):
    stats, mv, rs = st
    for t in range(NT):
        a = c.dve.do(lambda e, t=t: e.bn_stats(stats[:, t, :], src[:, t, :]), ready)
        last = c.dve.do(lambda e, t=t: e.bn_aggr(mv[:, t, :], stats[:, t, :]), a)
    a = c.dve.do(lambda e: e.tensor_scalar(rs[:, 0, :], mv[:, :, 1], LN_EPS, None, ALU.add), last)
    a = rsqrt(c, rs[:, 2, :], rs[:, 0, :], NT, a)
    out = []
    for t in range(NT):
        out.append(c.dve.do(lambda e, t=t: e.tensor_scalar(
            dst[:, t, :], src[:, t, :], mv[:, t, 0:1], rs[:, 2, t:t + 1],
            ALU.subtract, ALU.mult), a))
    return out


def to_features(c, src, dst, ready, banks, ring, affine=None, tiles=NT, lanes=None):
    width = src.shape[2] if len(src.shape) == 3 else D
    out = []
    for g in range(tiles // 4):
        group = []
        for k in range(width // P):
            b, users = ring.take()
            for j in range(4):
                t = 4 * g + j
                tr = c.pe.do(lambda e, t=t, k=k, j=j, b=b: e.transpose(
                    banks[b][:, j * P:(j + 1) * P], src[:, t, k * P:(k + 1) * P], c.ident[:, :]),
                    ready[t], users, c.ident_ready, count=(j == 3))
            o = dst[:, k, g * 512:(g + 1) * 512]
            if affine is not None:
                gain, bias = affine
                ev = c.dve.do(lambda e, o=o, b=b, k=k: e.tensor_scalar(
                    o, banks[b][:, :], gain[:, k:k + 1], bias[:, k:k + 1], ALU.mult, ALU.add), tr)
            elif k % 2:
                ev = c.act.do(lambda e, o=o, b=b: e.activation(o, banks[b][:, :], ACT.Copy), tr)
            else:
                ev = c.dve.do(lambda e, o=o, b=b: e.tensor_copy(o, banks[b][:, :]), tr)
            ring.used(b, ev)
            group.append(ev)
        out.append(group)
    return out


def matmuls(c, out, pairs, *waits):
    n = len(pairs)
    for i, (l, r) in enumerate(pairs):
        m = c.pe.do(lambda e, i=i, l=l, r=r: e.matmul(out, l, r, start=(i == 0), stop=(i == n - 1)),
                    waits if i == 0 else [], count=(i == n - 1))
    return m


def cross_attention(c, name, ctx_t, wq, wk, wv, wo, bq, bk, bv, bo, kscratch):
    nc = c.nc
    KB = 1024
    NKB = SK // KB
    ITEMS = B * NKB
    DH = D // H
    STACK = 6 * DH
    ROWS = STACK + 3
    Q_PART = (0, 1, 0, 1, 2, 0)
    K_PART = (0, 0, 1, 1, 0, 2)
    KT = KB // P
    QUADS = H // 4
    SLOTS = QUADS * KT
    VW = DH + 1
    NU = 5
    NV = 3
    c.stage(name)
    pe, act, dve, pool, sp = c.lanes
    outer = ExitStack()
    att = outer.enter_context(nc.sbuf_tensor(f"{name}_att", [P, NT, D], F32))
    with ExitStack() as long:
        def sb(n, shape, dt=F32, ctx=long):
            return ctx.enter_context(nc.sbuf_tensor(f"{name}_{n}", shape, dt))

        def ps(n, shape, dt=F32, ctx=long):
            return ctx.enter_context(nc.psum_tensor(f"{name}_{n}", shape, dt))

        q_base = sb("q_base", [P, H, N], BF16)
        wk_sb, wv_sb = sb("wk", [P, KC, D]), sb("wv", [P, KC, D])
        w_slot = c.slot(f"{name}_w")
        w_mark = sp.dma(w_slot, wk_sb[:, :, :], wk.rearrange("(k p) n -> p k n", p=P))
        w_mark = sp.dma(w_slot, wv_sb[:, :, :], wv.rearrange("(k p) n -> p k n", p=P))
        if bk is not None:
            bk_sb = sb("bk", [P, KC])
            w_mark = sp.dma(w_slot, bk_sb[:, :], bk)
        with ExitStack() as short:
            xn = sb("xn", [P, NT, D], ctx=short)
            xt = sb("xt", [P, KC, N], ctx=short)
            wq_sb = sb("wq", [P, KC, D], ctx=short)
            st = (sb("st", [P, NT, 6], ctx=short), sb("mv", [P, NT, 2], ctx=short),
                  sb("rs", [P, 3, NT], ctx=short))
            qf = sb("qf", [P, 2, 4, D], ctx=short)
            qr = sb("qr", [P, 2, 4, D], ctx=short)
            qtm = sb("qtm", [P, 2, 4 * H, STACK], BF16, ctx=short)
            bq_sb = sb("bq", [P, D], ctx=short)
            banks = [ps(f"bank{i}", [P, 512], ctx=short) for i in range(4)]
            tbank = [ps(f"tbank{i}", [P, 8, P], BF16, ctx=short) for i in range(4)]
            ring, tring = Ring(4), Ring(4)
            q_slot = c.slot(f"{name}_wq")
            wq_mark = sp.dma(q_slot, wq_sb[:, :, :], wq.rearrange("(k p) n -> p k n", p=P))
            if bq is not None:
                wq_mark = sp.dma(q_slot, bq_sb[:, :], bq)
            normed = layernorm(c, c.x, xn, st, c.x_ready)
            xt_ready = to_features(c, xn, xt, normed, banks, ring)
            for grp in range(NT // 4):
                got = []
                for pair in range(2):
                    b, users = ring.take()
                    for j in range(2):
                        t = 4 * grp + 2 * pair + j
                        mm = matmuls(c, banks[b][:, j * D:(j + 1) * D],
                                     [(xt[:, k, t * P:(t + 1) * P], wq_sb[:, k, :]) for k in range(KC)],
                                     xt_ready[grp], wq_mark, users)
                    f2 = qf[:, grp, 2 * pair:2 * pair + 2, :]
                    p2 = banks[b][:, :].rearrange("p (j n) -> p j n", j=2)
                    if bq is not None:
                        bqb = bq_sb[:, :].rearrange("p (o n) -> p o n", o=1).to_broadcast([P, 2, D])
                        a = dve.do(lambda e, f2=f2, p2=p2, bqb=bqb: e.tensor_tensor(f2, p2, bqb, ALU.add), mm)
                    else:
                        a = dve.do(lambda e, f2=f2, p2=p2: e.tensor_copy(f2, p2), mm)
                    ring.used(b, a)
                    got.append(a)

                def part(j, grp=grp):
                    return qtm[:, grp, :, j * DH:(j + 1) * DH]
                f3 = qf[:, grp, :, :].rearrange("p t (h d) -> p (t h) d", d=DH)
                r3 = qr[:, grp, :, :].rearrange("p t (h d) -> p (t h) d", d=DH)
                a0 = act.do(lambda e, o=part(0), f3=f3: e.activation(o, f3, ACT.Copy, scale=0.25), got)
                a = dve.do(lambda e, r3=r3, f3=f3, o=part(0): e.scalar_tensor_tensor(
                    r3, f3, 0.25, o, ALU.mult, ALU.subtract), a0)
                a1 = act.do(lambda e, o=part(1), r3=r3: e.activation(o, r3, ACT.Copy), a)
                a2 = dve.do(lambda e, r3=r3, o=part(4), s=part(1): e.tensor_tensor(
                    o, r3, s, ALU.subtract), a1)
                done = [a2, pool.do(lambda e, o=part(2), s=part(0): e.tensor_copy(o, s), a0),
                        act.do(lambda e, o=part(5), s=part(0): e.activation(o, s, ACT.Copy), a0),
                        dve.do(lambda e, o=part(3), s=part(1): e.tensor_copy(o, s), a1)]
                for g in range(H // 2):
                    tb, tusers = tring.take()
                    for j in range(8):
                        hh, t = divmod(j, 4)
                        tr = pe.do(lambda e, tb=tb, j=j, hh=hh, t=t, g=g, grp=grp: e.transpose(
                            tbank[tb][0:STACK, j, :], qtm[:, grp, t * H + 2 * g + hh, :], c.ident_bf[:, :]),
                            done, tusers, c.ident_ready, count=(j == 7))
                    src = tbank[tb][0:STACK, :, :].rearrange("p (h t) n -> p h (t n)", h=2)
                    dst = q_base[0:STACK, 2 * g:2 * g + 2, grp * 512:(grp + 1) * 512]
                    if g % 2:
                        ev = act.do(lambda e, dst=dst, src=src: e.activation(dst, src, ACT.Copy), tr)
                    else:
                        ev = dve.do(lambda e, dst=dst, src=src: e.tensor_copy(dst, src), tr)
                    tring.used(tb, ev)
        c.stage(f"{name}_blocks")
        ks = sb("ks", [P, NU, 8, KB], BF16)
        vs = sb("vs", [P, NV, KT, H, VW])
        cx = sb("cx", [P, 2, KC, KB])
        ex = sb("ex", [P, 2, 4, S])
        kp = sb("kp", [P, 2, 3, 512], BF16)
        kr = sb("kr", [P, 512])
        o_sb = sb("o_sb", [P, 2, S])
        o_all = sb("o_all", [P, NKB, 2, H, VW])
        m_part = sb("m_part", [P, 2, 2, H, 2])
        m_blk2 = sb("m_blk", [P, 2, 2, H, NKB])
        m_spl = sb("m_spl", [P, 2, 8, 4])
        mt_bf = sb("mt_bf", [P, 2, 8, 3], BF16)
        w_blk = sb("w_blk", [P, 2, H, NKB])
        m_all = sb("m_all", [P, 2, H])
        acc = sb("acc", [P, 2, H, VW])
        sc = [ps(f"sc{i}", [P, 4, S]) for i in range(2)]
        mx = [ps(f"mx{i}", [P, 512]) for i in range(2)]
        pv = ps("pv", [P, S])
        pj = ps("pj", [P, 512])
        pj_bf = pj[:, :].bitcast(BF16)
        sc_ring, mx_ring, pv_ring, pj_ring = Ring(2), Ring(2), Ring(1), Ring(1)
        ks_ring, vs_ring, cx_ring, ex_ring, kp_ring, o_ring = (
            Ring(NU), Ring(NV), Ring(2), Ring(2), Ring(2), Ring(2))
        mp_ring, ms_ring = Ring(2), Ring(2)
        ks_slot = [c.slot(f"{name}_ks{i}") for i in range(NU)]
        cx_slot = [c.slot(f"{name}_cx{i}") for i in range(2)]
        kd_slot = [c.slot(f"{name}_kd{i}") for i in range(4)]
        ones_k = pool.do(lambda e: e.memset(ks[96:128, :, :, :], 1.0))
        init = [pool.do(lambda e: e.memset(vs[:, :, :, :, DH:VW], 1.0), ones_k),
                dve.do(lambda e: e.memset(pv[:, :], 0.0))]
        ctx_r = ctx_t.rearrange("b (k p) s -> b p k s", p=P)

        item = [dict() for _ in range(ITEMS)]
        q_m_users = [[] for _ in range(QUADS)]
        blk_users = []
        m_blk_users = [[], []]
        att_ready = []

        def load_ctx(i):
            b, kb = divmod(i, NKB)
            s, users = cx_ring.take()
            item[i]["cx"] = s
            item[i]["cx_ready"] = sp.dma(cx_slot[s], cx[:, s, :, :],
                                         ctx_r[b, :, :, kb * KB:(kb + 1) * KB], users)

        def project_keys(i, mt, ch):
            b, kb = divmod(i, NKB)
            s = item[i]["cx"]
            _, users = pj_ring.take()
            mm = matmuls(c, pj[:, :],
                         [(wk_sb[:, k, mt * P:(mt + 1) * P], cx[:, s, k, ch * 512:(ch + 1) * 512])
                          for k in range(KC)], item[i]["cx_ready"], w_mark, users)
            cx_ring.used(s, mm)
            p, pusers = kp_ring.take()
            bias = bk_sb[:, mt:mt + 1] if bk is not None else 0.0
            if bk is not None:
                a = act.do(lambda e: e.activation(kp[:, p, 0, :], pj[:, :], ACT.Identity, bias=bias),
                           mm, pusers)
            else:
                a = act.do(lambda e: e.activation(kp[:, p, 0, :], pj[:, :], ACT.Copy), mm, pusers)
            r = dve.do(lambda e: e.scalar_tensor_tensor(
                kr[:, :], pj[:, :], bias, kp[:, p, 0, :], ALU.add, ALU.subtract),
                a, item[i].get("kr_users"), c.kr_users)
            pj_ring.used(0, a, r)
            a2 = pool.do(lambda e: e.tensor_copy(kp[:, p, 1, :], kr[:, :]), r, pusers)
            a3 = pool.do(lambda e: e.tensor_tensor(
                kp[:, p, 2, :], kr[:, :], kp[:, p, 1, :], ALU.subtract), a2)
            c.kr_users = [a3]
            d = (2 * i + mt) % 2
            out = sp.dma(kd_slot[2 * d + ch], kscratch[2 * i + mt, :, :, ch * 512:(ch + 1) * 512]
                         .rearrange("c p n -> p c n"), kp[:, p, :, :], a, a2, a3)
            kp_ring.used(p, out)
            item[i].setdefault(("k", mt), []).append(out)

        def stack_keys(i, mt):
            u, users = ks_ring.take()
            item[i][("unit", mt)] = u
            for j, part in enumerate(K_PART):
                m = sp.dma(ks_slot[u], ks[DH * j:DH * (j + 1), u, :, :],
                           kscratch[2 * i + mt, part, :, :].rearrange("(h d) n -> d h n", d=DH),
                           users, item[i][("k", mt)])
            item[i][("ready", mt)] = m

        def project_values(i, t):
            s = item[i]["cx"]
            if t == 0:
                item[i]["vs"], item[i]["vs_users"] = vs_ring.take()
                item[i]["v_ready"] = []
            v = item[i]["vs"]
            _, users = pj_ring.take()
            mm = matmuls(c, pj[:, 0:D],
                         [(cx[:, s, k, t * P:(t + 1) * P], wv_sb[:, k, :]) for k in range(KC)],
                         item[i]["cx_ready"], w_mark, users)
            cx_ring.used(s, mm)
            a = act.do(lambda e: e.activation(
                vs[:, v, t, :, 0:DH], pj[:, 0:D].rearrange("p (h d) -> p h d", d=DH), ACT.Copy),
                mm, item[i]["vs_users"], init)
            pj_ring.used(0, a)
            item[i]["v_ready"].append(a)

        def block_max(i, h, qt):
            b, kb = divmod(i, NKB)
            mt, hl = divmod(h, 8)
            u = item[i][("unit", mt)]
            par = i % 2
            if h == 0 and qt == 0:
                item[i]["mx"] = []
            for ch in range(2):
                s, users = mx_ring.take()
                mm = pe.do(lambda e, s=s, ch=ch: e.matmul(
                    mx[s][:, :], q_base[0:STACK, h, b * S + qt * P:b * S + (qt + 1) * P],
                    ks[0:STACK, u, hl, ch * 512:(ch + 1) * 512], start=True, stop=True),
                    item[i][("ready", mt)], users)
                r = dve.do(lambda e, s=s, ch=ch: e.tensor_reduce(
                    m_part[:, par, qt, h, ch:ch + 1], mx[s][:, :], AX.X, ALU.max), mm,
                    c.m_part_users.get((par, h)))
                mx_ring.used(s, r)
                item[i]["mx"].append(r)

        def place_max(i, g):
            b, kb = divmod(i, NKB)
            par = i % 2
            hs = slice(4 * g, 4 * g + 4)
            s, users = ms_ring.take()
            m_blk = m_blk2[:, b % 2, :, :, :]
            a = dve.do(lambda e: e.tensor_reduce(m_blk[:, :, hs, kb:kb + 1], m_part[:, par, :, hs, :],
                                                 AX.X, ALU.max), item[i]["mx"], m_blk_users[b % 2])
            c.m_part_users.update({(par, h): [a] for h in range(4 * g, 4 * g + 4)})
            item[i].setdefault("blk", []).append(a)
            m8 = m_spl[:, s, :, :]
            neg = m8[:, :, 0].rearrange("p (q h) -> p q h", q=2)
            a = dve.do(lambda e: e.tensor_scalar(neg, m_blk[:, :, hs, kb], -1.0, None, ALU.mult), a, users)
            a = dve.do(lambda e: e.tensor_copy(mt_bf[:, s, :, 0], m8[:, :, 0]), a)
            a = dve.do(lambda e: e.tensor_tensor(m8[:, :, 1], m8[:, :, 0], mt_bf[:, s, :, 0],
                                                 ALU.subtract), a)
            a = dve.do(lambda e: e.tensor_copy(mt_bf[:, s, :, 1], m8[:, :, 1]), a)
            a = dve.do(lambda e: e.tensor_tensor(mt_bf[:, s, :, 2], m8[:, :, 1], mt_bf[:, s, :, 1],
                                                 ALU.subtract), a)
            item[i]["spl", g] = (s, a)

        def place_max_rows(i, g):
            b = i // NKB
            hs = slice(4 * g, 4 * g + 4)
            s, a = item[i]["spl", g]
            _, pusers = pj_ring.take()
            for j in range(8):
                tr = pe.do(lambda e, j=j: e.transpose(
                    pj_bf[96:99, j * P:(j + 1) * P], mt_bf[:, s, j, :], c.ident_bf[:, :]),
                    a, pusers, count=(j == 7))
            ms_ring.used(s, tr)
            a = act.do(lambda e: e.activation(
                q_base[96:99, hs, b * S:(b + 1) * S].rearrange("p h (q t) -> p q h t", q=2),
                pj_bf[96:99, :].rearrange("p (q h t) -> p q h t", q=2, h=4), ACT.Copy),
                tr, q_m_users[g])
            q_m_users[g] = []
            pj_ring.used(0, a)
            item[i][("m", g)] = a

        def scores(i, g, kt):
            b = i // NKB
            s, users = sc_ring.take()
            for j in range(4):
                h = 4 * g + j
                mt, hl = divmod(h, 8)
                u = item[i][("unit", mt)]
                mm = pe.do(lambda e, s=s, j=j, h=h, u=u, hl=hl: e.matmul(
                    sc[s][:, j, :], ks[0:ROWS, u, hl, kt * P:(kt + 1) * P],
                    q_base[0:ROWS, h, b * S:(b + 1) * S], start=True, stop=True),
                    users, item[i][("m", g)], item[i][("ready", mt)], init, count=(j == 3))
            ks_ring.used(u, mm)
            q_m_users[g].append(mm)
            x, xusers = ex_ring.take()
            a = act.do(lambda e: e.activation(ex[:, x, :, :], sc[s][:, :, :], ACT.Exp), mm, xusers)
            sc_ring.used(s, a)
            return (i, g, kt, x, a)

        def weigh(unit):
            i, g, kt, x, a = unit
            v = item[i]["vs"]
            if kt == 0:
                _, c.pv_users = pv_ring.take()
            for j in range(4):
                mm = pe.do(lambda e, j=j: e.matmul(
                    pv[32 * j:32 * j + VW, :], vs[:, v, kt, 4 * g + j, :], ex[:, x, j, :],
                    start=(kt == 0), stop=(kt == KT - 1)),
                    a, item[i]["v_ready"], c.pv_users, init, count=(j == 3))
            ex_ring.used(x, mm)
            vs_ring.used(v, mm)
            if kt < KT - 1:
                return
            o, ousers = o_ring.take()
            ev = dve.do(lambda e: e.tensor_copy(o_sb[:, o, :], pv[:, :]), mm, ousers)
            pv_ring.used(0, ev)
            item[i][("o", g)] = (o, ev)

        def gather(i, g):
            kb = i % NKB
            o, ev = item[i][("o", g)]
            _, users = pj_ring.take()
            for q in range(2):
                tr = pe.do(lambda e, q=q: e.transpose(pj[:, q * P:(q + 1) * P],
                                                      o_sb[:, o, q * P:(q + 1) * P], c.ident[:, :]),
                           ev, users, count=(q == 1))
            o_ring.used(o, tr)
            a = dve.do(lambda e: e.tensor_copy(
                o_all[:, kb, :, 4 * g:4 * g + 4, :],
                pj[:, 0:S].rearrange("p (q h v) -> p q h v", q=2, h=4)[:, :, :, 0:VW]), tr, blk_users)
            pj_ring.used(0, a)
            item[i].setdefault("o", []).append(a)

        def combine(b):
            m_blk = m_blk2[:, b % 2, :, :, :]
            marks = [item[i][k] for i in range(b * NKB, (b + 1) * NKB) for k in ("o", "blk")]
            a = dve.do(lambda e: e.tensor_reduce(m_all[:, :, :].rearrange("p q (h o) -> p q h o", o=1),
                                                 m_blk[:, :, :, :], AX.X, ALU.max), marks)
            for kb in range(NKB):
                a2 = dve.do(lambda e, kb=kb: e.tensor_tensor(w_blk[:, :, :, kb], m_blk[:, :, :, kb],
                                                             m_all[:, :, :], ALU.subtract), a)
            a = act.do(lambda e: e.activation(w_blk[:, :, :, :], w_blk[:, :, :, :], ACT.Exp), a2)
            for kb in range(NKB):
                ob = o_all[:, kb, :, :, :].rearrange("p q h v -> p (q h) v")
                wb = (w_blk[:, :, :, kb:kb + 1].rearrange("p q h o -> p (q h) o")
                      .to_broadcast([P, 2 * H, VW]))
                a3 = dve.do(lambda e, ob=ob, wb=wb: e.tensor_tensor(ob, ob, wb, ALU.mult), a)
                ac = acc[:, :, :, :].rearrange("p q h v -> p (q h) v")
                if kb == 0:
                    a4 = dve.do(lambda e, ob=ob, ac=ac: e.tensor_copy(ac, ob), a3)
                else:
                    a4 = dve.do(lambda e, ob=ob, ac=ac: e.tensor_tensor(ac, ac, ob, ALU.add), a3, a4)
            blk_users[:] = [a4]
            m_blk_users[b % 2] = [a2]
            a = dve.do(lambda e: e.reciprocal(m_all[:, :, :], acc[:, :, :, DH]), a4)
            rb = m_all[:, :, :].rearrange("p q (h o) -> p (q h) o", o=1).to_broadcast([P, 2 * H, DH])
            av = acc[:, :, :, 0:DH].rearrange("p q h v -> p (q h) v")
            ov = att[:, 2 * b:2 * b + 2, :].rearrange("p q (h v) -> p (q h) v", v=DH)
            a = dve.do(lambda e: e.tensor_tensor(ov, av, rb, ALU.mult), a)
            att_ready.extend([a, a])

        c.kr_users, c.m_part_users, c.pv_users = [], {}, []
        for w in range(-2, ITEMS):
            fill, top, run = w + 2, w + 1, w
            if fill < ITEMS:
                if fill == 0:
                    load_ctx(0)
                if fill + 1 < ITEMS:
                    load_next = fill + 1
                else:
                    load_next = None
            pending = None
            for s in range(SLOTS):
                g, kt = divmod(s, KT)
                unit = None
                if run >= 0:
                    unit = scores(run, g, kt)
                if 0 <= top < ITEMS:
                    block_max(top, s // 2, s % 2)
                if fill < ITEMS:
                    if s in (0, 2):
                        project_keys(fill, 0, s // 2)
                    elif s == 4:
                        stack_keys(fill, 0)
                    elif s in (16, 18):
                        project_keys(fill, 1, (s - 16) // 2)
                    elif s == 20:
                        stack_keys(fill, 1)
                    elif s % 2 == 0 and s // 2 in (3, 4, 5, 6, 7, 11, 12, 13):
                        project_values(fill, (3, 4, 5, 6, 7, 11, 12, 13).index(s // 2))
                    if s == 1 and load_next is not None:
                        load_ctx(load_next)
                if run >= 0 and pending is not None:
                    weigh(pending)
                pending = unit
                if kt == 2 and run >= 0 and g > 0:
                    gather(run, g - 1)
                if kt == 3 and 0 <= top < ITEMS and g > 0:
                    place_max_rows(top, g - 1)
                if kt == KT - 1 and 0 <= top < ITEMS:
                    place_max(top, g)
            if run >= 0:
                weigh(pending)
                gather(run, QUADS - 1)
            if 0 <= top < ITEMS:
                place_max_rows(top, QUADS - 1)
            if run >= 0:
                if run % NKB == NKB - 1:
                    combine(run // NKB)
    c.stage(f"{name}_out")
    with ExitStack() as short:
        def sb(n, shape, dt=F32):
            return short.enter_context(nc.sbuf_tensor(f"{name}_{n}", shape, dt))
        wo_sb, bo_sb, bv_sb = sb("wo", [P, KC, D]), sb("bo", [P, D]), sb("bv", [P, D])
        at = sb("at", [P, KC, N])
        out_banks = [short.enter_context(nc.psum_tensor(f"{name}_ob{i}", [P, 512], F32)) for i in range(8)]
        ring = Ring(8)
        slot = c.slot(f"{name}_wo")
        m = sp.dma(slot, wo_sb[:, :, :], wo.rearrange("(k p) n -> p k n", p=P))
        m = sp.dma(slot, bo_sb[:, :], bo)
        if bv is not None:
            m = sp.dma(slot, bv_sb[:, :], bv)
            ready = [dve.do(lambda e, t=t: e.tensor_tensor(att[:, t, :], att[:, t, :], bv_sb[:, :],
                                                           ALU.add), m) for t in range(NT)]
        else:
            ready = [None] * NT
        at_ready = to_features(c, att, at, ready, out_banks, ring)
        c.x_ready = project_residual(c, at, wo_sb, KC, bo_sb, out_banks, ring, at_ready, m)
    outer.close()


def project_residual(c, src, w_sb, chunks, bias_sb, banks, ring, ready, w_mark):
    for t in range(NT):
        b, users = ring.take()
        mm = matmuls(c, banks[b][:, 0:D],
                     [(src[:, k, t * P:(t + 1) * P], w_sb[:, k, :]) for k in range(chunks)],
                     ready[t // 4], w_mark, users)
        a = c.dve.do(lambda e, t=t, b=b: e.tensor_tensor(c.x[:, t, :], c.x[:, t, :],
                                                         banks[b][:, 0:D], ALU.add), mm)
        ring.used(b, a)
        last = c.dve.do(lambda e, t=t: e.tensor_tensor(c.x[:, t, :], c.x[:, t, :],
                                                       bias_sb[:, :], ALU.add), a)
    return last


def self_attention(c, name, sb, ps_s, ps_t, ps_o, rings, q_of, k_of, v_of, mask, scale, heads_per_out,
                   emit, ready, v_ready, extra, batches=range(B), scale_of=None):
    pe, act, dve, pool, sp = c.lanes
    s_ring, t_ring, o_ring, p_ring, pt_ring, st_ring = rings
    p_sb, pt_sb, stat = sb
    KEYS = (P, 2 * P)
    OFF = (0, P)
    step = P // heads_per_out

    def front(b, h):
        p, pusers = p_ring.take()
        st, stusers = st_ring.take()
        t3 = stat[:, st, :, :]
        s, susers = s_ring.take()
        for q in range(2):
            ql, qt = q_of(b, h, q)
            kr = k_of(b, h, KEYS[q])
            mm = pe.do(lambda e, q=q, ql=ql, kr=kr: e.matmul(
                ps_s[s][:, OFF[q]:OFF[q] + KEYS[q]], ql, kr, start=True, stop=True),
                ready, susers, count=(q == 1))
        sv = p_sb[:, p, :]
        a = dve.do(lambda e: e.tensor_tensor(sv, ps_s[s][:, 0:3 * P], mask[:, :], ALU.add), mm,
                   pusers, extra)
        s_ring.used(s, a)
        for q in range(2):
            m = dve.do(lambda e, q=q: e.tensor_reduce(
                t3[:, 0, q:q + 1], sv[:, OFF[q]:OFF[q] + KEYS[q]], AX.X, ALU.max), a, stusers)
        if scale_of is not None:
            m = dve.do(lambda e: e.scalar_tensor_tensor(
                t3[:, 1, :], t3[:, 0, :], -1.0, scale_of(h, slice(0, 2)), ALU.mult, ALU.mult), m)
        else:
            m = dve.do(lambda e: e.tensor_scalar(t3[:, 1, :], t3[:, 0, :], -scale, None, ALU.mult), m)
        for q in range(2):
            x = act.do(lambda e, q=q: e.activation(
                sv[:, OFF[q]:OFF[q] + KEYS[q]], sv[:, OFF[q]:OFF[q] + KEYS[q]], ACT.Exp,
                bias=t3[:, 1, q:q + 1],
                scale=scale if scale_of is None else scale_of(h, slice(q, q + 1)), accum_out=t3[:, 2, q:q + 1]), m)
        return p, st, x

    def divide(p, st, x):
        sv, t3 = p_sb[:, p, :], stat[:, st, :, :]
        m = dve.do(lambda e: e.reciprocal(t3[:, 3, :], t3[:, 2, :]), x)
        n = [lane.do(lambda e, q=q: e.tensor_scalar(
            sv[:, OFF[q]:OFF[q] + KEYS[q]], sv[:, OFF[q]:OFF[q] + KEYS[q]],
            t3[:, 3, q:q + 1], None, ALU.mult), m) for q, lane in ((0, dve), (1, pool))]
        st_ring.used(st, n)
        return p, n

    def back(b, h, p, n):
        t, tusers = t_ring.take()
        for j in range(3):
            tr = pe.do(lambda e, j=j: e.transpose(
                ps_t[t][:, j * P:(j + 1) * P], p_sb[:, p, j * P:(j + 1) * P], c.ident[:, :]),
                n, tusers, count=(j == 2))
        p_ring.used(p, tr)
        pt, ptusers = pt_ring.take()
        if h % 2:
            ev = act.do(lambda e: e.activation(pt_sb[:, pt, :], ps_t[t][:, 0:3 * P], ACT.Copy),
                        tr, ptusers)
        else:
            ev = dve.do(lambda e: e.tensor_copy(pt_sb[:, pt, :], ps_t[t][:, 0:3 * P]), tr, ptusers)
        t_ring.used(t, ev)
        return pt, ev

    def apply(b, heads):
        g = heads[0][0] // heads_per_out
        o, users = o_ring.take()
        for first, cols, keys, n in ((True, slice(0, 2 * P), slice(0, 2 * P), 0),
                                     (False, slice(P, 2 * P), slice(2 * P, 3 * P), 1)):
            for j, (h, pt, ev) in enumerate(heads):
                rows = slice(step * j, step * j + step)
                mm = pe.do(lambda e, rows=rows, pt=pt, h=h, first=first, cols=cols, keys=keys, n=n:
                           e.matmul(ps_o[o][rows, cols], v_of(b, n, h), pt_sb[:, pt, keys],
                                    start=first, stop=not first),
                           ev, v_ready, users, count=(not first and j == heads_per_out - 1))
        for h, pt, ev in heads:
            pt_ring.used(pt, mm)
        o_ring.used(o, emit(b, g, ps_o[o], mm))

    todo = [(b, h) for b in batches for h in range(H)]
    fronts, full = {}, []
    LAG1 = 3
    for i in range(len(todo) + LAG1 + 1):
        if i < len(todo):
            fronts[i] = front(*todo[i])
        if 0 <= i - 1 < len(todo):
            fronts[i - 1] = divide(*fronts[i - 1])
        if 0 <= i - LAG1 < len(todo):
            if len(full) == heads_per_out + 1:
                apply(full[0][0], [x[1:] for x in full[:-1]])
                full = full[-1:]
            b, h = todo[i - LAG1]
            full.append((b, h, *back(b, h, *fronts[i - LAG1])))
        if i == len(todo) + LAG1:
            apply(full[0][0], [x[1:] for x in full])
        yield


def run(*jobs):
    jobs = list(jobs)
    while jobs:
        jobs = [j for j in jobs if next(j, "end") != "end"]


def run_even(*jobs):
    ticks = max(steps for _, steps, _ in jobs)
    taken = [0] * len(jobs)
    for tick in range(ticks):
        for n, (job, steps, late) in enumerate(jobs):
            start = late * ticks
            due = steps * (tick + 1 - start) / (ticks - start)
            while taken[n] < due:
                next(job, None)
                taken[n] += 1
    run(*[job for job, _, _ in jobs])


def attention_buffers(c, name, ctx, n_pt):
    nc = c.nc
    sb = (ctx.enter_context(nc.sbuf_tensor(f"{name}_p", [P, 5, 3 * P], F32)),
          ctx.enter_context(nc.sbuf_tensor(f"{name}_pt", [P, n_pt, 3 * P], F32)),
          ctx.enter_context(nc.sbuf_tensor(f"{name}_stat", [P, 5, 4, 2], F32)))
    return sb


def conv_attention(c, name, g):
    nc = c.nc
    c.stage(name)
    pe, act, dve, pool, sp = c.lanes
    G = 4
    HW = P // G
    DH = D // H
    with ExitStack() as ctx:
        def sb(n, shape, dt=F32):
            return ctx.enter_context(nc.sbuf_tensor(f"{name}_{n}", shape, dt))
        wq, wk = sb("wq", [P, KC, G * P]), sb("wk", [P, KC, G * P])
        wv = sb("wv", [P, KC, G * P])
        wo = sb("wo", [P, G, D])
        cw = sb("cw", [P, 3, G, G * P])
        cols = sb("cols", [P, 3, G])
        bv, bo = sb("bv", [P, G * P]), sb("bo", [P, D])
        mask = sb("mask", [P, 3 * P])
        xn, xt = sb("xn", [P, NT, D]), sb("xt", [P, KC, N])
        q, k = sb("q", [P, G, G, N]), sb("k", [P, G, N])
        v = sb("v", [P, NT, G * P])
        cc = sb("cc", [P, G, B, S + 2])
        st = (sb("st", [P, NT, 6]), sb("mv", [P, NT, 2]), sb("rs", [P, 3, NT]))
        asb = attention_buffers(c, name, ctx, 6)
        banks = [ctx.enter_context(nc.psum_tensor(f"{name}_bank{i}", [P, 512], F32)) for i in range(8)]
        slot = c.slot(f"{name}_w")
        for dst, src in ((wq, "ca_wq"), (wk, "ca_wk"), (wv, "ca_wv"), (wo, "ca_wo")):
            w = sp.dma(slot, dst[:, :, :], g(src).rearrange("(k p) n -> p k n", p=P))
        for dst, src in ((cols, "ca_cols"),):
            w = sp.dma(slot, dst[:, :, :], g(src).rearrange("p (a b) -> p a b", a=3))
        for dst, src in ((bv, "ca_bv"), (bo, "ca_bo"), (mask, "causal")):
            w = sp.dma(slot, dst[:, :], g(src))
        slot2 = c.slot(f"{name}_cw")
        cw_mark = sp.dma(slot2, cw[:, :, :, :], g("ca_cw").rearrange("t (k p) n -> p t k n", p=P))
        zero = [pool.do(lambda e, b=b: e.memset(cc[:, :, :, b:b + 1], 0.0)) for b in (0, S + 1)]
        q_zero = [pool.do(lambda e: e.memset(q[:, 0:2, :, :], 0.0)),
                  act.do(lambda e: e.activation(q[:, 2:4, :, :], q[:, 0:2, :, :], ACT.Copy), pool.last())]

        def spread(gr, b, cols_, bank_cols, bias, mm):
            marks = []
            for j in range(G):
                rows = slice(HW * j, HW * j + HW)
                o, src, bi = q[rows, j, gr, cols_], banks[b][rows, bank_cols], bias[rows, :]
                if j < 2:
                    marks.append(act.do(lambda e, o=o, src=src, bi=bi: e.activation(
                        o, src, ACT.Identity, bias=bi), mm, q_zero))
                else:
                    marks.append(dve.do(lambda e, o=o, src=src, bi=bi: e.tensor_scalar(
                        o, src, bi, None, ALU.add), mm, q_zero))
            return marks
        ring = Ring(8)
        normed = layernorm(c, c.x, xn, st, c.x_ready)
        xr = to_features(c, xn, xt, normed, banks, ring)

        def project(dst, w_sb, bias_col, src_of, chunks, marks, n_of=2):
            out = []
            for gr in range(G):
                for half in range(2):
                    b, users = ring.take()
                    mm = matmuls(c, banks[b][:, :], [
                        (w_sb(i, gr), src_of(i, half)) for i in range(chunks)], marks, users)
                    bias = cols[:, bias_col, gr:gr + 1]
                    if dst is q:
                        a = spread(gr, b, slice(half * 512, (half + 1) * 512), slice(0, 512), bias, mm)
                        ring.used(b, a)
                        out += a
                        continue
                    o = dst[:, gr, half * 512:(half + 1) * 512]
                    if half:
                        a = act.do(lambda e, o=o, b=b, bias=bias: e.activation(
                            o, banks[b][:, :], ACT.Identity, bias=bias), mm)
                    else:
                        a = dve.do(lambda e, o=o, b=b, bias=bias: e.tensor_scalar(
                            o, banks[b][:, :], bias, None, ALU.add), mm)
                    ring.used(b, a)
                    out.append(a)
            return out

        def xsrc(i, half):
            return xt[:, i, half * 512:(half + 1) * 512]
        qk = project(q, lambda i, gr: wq[:, i, gr * P:(gr + 1) * P], 0, xsrc, KC, [xr, w])
        qk += project(k, lambda i, gr: wk[:, i, gr * P:(gr + 1) * P], 1, xsrc, KC, [xr, w])
        v_ready = []
        for t in range(NT):
            b, users = ring.take()
            mm = matmuls(c, banks[b][:, :], [(xt[:, i, t * P:(t + 1) * P], wv[:, i, :])
                                             for i in range(KC)], users)
            a = dve.do(lambda e, t=t, b=b: e.tensor_tensor(v[:, t, :], banks[b][:, :], bv[:, :],
                                                           ALU.add), mm)
            ring.used(b, a)
            v_ready.append(a)

        free = [Ring(2), Ring(2), Ring(2), Ring(5), Ring(6), Ring(5)]
        for r, b0 in ((free[0], 0), (free[1], 2), (free[2], 4)):
            for i in range(2):
                r.used(i, ring.users[b0 + i])
        ring.users[0:6] = [[] for _ in range(6)]

        def q_of(b, h, qt):
            gr, j = divmod(h, G)
            return q[:, j, gr, b * S + qt * P:b * S + (qt + 1) * P], None

        def k_of(b, h, n):
            gr, j = divmod(h, G)
            return k[:, gr, b * S:b * S + n]

        def v_of(b, kt, h):
            return v[:, 2 * b + kt, HW * h:HW * (h + 1)]
        conv_in = []

        def keep(b, gr, bank, mm):
            a = act.do(lambda e: e.activation(cc[:, gr, b, 1:S + 1], bank[:, 0:S], ACT.Copy), mm)
            conv_in.append(a)
            return a
        run(self_attention(c, name, asb, banks[0:2], banks[2:4], banks[4:6], free, q_of, k_of, v_of,
                       mask, 1.0 / float(np.sqrt(DH)), G, keep, qk, v_ready, w))
        q2 = []
        for gr in range(G):
            for half in range(2):
                for bb in range(2):
                    b = 2 * half + bb
                    i = 6 + (bb % 2)
                    users, ring.users[i] = ring.users[i], []
                    pairs = [(cw[:, t, kk, gr * P:(gr + 1) * P], cc[:, kk, b, t:t + S])
                             for t in range(3) for kk in range(G)]
                    mm = matmuls(c, banks[i][:, 0:S], pairs, conv_in, zero, cw_mark, users)
                    a = spread(gr, i, slice(b * S, (b + 1) * S), slice(0, S), cols[:, 2, gr:gr + 1], mm)
                    ring.users[i] = a
                    q2 += a
        ctx2 = []

        def keep2(b, gr, bank, mm):
            a = act.do(lambda e: e.activation(cc[:, gr, b, 1:S + 1], bank[:, 0:S], ACT.Copy), mm, q2)
            ctx2.append(a)
            return a
        run(self_attention(c, name, asb, banks[0:2], banks[2:4], banks[4:6], free, q_of, k_of, v_of,
                       mask, 1.0 / float(np.sqrt(DH)), G, keep2, [q2, qk], v_ready, w))
        for t in range(NT):
            b, qt = divmod(t, 2)
            i = 6 + t % 2
            users, ring.users[i] = ring.users[i], []
            mm = matmuls(c, banks[i][:, 0:D],
                         [(cc[:, kk, b, 1 + qt * P:1 + (qt + 1) * P], wo[:, kk, :]) for kk in range(G)],
                         ctx2, users)
            a = dve.do(lambda e, t=t, i=i: e.tensor_tensor(c.x[:, t, :], c.x[:, t, :],
                                                           banks[i][:, 0:D], ALU.add), mm)
            ring.users[i] = [a]
            last = dve.do(lambda e, t=t: e.tensor_tensor(c.x[:, t, :], c.x[:, t, :], bo[:, :],
                                                         ALU.add), a)
        c.x_ready = last


DEPTH = 6
LH = 64
INNER = H * LH
FF = int(D * 4 * 2 / 3)
FC = -(-FF // P)
FFP = FC * P


def local_transformer(c, name, g):
    nc = c.nc
    c.stage(name)
    pe, act, dve, pool, sp = c.lanes
    HP = H // 2
    with ExitStack() as ctx:
        def sb(n, shape, dt=F32):
            return ctx.enter_context(nc.sbuf_tensor(f"{name}_{n}", shape, dt))
        park = c.slot(f"{name}_park")
        y = c.x
        parked = sp.dma(park, c.parked, c.x[:, :, :], c.x_ready)
        wqk = sb("wqk", [P, 2, KC, 2 * INNER])
        wval = sb("wval", [P, KC, INNER])
        wo, w1, w2 = sb("wo", [P, HP, D]), sb("w1", [P, KC, 2 * FFP]), sb("w2", [P, FC, D])
        scl = sb("scl", [P, 2, 4, LH])
        rot = sb("rot", [P, 4, 2, LH])
        tab = sb("tab", [P, 2, 4, 2, LH])
        b2, ffc, lnc = sb("b2", [P, 2, D]), sb("ffc", [P, DEPTH, 2, FC]), sb("lnc", [P, DEPTH, 2, KC])
        mask = sb("mask", [P, 3 * P])
        xs, xt = sb("xs", [P, 2, 2, P]), sb("xt", [P, 2, KC, S])
        r_qk = sb("r_qk", [P, 2, INNER])
        t_sq = sb("t_sq", [P, 2, 512])
        t_rot = sb("t_rot", [P, 2, 512])
        nrm = sb("nrm", [P, 2, 3, H])
        rq = sb("rq", [P, 2, 2, H])
        q_even, q_odd = sb("q_even", [P, 2, HP, S]), sb("q_odd", [P, 2, HP, S])
        kt = sb("kt", [P, 2, HP, S])
        v = sb("v", [P, 2, 2, INNER])
        ot = sb("ot", [P, HP, S])
        fs, ft = sb("fs", [P, 2, D]), sb("ft", [P, KC, S])
        fst, fmv, frs = sb("fst", [P, 2, 6]), sb("fmv", [P, 2, 2]), sb("frs", [P, 2, 2])
        gl, u = sb("gl", [P, 2, S]), sb("u", [P, FC, S])
        st = (sb("st", [P, NT, 6]), sb("mv", [P, NT, 2]), sb("rs", [P, 3, NT]))
        asb = attention_buffers(c, name, ctx, 4)
        banks = [ctx.enter_context(nc.psum_tensor(f"{name}_bank{i}", [P, 512], F32)) for i in range(8)]
        arings = [Ring(2), Ring(2), Ring(1), Ring(5), Ring(4), Ring(5)]
        gen = Ring(3)
        r_ring, t_ring, n_ring = Ring(2), Ring(2), Ring(2)
        gl_ring = Ring(2)

        slot = c.slot(f"{name}_small")
        small = sp.dma(slot, rot[:, :, :, :], g("lt_rot").rearrange("p (a b c) -> p a b c", a=4, b=2))
        small = sp.dma(slot, ffc[:, :, :, :], g("lt_ffc").rearrange("p (a b c) -> p a b c", a=DEPTH, b=2))
        small = sp.dma(slot, lnc[:, :, :, :], g("lt_lnc").rearrange("p (a b c) -> p a b c", a=DEPTH, b=2))
        small = sp.dma(slot, mask[:, :], g("band"))
        zeros = [dve.do(lambda e: e.memset(q_even[64:128, :, :, :], 0.0)),
                 dve.do(lambda e: e.memset(q_odd[0:64, :, :, :], 0.0)),
                 dve.do(lambda e: e.memset(xs[0:1, :, 0, :], 0.0))]
        normed = layernorm(c, c.x, y, st, [c.x_ready, parked])
        y_ready = {b: [normed[2 * b], normed[2 * b + 1]] for b in range(B)}

        wq_slot = [c.slot(f"{name}_wqkv{i}") for i in range(2)]
        wb_slot = [c.slot(f"{name}_w{n}") for n in ("o", "1", "2")]
        xs_slot = [c.slot(f"{name}_xs{i}") for i in range(2)]
        fs_slot = c.slot(f"{name}_fs")
        wv_slot = c.slot(f"{name}_wval")
        wval_ready, wval_users = {}, {l: [] for l in range(-1, DEPTH)}
        wqkv_ready, wqkv_users = {}, {l: [] for l in range(-2, DEPTH)}
        wb_ready, wb_users = {}, {l: [[], [], []] for l in range(-1, DEPTH)}
        tab_ready, tab_users = {}, {l: [] for l in range(-2, DEPTH)}
        b2_users = {l: [] for l in range(-2, DEPTH)}
        par_users = {}
        ot_users, fs_users, ft_users, u_users = [[]], [[]], [[]], [[]]

        def load_values(l):
            w = g("lt_wqkv")[l].rearrange("(k p) n -> p k n", p=P)
            wval_ready[l] = sp.dma(wv_slot, wval[:, :, :], w[:, :, 2 * INNER:], wval_users[l - 1])

        def load_front(l):
            i = l % 2
            w = g("lt_wqkv")[l].rearrange("(k p) n -> p k n", p=P)
            sp.dma(wq_slot[i], scl[:, i, :, :], g("lt_scl")[l].rearrange("p (a b) -> p a b", a=4),
                   tab_users[l - 2])
            sp.dma(wq_slot[i], b2[:, i, :], g("lt_b2")[l], b2_users[l - 2])
            wqkv_ready[l] = sp.dma(wq_slot[i], wqk[:, i, :, :], w[:, :, 0:2 * INNER], wqkv_users[l - 2])

        def tables(l):
            i = l % 2
            for tile in range(2):
                a = dve.do(lambda e, tile=tile: e.tensor_tensor(
                    tab[:, i, :, tile, :], rot[:, :, tile, :], scl[:, i, :, :], ALU.mult),
                    wqkv_ready[l], small, tab_users[l - 2])
            tab_ready[l] = a

        def load_back(l, n):
            dst = (wo, w1, w2)[n]
            src = (g("lt_wo"), g("lt_w1"), g("lt_w2"))[n]
            wb_ready[l, n] = sp.dma(wb_slot[n], dst[:, :, :], src[l].rearrange("(k p) n -> p k n", p=P),
                                    wb_users[l - 1][n])

        def shift(dst, slot_, b, cols, *waits):
            sp.dma(slot_, dst[1:P, :, cols], y[0:P - 1, 2 * b:2 * b + 2, P:D], waits)
            return sp.dma(slot_, dst[0:1, 1, cols], y[P - 1:P, 2 * b, P:D])

        def shift_ahead(l, b):
            par = (l * B + b) % 2
            xs_ready[l, b] = shift(xs[:, par, :, :], xs_slot[par], b, slice(0, P), y_ready[b],
                                   zeros, xs_users[par])

        def features(l, b):
            par = (l * B + b) % 2
            i, users = gen.take()
            for k in range(KC):
                for q in range(2):
                    src = y[:, 2 * b + q, 0:P] if k == 0 else xs[:, par, q, :]
                    tr = pe.do(lambda e, k=k, q=q, src=src: e.transpose(
                        banks[5 + i][:, (2 * k + q) * P:(2 * k + q + 1) * P], src, c.ident[:, :]),
                        xs_ready[l, b], y_ready[b], users, count=(k + q == 2))
            a = act.do(lambda e: e.activation(
                xt[:, par, :, :], banks[5 + i][:, :].rearrange("p (k s) -> p k s", k=KC), ACT.Copy), tr)
            gen.used(i, a)
            xs_users[par] = tr
            xt_ready[l, b] = a
            if l == 0 and b + 2 < B:
                shift_ahead(0, b + 2)

        def front(l, b):
            par, lp = (l * B + b) % 2, l % 2
            prev = par_users.get((l * B + b) - 2, [])
            if b == 2 and l + 1 < DEPTH:
                load_front(l + 1)
            if b == 3 and l + 1 < DEPTH:
                tables(l + 1)
            x_mark = xt_ready[l, b]
            done_k, done_q, done_v = [], [], []
            yield

            def project(tile, sec):
                r, rusers = r_ring.take()
                n, nusers = n_ring.take()
                parts = []
                for half in range(2):
                    i, users = gen.take()
                    col = sec * INNER + half * 512
                    mm = matmuls(c, banks[5 + i][:, :], [
                        (xt[:, par, k, tile * P:(tile + 1) * P], wqk[:, lp, k, col:col + 512])
                        for k in range(KC)], x_mark, wqkv_ready[l], users)
                    wqkv_users[l].append(mm)
                    t, tusers = t_ring.take()
                    p3 = banks[5 + i][:, :].rearrange("p (h d) -> p h d", d=LH)
                    sq3 = t_sq[:, t, :].rearrange("p (h d) -> p h d", d=LH)
                    ro3 = t_rot[:, t, :].rearrange("p (h d) -> p h d", d=LH)
                    out3 = r_qk[:, r, half * 512:(half + 1) * 512].rearrange("p (h d) -> p h d", d=LH)

                    def table(j, lo, hi):
                        return (tab[:, lp, 2 * sec + j, tile:tile + 1, lo:hi]
                                .to_broadcast([P, 8, hi - lo]))
                    c1 = dve.do(lambda e, out3=out3, p3=p3, tb=table(0, 0, LH): e.tensor_tensor(
                        out3, p3, tb, ALU.mult), mm, rusers, tab_ready[l])
                    dve.do(lambda e, ro3=ro3, p3=p3, tb=table(1, 0, 32): e.tensor_tensor(
                        ro3[:, :, 0:32], p3[:, :, 32:64], tb, ALU.mult), tusers)
                    c2 = dve.do(lambda e, ro3=ro3, p3=p3, tb=table(1, 32, 64): e.tensor_tensor(
                        ro3[:, :, 32:64], p3[:, :, 0:32], tb, ALU.mult))
                    a = act.do(lambda e, sq3=sq3, p3=p3: e.activation(sq3, p3, ACT.Square), c2, tusers)
                    gen.used(i, a)
                    c3 = dve.do(lambda e, out3=out3, ro3=ro3: e.tensor_tensor(
                        out3, out3, ro3, ALU.add), c1, c2)
                    parts.append(c3)
                    yield
                    s_ = dve.do(lambda e, half=half, sq3=sq3: e.tensor_reduce(
                        nrm[:, n, 0, half * 8:half * 8 + 8], sq3, AX.X, ALU.add), a, nusers)
                    parts.append(s_)
                    t_ring.used(t, s_, c3)
                f = dve.do(lambda e: e.tensor_scalar(nrm[:, n, 1, :], nrm[:, n, 0, :], 1e-24,
                                                     None, ALU.max), parts)
                f = rsqrt(c, nrm[:, n, 2, :], nrm[:, n, 1, :], H, f)
                if sec == 0:
                    f = pool.do(lambda e: e.tensor_scalar(
                        rq[:, par, tile, :], nrm[:, n, 2, :], 8.0, None, ALU.mult), f, prev)
                    done_q.append(f)
                    n_ring.used(n, f)
                projected[tile, sec] = r, n, f, parts

            def normalise(tile):
                r, n, f, parts = projected[tile, 1]
                full = r_qk[:, r, :].rearrange("p (h d) -> p h d", d=LH)
                nb = nrm[:, n, 2, :].rearrange("p (h o) -> p h o", o=1).to_broadcast([P, H, LH])
                f = dve.do(lambda e: e.tensor_tensor(full, full, nb, ALU.mult), f)
                n_ring.used(n, f)
                parts.append(f)

            def turn(tile, sec):
                r, _, _, parts = projected[tile, sec]
                for half in range(2):
                    i, users = gen.take()
                    for j in range(4):
                        hp = 4 * half + j
                        tr = pe.do(lambda e, i=i, j=j, hp=hp: e.transpose(
                            banks[5 + i][:, j * P:(j + 1) * P], r_qk[:, r, hp * P:(hp + 1) * P],
                            c.ident[:, :]), parts, users, count=(j == 3))
                    src = banks[5 + i][:, :].rearrange("p (j t) -> p j t", j=4)
                    hs, ts = slice(4 * half, 4 * half + 4), slice(tile * P, (tile + 1) * P)
                    if sec == 0:
                        a = act.do(lambda e, src=src, hs=hs, ts=ts: e.activation(
                            q_even[0:64, par, hs, ts], src[0:64, :, :], ACT.Copy), tr, prev)
                        a2 = dve.do(lambda e, src=src, hs=hs, ts=ts: e.tensor_copy(
                            q_odd[64:128, par, hs, ts], src[64:128, :, :]), tr, prev)
                        done_q.extend([a, a2])
                        gen.used(i, a, a2)
                    else:
                        a = act.do(lambda e, src=src, hs=hs, ts=ts: e.activation(
                            kt[:, par, hs, ts], src, ACT.Copy), tr, prev)
                        done_k.append(a)
                        gen.used(i, a)
                    r_ring.used(r, tr)
                    yield

            def values(tile):
                for half in range(2):
                    i, users = gen.take()
                    col = half * 512
                    mm = matmuls(c, banks[5 + i][:, :], [
                        (xt[:, par, k, tile * P:(tile + 1) * P], wval[:, k, col:col + 512])
                        for k in range(KC)], x_mark, wval_ready[l], users)
                    wval_users[l].append(mm)
                    a = act.do(lambda e, i=i, half=half: e.activation(
                        v[:, par, tile, half * 512:(half + 1) * 512], banks[5 + i][:, :], ACT.Copy),
                        mm, prev)
                    gen.used(i, a)
                    done_v.append(a)
                    yield
            projected = {}
            for tile in range(2):
                yield from project(tile, 0)
                yield from project(tile, 1)
                yield from turn(tile, 0)
                yield from values(tile)
                if (tile, b) == (1, B - 1) and l + 1 < DEPTH:
                    load_values(l + 1)
                normalise(tile)
                yield
                if tile == 1 and (l, b) != jobs[-1]:
                    features(*jobs[l * B + b + 1])
                yield from turn(tile, 1)
            parts = projected[1, 1][3]
            tab_users[l].append(done_k[-1])
            tab_users[l] += parts
            ready[l * B + b] = ([done_q, done_k], done_v)

        def back(l, b):
            par = (l * B + b) % 2
            qk_ready, v_ready = ready[l * B + b]
            emitted = []

            def keep(b_, gr, bank, mm):
                a = act.do(lambda e: e.activation(ot[:, gr, :], bank[:, 0:S], ACT.Copy), mm, ot_users[0])
                emitted.append(a)
                return a

            def q_of(b_, h, qt):
                q = q_odd if h % 2 else q_even
                return q[:, par, h // 2, qt * P:(qt + 1) * P], None
            yield from self_attention(
                c, name, asb, banks[0:2], banks[2:4], banks[4:5], arings, q_of,
                lambda b_, h, n: kt[:, par, h // 2, 0:n],
                lambda b_, t, h: v[:, par, t, h * LH:(h + 1) * LH],
                mask, 8.0, 2, keep, [qk_ready, zeros], v_ready, small, batches=[b],
                scale_of=lambda h, q: rq[:, par, q, h])
            par_users[l * B + b] = [emitted, pe.last(), dve.last(), act.last()]
            m = []
            for tile in range(2):
                t = 2 * b + tile
                i, users = gen.take()
                mm = matmuls(c, banks[5 + i][:, 0:D], [
                    (ot[:, k, tile * P:(tile + 1) * P], wo[:, k, :]) for k in range(HP)],
                    emitted, wb_ready[l, 0], users)
                a = dve.do(lambda e, t=t, i=i: e.tensor_tensor(y[:, t, :], y[:, t, :],
                                                               banks[5 + i][:, 0:D], ALU.add), mm)
                gen.used(i, a)
                m.append(a)
                yield
            ot_users[0] = [mm]
            wb_users[l][0] = [mm]
            if b == B - 1 and l + 1 < DEPTH:
                load_back(l + 1, 0)
            y_ready[b] = m

        def gated(l, b):
            sp.dma(fs_slot, fs[:, :, 0:P], y[:, 2 * b:2 * b + 2, 0:P], y_ready[b], fs_users[0])
            f = [shift(fs, fs_slot, b, slice(P, D)),
                 dve.do(lambda e: e.memset(fs[0:1, 0, P:D], 0.0), fs_users[0])]
            yield
            yield
            yield
            for q in range(2):
                a = dve.do(lambda e, q=q: e.bn_stats(fst[:, q, :], fs[:, q, :]), f)
                a = dve.do(lambda e, q=q: e.bn_aggr(fmv[:, q, :], fst[:, q, :]), a)
            a = dve.do(lambda e: e.tensor_scalar(frs[:, 0, :], fmv[:, :, 1], LN_EPS, None, ALU.add), a)
            a = rsqrt(c, frs[:, 1, :], frs[:, 0, :], 2, a)
            yield
            yield
            n = []
            for q in range(2):
                n.append(dve.do(lambda e, q=q: e.tensor_scalar(
                    fs[:, q, :], fs[:, q, :], fmv[:, q, 0:1], frs[:, 1, q:q + 1],
                    ALU.subtract, ALU.mult), a))
            yield
            i, users = gen.take()
            for k in range(KC):
                for q in range(2):
                    tr = pe.do(lambda e, k=k, q=q, i=i: e.transpose(
                        banks[5 + i][:, (2 * k + q) * P:(2 * k + q + 1) * P],
                        fs[:, q, k * P:(k + 1) * P], c.ident[:, :]), n, users, count=(k + q == 2))
            fs_users[0] = [tr]
            fx = []
            for k in range(KC):
                fx.append(dve.do(lambda e, k=k, i=i: e.tensor_scalar(
                    ft[:, k, :], banks[5 + i][:, k * S:(k + 1) * S], lnc[:, l, 0, k:k + 1],
                    lnc[:, l, 1, k:k + 1], ALU.mult, ALU.add), tr, small, ft_users[0]))
            gen.used(i, fx)
            yield
            ud = []
            for mc in range(0, FC, 2):
                got = []
                for m_ in (mc, mc + 1):
                    i, users = gen.take()
                    matmuls(c, banks[5 + i][:, S:2 * S], [
                        (w1[:, k, FFP + m_ * P:FFP + (m_ + 1) * P], ft[:, k, :]) for k in range(KC)],
                        fx, wb_ready[l, 1], users)
                    mm = matmuls(c, banks[5 + i][:, 0:S], [
                        (w1[:, k, m_ * P:(m_ + 1) * P], ft[:, k, :]) for k in range(KC)])
                    got.append((m_, i, mm))
                for n_, (m_, i, mm) in enumerate(got):
                    j, jusers = gl_ring.take()
                    a = act.do(lambda e, i=i, j=j, m_=m_: e.activation(
                        gl[:, j, :], banks[5 + i][:, S:2 * S], ACT.Gelu, bias=ffc[:, l, 1, m_:m_ + 1]),
                        got[-1][2], jusers)
                    got[n_] = m_, i, j, a
                for m_, i, j, a in got:
                    a = dve.do(lambda e, i=i, j=j, m_=m_: e.scalar_tensor_tensor(
                        u[:, m_, :], banks[5 + i][:, 0:S], ffc[:, l, 0, m_:m_ + 1], gl[:, j, :],
                        ALU.add, ALU.mult), a, u_users[0])
                    gen.used(i, a)
                    gl_ring.used(j, a)
                    ud.append(a)
                yield
            ft_users[0] = [mm]
            wb_users[l][1] = [mm]
            if b == B - 1 and l + 1 < DEPTH:
                load_back(l + 1, 1)
            fin = []
            for tile in range(2):
                t = 2 * b + tile
                i, users = gen.take()
                mm = matmuls(c, banks[5 + i][:, 0:D], [
                    (u[:, k, tile * P:(tile + 1) * P], w2[:, k, :]) for k in range(FC)],
                    ud, wb_ready[l, 2], users)
                a = dve.do(lambda e, t=t, i=i: e.tensor_tensor(y[:, t, :], y[:, t, :],
                                                               banks[5 + i][:, 0:D], ALU.add), mm)
                gen.used(i, a)
                a = dve.do(lambda e, t=t: e.tensor_tensor(y[:, t, :], y[:, t, :], b2[:, l % 2, :],
                                                          ALU.add), a)
                fin.append(a)
                yield
            b2_users[l] = fin
            u_users[0] = [mm]
            wb_users[l][2] = [mm]
            if b == B - 1 and l + 1 < DEPTH:
                load_back(l + 1, 2)
            y_ready[b] = fin
            if l + 1 < DEPTH:
                shift_ahead(l + 1, b)

        ready, xt_ready, xs_ready, xs_users = {}, {}, {}, [None, None]
        ot_all = ot[:, :, :]
        jobs = [(l, b) for l in range(DEPTH) for b in range(B)]
        load_front(0)
        load_values(0)
        tables(0)
        for n in range(3):
            load_back(0, n)
        for b in range(2):
            shift_ahead(0, b)
        features(0, 0)
        for n in range(len(jobs) + 2):
            run_even(*[(part(*jobs[n - lag]), steps, late) for lag, (part, steps, late) in
                       enumerate(((front, 24, 0), (back, 23, 0), (gated, 16, 0.1)))
                       if 0 <= n - lag < len(jobs)])
        back_in = sp.dma(park, ot_all, c.parked, par_users[len(jobs) - 1], parked, ot_users[0])
        for t in range(NT):
            last = dve.do(lambda e, t=t: e.tensor_tensor(y[:, t, :], y[:, t, :], ot_all[:, t, :],
                                                         ALU.add), y_ready[t // 2], back_in)
        c.x_ready = last


DK = D // 2 // H
DV = D // H
TAPS = 4


def gated_linear_attention(c, name, g):
    nc = c.nc
    c.stage(name)
    pe, act, dve, pool, sp = c.lanes
    with ExitStack() as ctx:
        def sb(n, shape, dt=F32):
            return ctx.enter_context(nc.sbuf_tensor(f"{name}_{n}", shape, dt))
        taps = sb("taps", [P, KC, TAPS])
        w_in, w_out = sb("w_in", [P, KC, 3 * D]), sb("w_out", [P, KC, D])
        bg, aug = sb("bg", [P, D]), sb("aug", [P, P])
        xn, xt = sb("xn", [P, NT, D]), sb("xt", [P, KC, N])
        yc = sb("yc", [P, KC, N])
        q, kg, eg, kk = (sb(n, [P, NT, P]) for n in ("q", "kg", "eg", "kk"))
        v, gt = sb("v", [P, NT, D]), sb("gt", [P, NT, D])
        t1, t2 = sb("t1", [P, NT, P]), sb("t2", [P, NT, P])
        kd = sb("kd", [P, NT, P])
        cf = sb("cf", [P, NT, H])
        tv = sb("tv", [P, NT, D])
        o = sb("o", [P, NT, D])
        mu, var = sb("mu", [P, NT * H]), sb("var", [P, NT * H])
        ot = sb("ot", [P, KC, N])
        st = (sb("st", [P, NT, 6]), sb("mv", [P, NT, 2]), sb("rs", [P, 3, NT]))
        banks = [ctx.enter_context(nc.psum_tensor(f"{name}_bank{i}", [P, 512], F32)) for i in range(8)]
        ring = Ring(8)
        slot = c.slot(f"{name}_w")
        sp.dma(slot, taps[:, :, :], g("gla_taps").rearrange("p (k t) -> p k t", k=KC))
        sp.dma(slot, w_in[:, :, :], g("gla_win").rearrange("(k p) n -> p k n", p=P))
        sp.dma(slot, w_out[:, :, :], g("gla_wout").rearrange("(k p) n -> p k n", p=P))
        sp.dma(slot, bg[:, :], g("gla_bg"))
        w = sp.dma(slot, aug[:, :], g("gla_aug"))
        normed = layernorm(c, c.x, xn, st, c.x_ready)
        xr = to_features(c, xn, xt, normed, banks, ring)

        yr = []
        for k in range(KC):
            a = dve.do(lambda e, k=k: e.tensor_scalar(yc[:, k, :], xt[:, k, :],
                                                      taps[:, k, TAPS - 1:TAPS], None, ALU.mult), xr, w)
            for back in range(1, TAPS):
                a = dve.do(lambda e, k=k, back=back: e.scalar_tensor_tensor(
                    yc[:, k, back * S:N], xt[:, k, 0:N - back * S], taps[:, k, TAPS - 1 - back:TAPS - back],
                    yc[:, k, back * S:N], ALU.mult, ALU.add), a)
            yr.append(act.do(lambda e, k=k: e.activation(xt[:, k, :], yc[:, k, :], ACT.Silu), a))

        qr, kr, vr, gr = [], [], [], []
        for t in range(NT):
            b, users = ring.take()
            mm = matmuls(c, banks[b][:, :], [(xt[:, k, t * P:(t + 1) * P], w_in[:, k, 0:512])
                                             for k in range(KC)], yr, users)
            a1 = dve.do(lambda e, t=t, b=b: e.tensor_copy(q[:, t, :], banks[b][:, 0:P]), mm)
            a2 = dve.do(lambda e, t=t, b=b: e.tensor_copy(kg[:, t, :], banks[b][:, P:2 * P]), mm)
            a3 = act.do(lambda e, t=t, b=b: e.activation(v[:, t, :], banks[b][:, 2 * P:], ACT.Copy), a2)
            ring.used(b, a1, a2, a3)
            b, users = ring.take()
            mm = matmuls(c, banks[b][:, 0:D], [(xt[:, k, t * P:(t + 1) * P], w_in[:, k, 512:768])
                                               for k in range(KC)], users)
            a4 = dve.do(lambda e, t=t, b=b: e.tensor_tensor(gt[:, t, :], banks[b][:, 0:D], bg[:, :],
                                                            ALU.add), mm)
            ring.used(b, a4)
            qr.append(a1), kr.append(a2), vr.append(a3), gr.append(a4)

        sg = act.do(lambda e: e.activation(gt[:, :, :], gt[:, :, :], ACT.Silu), gr)
        a = act.do(lambda e: e.activation(t1[:, :, :], kg[:, :, :], ACT.Abs), kr)
        a = act.do(lambda e: e.activation(t1[:, :, :], t1[:, :, :], ACT.Exp, scale=-1.0), a)
        a = dve.do(lambda e: e.tensor_scalar(t1[:, :, :], t1[:, :, :], 1.0, None, ALU.add), a)
        a = act.do(lambda e: e.activation(t2[:, :, :], t1[:, :, :], ACT.Ln), a)
        a = dve.do(lambda e: e.scalar_tensor_tensor(t1[:, :, :], kg[:, :, :], 0.0, t2[:, :, :],
                                                    ALU.min, ALU.subtract), a)
        er = act.do(lambda e: e.activation(eg[:, :, :], t1[:, :, :], ACT.Exp, scale=1.0 / 16.0), a)
        kr = dve.do(lambda e: e.tensor_scalar(kk[:, :, :], eg[:, :, :], -1.0, 1.0, ALU.mult, ALU.add), er)

        def steps(x, s, n):
            return x[:, 2 * s:2 * (s + n), :]

        def heads(x, width):
            return x.rearrange("p t (h d) -> p (t h) d", d=width)

        a = dve.do(lambda e: e.tensor_tensor(t2[:, :, :], q[:, :, :], kk[:, :, :], ALU.mult), qr, kr)
        augb = aug[:, :].rearrange("p (o n) -> p o n", o=1).to_broadcast([P, NT, P])
        a = dve.do(lambda e: e.tensor_tensor(t2[:, :, :], t2[:, :, :], augb, ALU.mult), a)
        a = dve.do(lambda e: e.tensor_reduce(cf[:, :, :].rearrange("p t (h o) -> p (t h) o", o=1),
                                             heads(t2[:, :, :], DK), AX.X, ALU.add), a)
        cb = cf[:, :, :].rearrange("p t (h o) -> p (t h) o", o=1).to_broadcast([P, NT * H, DV])
        a = dve.do(lambda e: e.tensor_tensor(heads(o[:, :, :], DV), heads(v[:, :, :], DV), cb, ALU.mult),
                   a, vr)
        oa = act.do(lambda e: e.activation(o[:, :, :], o[:, :, :], ACT.Sigmoid), a)
        qs = dve.do(lambda e: e.tensor_scalar(q[:, :, :], q[:, :, :], float(DK) ** -0.5, None, ALU.mult), a)
        for s in range(B):
            if s:
                dec = (steps(eg, s, 1).rearrange("p t d -> p (t d)").rearrange("p (o n) -> p o n", o=1)
                       .to_broadcast([P, s, 2 * P]))
                kds = steps(kd, 0, s).rearrange("p (s t) d -> p s (t d)", t=2)
                a = dve.do(lambda e, kds=kds, dec=dec: e.tensor_tensor(kds, kds, dec, ALU.mult), a)
            a = dve.do(lambda e, s=s: e.tensor_copy(steps(kd, s, 1), steps(kk, s, 1)), a)
            qb = (steps(q, s, 1).rearrange("p t d -> p (t d)").rearrange("p (o n) -> p o n", o=1)
                  .to_broadcast([P, s + 1, 2 * P]))
            a = dve.do(lambda e, s=s, qb=qb: e.tensor_tensor(
                steps(t1, 0, s + 1).rearrange("p (s t) d -> p s (t d)", t=2),
                steps(kd, 0, s + 1).rearrange("p (s t) d -> p s (t d)", t=2), qb, ALU.mult), a, qs)
            a = dve.do(lambda e, s=s: e.tensor_reduce(
                steps(cf, 0, s + 1).rearrange("p t (h o) -> p (t h) o", o=1),
                heads(steps(t1, 0, s + 1), DK), AX.X, ALU.add), a)
            cbs = (steps(cf, 0, s + 1).rearrange("p t (h o) -> p (t h) o", o=1)
                   .to_broadcast([P, 2 * (s + 1) * H, DV]))
            a = dve.do(lambda e, s=s, cbs=cbs: e.tensor_tensor(
                heads(steps(tv, 0, s + 1), DV), heads(steps(v, 0, s + 1), DV), cbs, ALU.mult), a)
            for j in range(s + 1):
                a = dve.do(lambda e, s=s, j=j: e.tensor_tensor(
                    steps(o, s, 1), steps(o, s, 1), steps(tv, j, 1), ALU.add), a, oa)
        oh = heads(o[:, :, :], DV)
        th = heads(tv[:, :, :], DV)

        def col(x):
            return x[:, :].rearrange("p (n o) -> p n o", o=1)
        a = dve.do(lambda e: e.tensor_reduce(col(mu), oh, AX.X, ALU.add), a)
        a = dve.do(lambda e: e.tensor_scalar(mu[:, :], mu[:, :], 1.0 / DV, None, ALU.mult), a)
        a = dve.do(lambda e: e.tensor_tensor(oh, oh, col(mu).to_broadcast([P, NT * H, DV]), ALU.subtract), a)
        a2 = act.do(lambda e: e.activation(tv[:, :, :], o[:, :, :], ACT.Square), a)
        a = dve.do(lambda e: e.tensor_reduce(col(var), th, AX.X, ALU.add), a2)
        a = dve.do(lambda e: e.tensor_scalar(var[:, :], var[:, :], 1.0 / DV, LN_EPS, ALU.mult, ALU.add), a)
        a = act.do(lambda e: e.activation(mu[:, :], var[:, :], ACT.Sqrt), a)
        a = dve.do(lambda e: e.reciprocal(var[:, :], mu[:, :]), a)
        a = dve.do(lambda e: e.tensor_tensor(oh, oh, col(var).to_broadcast([P, NT * H, DV]), ALU.mult), a)
        fin = []
        for t in range(NT):
            fin.append(dve.do(lambda e, t=t: e.tensor_tensor(o[:, t, :], o[:, t, :], gt[:, t, :],
                                                             ALU.mult), a, sg))
        orr = to_features(c, o, ot, fin, banks, ring)
        for t in range(NT):
            b, users = ring.take()
            mm = matmuls(c, banks[b][:, 0:D], [(ot[:, k, t * P:(t + 1) * P], w_out[:, k, :])
                                               for k in range(KC)], orr[t // 4], users)
            last = dve.do(lambda e, t=t, b=b: e.tensor_tensor(c.x[:, t, :], c.x[:, t, :],
                                                              banks[b][:, 0:D], ALU.add), mm)
            ring.used(b, last)
        c.x_ready = last


EXPERTS, GROUPS, TOP_GROUPS, TOP = 64, 8, 4, 8
GE = EXPERTS // GROUPS
FI = 128
CAP = 256
ROUTE_SCALE = 2.5
OUT = -1e30
TAKEN = -3e38


def experts(c, name, g):
    nc = c.nc
    c.stage(name)
    pe, act, dve, pool, sp = c.lanes
    NW = 3
    with ExitStack() as ctx:
        def sb(n, shape, dt=F32):
            return ctx.enter_context(nc.sbuf_tensor(f"{name}_{n}", shape, dt))
        gw, gb = sb("gw", [P, KC, EXPERTS]), sb("gb", [P, EXPERTS])
        upper, ones = sb("upper", [P, P]), sb("ones", [P, P])
        xn, xt = sb("xn", [P, NT, D]), sb("xt", [P, KC, N])
        sc, sf, pick = (sb(n, [P, NT, EXPERTS]) for n in ("sc", "sf", "pick"))
        srt = sb("srt", [P, NT, GROUPS, 8])
        gs, gm, g8, v8 = (sb(n, [P, NT, 8]) for n in ("gs", "gm", "g8", "v8"))
        wt, den = sb("wt", [P, NT, EXPERTS]), sb("den", [P, 2, NT])
        wg, wu, wd = sb("wg", [P, NW, KC, FI]), sb("wu", [P, NW, KC, FI]), sb("wd", [P, NW, D])
        sg, hh = sb("sg", [P, 2, 512]), sb("hh", [P, 2, 512])
        st = (sb("st", [P, NT, 6]), sb("mv", [P, NT, 2]), sb("rs", [P, 3, NT]))
        banks = [ctx.enter_context(nc.psum_tensor(f"{name}_bank{i}", [P, 512], F32)) for i in range(8)]
        ring = Ring(8)
        slot = c.slot(f"{name}_w")
        w_slot = [c.slot(f"{name}_w{i}") for i in range(NW)]
        sp.dma(slot, gw[:, :, :], g("moe_gw").rearrange("(k p) n -> p k n", p=P))
        sp.dma(slot, gb[:, :], g("moe_gb"))
        w = sp.dma(slot, upper[:, :], g("upper"))
        w_ring = Ring(NW)

        def load(e_):
            i, users = w_ring.take()
            sp.dma(w_slot[i], wg[:, i, :, :], g("moe_wg")[e_].rearrange("(k p) n -> p k n", p=P), users)
            sp.dma(w_slot[i], wu[:, i, :, :], g("moe_wu")[e_].rearrange("(k p) n -> p k n", p=P))
            return i, sp.dma(w_slot[i], wd[:, i, :], g("moe_wd")[e_])
        loaded = {e_: load(e_) for e_ in range(NW - 1)}
        one = dve.do(lambda e: e.memset(ones[:, :], 1.0))
        normed = layernorm(c, c.x, xn, st, c.x_ready)
        xr = to_features(c, xn, xt, normed, banks, ring)
        sr = []
        for t in range(NT):
            b, users = ring.take()
            mm = matmuls(c, banks[b][:, 0:EXPERTS], [(xt[:, k, t * P:(t + 1) * P], gw[:, k, :])
                                                     for k in range(KC)], xr[t // 4], w, users)
            a = act.do(lambda e, t=t, b=b: e.activation(sc[:, t, :], banks[b][:, 0:EXPERTS],
                                                        ACT.Sigmoid), mm)
            ring.used(b, a)
            sr.append(dve.do(lambda e, t=t: e.tensor_tensor(sf[:, t, :], sc[:, t, :], gb[:, :], ALU.add), a))
        for t in range(NT):
            for gr in range(GROUPS):
                a = dve.do(lambda e, t=t, gr=gr: e.max(srt[:, t, gr, :], sf[:, t, gr * GE:(gr + 1) * GE]),
                           sr[t])
        a = dve.do(lambda e: e.tensor_tensor(gs[:, :, :], srt[:, :, :, 0], srt[:, :, :, 1], ALU.add), a)
        for t in range(NT):
            a1 = dve.do(lambda e, t=t: e.max(g8[:, t, :], gs[:, t, :]), a)
        a1 = dve.do(lambda e: e.memset(g8[:, :, TOP_GROUPS:], -OUT), a1)
        for t in range(NT):
            a2 = dve.do(lambda e, t=t: e.match_replace(gm[:, t, :], g8[:, t, :], gs[:, t, :], TAKEN), a1)
        a2 = dve.do(lambda e: e.tensor_scalar(gm[:, :, :], gm[:, :, :], TAKEN / 2, OUT, ALU.is_gt, ALU.mult), a2)
        gmb = gm[:, :, :].rearrange("p t (g o) -> p (t g) o", o=1).to_broadcast([P, NT * GROUPS, GE])
        a = dve.do(lambda e: e.tensor_tensor(
            sf[:, :, :].rearrange("p t (g j) -> p (t g) j", j=GE),
            sf[:, :, :].rearrange("p t (g j) -> p (t g) j", j=GE), gmb, ALU.add), a2)
        for t in range(NT):
            a1 = dve.do(lambda e, t=t: e.max(v8[:, t, :], sf[:, t, :]), a)
        for t in range(NT):
            a2 = dve.do(lambda e, t=t: e.match_replace(pick[:, t, :], v8[:, t, :], sf[:, t, :], TAKEN), a1)
        pr = dve.do(lambda e: e.tensor_scalar(pick[:, :, :], pick[:, :, :], TAKEN / 2, None, ALU.is_lt), a2)
        a = dve.do(lambda e: e.tensor_tensor(wt[:, :, :], sc[:, :, :], pick[:, :, :], ALU.mult), pr)
        a = dve.do(lambda e: e.tensor_reduce(den[:, 0, :].rearrange("p (t o) -> p t o", o=1),
                                             wt[:, :, :], AX.X, ALU.add), a)
        a = dve.do(lambda e: e.tensor_scalar(den[:, 0, :], den[:, 0, :], 1e-20, None, ALU.add), a)
        a = dve.do(lambda e: e.reciprocal(den[:, 1, :], den[:, 0, :]), a)
        for t in range(NT):
            wr = dve.do(lambda e, t=t: e.tensor_scalar(wt[:, t, :], wt[:, t, :], den[:, 1, t:t + 1],
                                                      ROUTE_SCALE, ALU.mult, ALU.mult), a)
        for t in range(NT):
            b, users = ring.take()
            mm = matmuls(c, banks[b][:, 0:EXPERTS],
                         [(ones[:, :], pick[:, j, :]) for j in range(t)] + [(upper[:, :], pick[:, t, :])],
                         pr, one, w, users)
            a = dve.do(lambda e, t=t, b=b: e.scalar_tensor_tensor(
                wt[:, t, :], banks[b][:, 0:EXPERTS], CAP + 0.5, wt[:, t, :], ALU.is_lt, ALU.mult),
                mm, wr)
            ring.used(b, a)
        w_done = a
        up_ring, y_ring, h_ring = Ring(2), Ring(4), Ring(2)
        for i in range(8):
            (up_ring.used(i // 2, ring.users[i]) if i < 4 else y_ring.used(i - 4, ring.users[i]))

        def up(e_, half):
            i, m = loaded[e_]
            b, users = up_ring.take()
            pairs = [(wg[:, i, k, :], xt[:, k, half * 512:(half + 1) * 512]) for k in range(KC)]
            m1 = matmuls(c, banks[2 * b][:, :], pairs, m, xr, users)
            pairs = [(wu[:, i, k, :], xt[:, k, half * 512:(half + 1) * 512]) for k in range(KC)]
            m2 = matmuls(c, banks[2 * b + 1][:, :], pairs)
            h, husers = h_ring.take()
            a = act.do(lambda e: e.activation(sg[:, h, :], banks[2 * b][:, :], ACT.Silu), m1, husers)
            a = dve.do(lambda e: e.tensor_tensor(hh[:, h, :], sg[:, h, :], banks[2 * b + 1][:, :],
                                                 ALU.mult), a, m2)
            up_ring.used(b, a)
            return e_, half, h, a

        def down(e_, half, h, a):
            i, _ = loaded[e_]
            for p in range(2):
                y, users = y_ring.take()
                for j in range(2):
                    t = 4 * half + 2 * p + j
                    mm = pe.do(lambda e, j=j, y=y, t=t: e.matmul(
                        banks[4 + y][:, j * D:(j + 1) * D], hh[:, h, (t % 4) * P:(t % 4 + 1) * P],
                        wd[:, i, :], start=True, stop=True), a, users, count=(j == 1))
                for j in range(2):
                    t = 4 * half + 2 * p + j
                    s = dve.do(lambda e, j=j, y=y, t=t: e.scalar_tensor_tensor(
                        c.x[:, t, :], banks[4 + y][:, j * D:(j + 1) * D], wt[:, t, e_:e_ + 1],
                        c.x[:, t, :], ALU.mult, ALU.add), mm, w_done, acc.get(t))
                    acc[t] = s
                y_ring.used(y, s)
            h_ring.used(h, mm)
            w_ring.used(i, mm)
            return s
        acc = {}
        pending = None
        for e_ in range(EXPERTS):
            for half in range(2):
                if half == 1 and e_ + NW - 1 < EXPERTS:
                    loaded[e_ + NW - 1] = load(e_ + NW - 1)
                unit = up(e_, half)
                if pending is not None:
                    down(*pending)
                pending = unit
        last = down(*pending)
        c.x_ready = last


def scratch_tensors(nc):
    return {"keys": nc.dram_tensor("keys", (2 * B * (SK // 1024), 3, P, 1024), BF16, kind="Internal").ap(),
            "parked": nc.dram_tensor("parked", (P, NT, D), F32, kind="Internal").ap()}


def head_rows(w):
    w = np.asarray(w)
    z = np.zeros(w.shape[:-1] + (H, 32), w.dtype)
    z[..., 0:16] = w.reshape(w.shape[:-1] + (H, 16))
    return np.ascontiguousarray(z.reshape(w.shape[:-1] + (2 * D,)))


def more_layout(a, o, rows, cols):
    w, b = a["L0_attn_Wqkv_w"], a["L0_attn_Wqkv_b"]
    for i, n in enumerate("qkv"):
        o[f"ca_w{n}"] = head_rows(w[i * D:(i + 1) * D].T)
    o["ca_bv"] = rows(head_rows(b[2 * D:]))
    o["ca_cols"] = np.ascontiguousarray(np.concatenate(
        [cols(head_rows(v)) for v in (b[0:D], b[D:2 * D], a["L0_attn_conv_b"])], 1))
    cw = a["L0_attn_conv_w"].transpose(2, 1, 0)
    cw = head_rows(cw)
    o["ca_cw"] = np.ascontiguousarray(head_rows(cw.transpose(0, 2, 1)).transpose(0, 2, 1))
    o["ca_wo"] = np.ascontiguousarray(head_rows(a["L0_attn_out_w"]).T)
    o["ca_bo"] = rows(a["L0_attn_out_b"])
    i, j = np.arange(P)[:, None], np.arange(2 * P)[None, :]
    o["causal"] = np.where(np.concatenate([j[:, :P] <= i, j <= i + P], 1), 0, NEG).astype(np.float32)
    f = np.float32
    o["lt_wqkv"] = a["L0_ffn_Wqkv"]
    o["lt_wo"] = a["L0_ffn_Wo"]
    w1 = np.zeros((DEPTH, D, 2, FFP), f)
    w1[..., :FF] = a["L0_ffn_W1"].reshape(DEPTH, D, 2, FF)
    o["lt_w1"] = w1.reshape(DEPTH, D, 2 * FFP)
    w2 = np.zeros((DEPTH, FFP, D), f)
    w2[:, :FF] = a["L0_ffn_W2"]
    o["lt_w2"] = w2
    b1 = np.zeros((DEPTH, 2, FFP), f)
    b1[..., :FF] = a["L0_ffn_b1"].reshape(DEPTH, 2, FF)
    o["lt_ffc"] = np.ascontiguousarray(b1.reshape(-1, P).T)
    ln = np.stack([a["L0_ffn_ln_g"], a["L0_ffn_ln_b"]], 1)
    o["lt_lnc"] = np.ascontiguousarray(ln.reshape(-1, P).T)
    o["lt_b2"] = np.ascontiguousarray(np.broadcast_to(a["L0_ffn_b2"][:, None], (DEPTH, P, D)))
    qs, ks = a["L0_ffn_q_scale"], a["L0_ffn_k_scale"]
    scl = np.stack([qs, np.roll(qs, 32, 1), ks, np.roll(ks, 32, 1)], 1).reshape(DEPTH, 1, 4 * LH)
    o["lt_scl"] = np.ascontiguousarray(np.broadcast_to(scl, (DEPTH, P, 4 * LH)))
    half = np.arange(0, LH, 2, dtype=f)
    t = np.arange(S, dtype=f)
    freqs = t[:, None] * (f(1) / f(10000) ** (half / f(LH)))[None, :]
    base = (half + f(0.4 * LH)) / f(1.4 * LH)
    scale = base[None, :] ** ((t - S // 2) / f(32))[:, None]
    cos, sin = np.cos(freqs), np.sin(freqs)
    two = lambda p, q: np.concatenate([p, q], 1)
    rot = np.stack([two(cos * scale, cos * scale), two(-sin * scale, sin * scale),
                    two(cos / scale, cos / scale), two(-sin / scale, sin / scale)])
    o["lt_rot"] = np.ascontiguousarray(
        rot.reshape(4, 2, P, LH).transpose(2, 0, 1, 3).reshape(P, -1).astype(f))
    band = np.concatenate([(j[:, :P] <= i) & (j[:, :P] >= i - 64),
                           (j <= i + P) & (j >= i + P - 64)], 1)
    o["band"] = np.where(band, 0, NEG).astype(f)
    o["gla_taps"] = np.ascontiguousarray(
        a["L1_attn_conv_w"].reshape(KC, P, TAPS).transpose(1, 0, 2).reshape(P, -1))
    o["gla_win"] = np.ascontiguousarray(np.concatenate(
        [a[f"L1_attn_W{n}"] for n in ("q", "kg", "v", "g")], 1))
    o["gla_wout"] = a["L1_attn_Wout"]
    o["gla_bg"] = rows(a["L1_attn_bg"])
    o["gla_aug"] = rows(a["L1_attn_aug_balance"])
    o["moe_gw"] = np.ascontiguousarray(a["L1_ffn_gate_w"].T)
    o["moe_gb"] = rows(a["L1_ffn_gate_bias"])
    o["moe_wg"], o["moe_wu"], o["moe_wd"] = (a[f"L1_ffn_w_{n}"] for n in ("gate", "up", "down"))
    o["upper"] = np.triu(np.ones((P, P), np.float32))


def build(nc, ins, out, scratch, first=0, last=5):
    with ExitStack() as ctx:
        c = Core(nc, ctx)
        sb = lambda n, shape, dt=F32: ctx.enter_context(nc.sbuf_tensor(n, shape, dt))
        c.x = sb("x_sb", [P, NT, D])
        c.parked = scratch["parked"]
        c.minus_half = sb("minus_half", [P, 64])
        c.ident = sb("ident", [P, P])
        c.ident_bf = sb("ident_bf", [P, P], BF16)
        c.stage("load")
        s = c.slot("load")
        c.sp.dma(s, c.x[:, :, :], ins["x"].rearrange("b (q p) d -> p (b q) d", p=P))
        m = c.sp.dma(s, c.ident[:, :], ins["ident"])
        half = c.dve.do(lambda e: e.memset(c.minus_half[:, :], -0.5))
        c.x_ready = [m, half]
        c.ident_ready = c.dve.do(lambda e: e.tensor_copy(c.ident_bf[:, :], c.ident[:, :]), m)
        g = ins.get
        for i in range(first, last + 1):
            STAGES[i](c, g, scratch)
        c.stage("store")
        s = c.slot("store")
        m = c.sp.dma(s, out.rearrange("b (q p) d -> p (b q) d", p=P), c.x[:, :, :])
        c.sp.hold(m)
        with nc.Block() as block:
            block.sync(lambda e: c.sp.replay(e))
            block.gpsimd(lambda e: c.pool.replay(e))
            block.scalar(lambda e: c.act.replay(e))
            block.vector(lambda e: c.dve.replay(e))
            block.tensor(lambda e: c.pe.replay(e))


STAGES = [
    lambda c, g, d: cross_attention(c, "xa0", g("ctx_t"), g("xa0_wq"), g("xa0_wk"), g("xa0_wv"), g("xa0_wo"),
                                 g("xa0_bq"), g("xa0_bk"), g("xa0_bv"), g("xa0_bo"), d["keys"]),
    lambda c, g, d: conv_attention(c, "ca", g),
    lambda c, g, d: local_transformer(c, "lt", g),
    lambda c, g, d: cross_attention(c, "xa1", g("ctx_t"), g("xa1_wq"), g("xa1_wk"), g("xa1_wv"), g("xa1_wo"),
                                 None, None, None, g("xa1_bo"), d["keys"]),
    lambda c, g, d: gated_linear_attention(c, "gla", g),
    lambda c, g, d: experts(c, "moe", g),
]


def layout(inputs):
    a = {k: np.asarray(v) for k, v in inputs.items()}

    def rows(v):
        return np.ascontiguousarray(np.broadcast_to(v, (P, v.shape[-1])))

    def cols(v):
        return np.ascontiguousarray(v.reshape(-1, P).T)

    o = {"x": a["x"], "ident": np.eye(P, dtype=np.float32)}
    o["ctx_t"] = np.ascontiguousarray(a["ctx_1024"].transpose(0, 2, 1))
    for n in "qkvo":
        o[f"xa0_w{n}"] = np.ascontiguousarray(a[f"L0_xattn_w_{n}"].T)
        o[f"xa1_w{n}"] = np.ascontiguousarray(a[f"L1_xattn_W{n}"].T)
    for n in "qvo":
        o[f"xa0_b{n}"] = rows(a[f"L0_xattn_b_{n}"])
    o["xa0_bk"] = cols(a["L0_xattn_b_k"])
    o["xa1_bo"] = rows(a["L1_xattn_bo"])
    more_layout(a, o, rows, cols)
    return o


def kernel(**inputs):
    import concourse.bacc as bacc
    from concourse.bass_utils import run_bass_kernel_spmd

    nc = bacc.Bacc("TRN2", target_bir_lowering=False, num_devices=1)
    arrays = layout(inputs)
    ins = {k: nc.dram_tensor(f"in_{k}", v.shape, mybir.dt.from_np(v.dtype), kind="ExternalInput").ap()
           for k, v in arrays.items()}
    out = nc.dram_tensor("result", (B, S, D), F32, kind="ExternalOutput").ap()
    build(nc, ins, out, scratch_tensors(nc))
    r = run_bass_kernel_spmd(nc, [{f"in_{k}": v for k, v in arrays.items()}], core_ids=[0])
    return r.results[0]["result"]
```

```python
from contextlib import ExitStack

import numpy as np

import concourse.bass as bass
from concourse import mybir

F32 = mybir.dt.float32
BF16 = mybir.dt.bfloat16
ALU = mybir.AluOpType
ACT = mybir.ActivationFunctionType
AX = mybir.AxisListType

P = 128
B, S, D = 4, 256, 256
N = B * S
NT = N // P
KC = D // P
H = 16
SK = 4096
LN_EPS = 1e-5
NEG = -1e30


class Mark:

    def __init__(self, sem, value):
        self.sem, self.value = sem, value


def flat(marks):
    for m in marks:
        if m is None:
            continue
        if isinstance(m, Mark):
            yield m
        else:
            yield from flat(m)


class Lane:

    def __init__(self, name):
        self.name, self.queue, self.sem, self.count = name, [], None, 0

    def use(self, sem):
        self.sem, self.count = sem, 0

    def do(self, build, *waits, count=True):
        self.queue.append((list(flat(waits)), build, self.sem if count else None, 1))
        if not count:
            return None
        self.count += 1
        return Mark(self.sem, self.count)

    def dma(self, slot, dst, src, *waits):
        self.queue.append((list(flat(waits)), lambda e: e.dma_start(dst, src), slot.sem, 16))
        slot.count += 16
        return Mark(slot.sem, slot.count)

    def hold(self, *waits):
        self.queue.append((list(flat(waits)), None, None, 0))

    def last(self):
        return Mark(self.sem, self.count) if self.count else None

    def replay(self, engine):
        reached = {}
        for waits, build, sem, step in self.queue:
            for m in waits:
                if reached.get(m.sem.name, 0) < m.value:
                    engine.wait_ge(m.sem, m.value)
                    reached[m.sem.name] = m.value
            if build is not None:
                ins = build(engine)
                if sem is not None:
                    ins.then_inc(sem, step)


class Slot:

    def __init__(self, sem):
        self.sem, self.count = sem, 0


class Ring:

    def __init__(self, n):
        self.users, self.at = [[] for _ in range(n)], -1

    def take(self):
        self.at = (self.at + 1) % len(self.users)
        users, self.users[self.at] = self.users[self.at], []
        return self.at, users

    def used(self, i, *marks):
        self.users[i] += list(flat(marks))


class Core:

    def __init__(self, nc, ctx):
        self.nc, self.ctx = nc, ctx
        self.pe, self.act, self.dve, self.pool, self.sp = (
            Lane(n) for n in ("pe", "act", "dve", "pool", "sp"))
        self.lanes = (self.pe, self.act, self.dve, self.pool, self.sp)
        self.nsem = 0
        self.slots = []

    def sem(self, name):
        self.nsem += 1
        return self.ctx.enter_context(self.nc.semaphore(f"{name}_{self.nsem}"))

    def slot(self, name):
        s = Slot(self.sem(name))
        self.slots.append(s)
        return s

    def stage(self, name):
        ends = [l.last() for l in self.lanes if l.sem is not None]
        ends += [Mark(s.sem, s.count) for s in self.slots if s.count]
        for lane in self.lanes:
            lane.hold(ends)
            lane.use(self.sem(f"{name}_{lane.name}"))


def rsqrt(c, out, src, n, *waits):
    return c.pool.do(lambda e: e.tensor_tensor(out, src, c.minus_half[:, 0:n], ALU.pow), *waits)


def token_stats(c, tiles, ready):
    for t in tiles:
        a = c.dve.do(lambda e, t=t: e.bn_stats(c.stats[:, t, :], c.x[:, t, :]), ready)
        last = c.dve.do(lambda e, t=t: e.bn_aggr(c.mean_var[:, t, :], c.stats[:, t, :]), a)
    if NT - 1 in tiles:
        a = c.dve.do(lambda e: e.tensor_scalar(c.rstd[:, 0, :], c.mean_var[:, :, 1], LN_EPS, None,
                                               ALU.add), last)
        c.stats_ready = rsqrt(c, c.rstd[:, 1, :], c.rstd[:, 0, :], NT, a)


def layernorm(c, dst, by_tile=[None] * NT):
    return [c.dve.do(lambda e, t=t: e.tensor_scalar(
        dst[:, t, :], c.x[:, t, :], c.mean_var[:, t, 0:1], c.rstd[:, 1, t:t + 1],
        ALU.subtract, ALU.mult), c.stats_ready, c.x_ready, by_tile[t]) for t in range(NT)]


def to_features(c, src, dst, ready, banks, ring, affine=None, tiles=NT, lanes=None):
    width = src.shape[2] if len(src.shape) == 3 else D
    out = []
    for g in range(tiles // 4):
        group = []
        for k in range(width // P):
            b, users = ring.take()
            for j in range(4):
                t = 4 * g + j
                tr = c.pe.do(lambda e, t=t, k=k, j=j, b=b: e.transpose(
                    banks[b][:, j * P:(j + 1) * P], src[:, t, k * P:(k + 1) * P], c.ident[:, :]),
                    ready[t], users, c.ident_ready, count=(j == 3))
            o = dst[:, k, g * 512:(g + 1) * 512]
            if affine is not None:
                gain, bias = affine
                ev = c.dve.do(lambda e, o=o, b=b, k=k: e.tensor_scalar(
                    o, banks[b][:, :], gain[:, k:k + 1], bias[:, k:k + 1], ALU.mult, ALU.add), tr)
            elif k % 2:
                ev = c.act.do(lambda e, o=o, b=b: e.activation(o, banks[b][:, :], ACT.Copy), tr)
            else:
                ev = c.dve.do(lambda e, o=o, b=b: e.tensor_copy(o, banks[b][:, :]), tr)
            ring.used(b, ev)
            group.append(ev)
        out.append(group)
    return out


def matmuls(c, out, pairs, *waits):
    n = len(pairs)
    for i, (l, r) in enumerate(pairs):
        m = c.pe.do(lambda e, i=i, l=l, r=r: e.matmul(out, l, r, start=(i == 0), stop=(i == n - 1)),
                    waits if i == 0 else [], count=(i == n - 1))
    return m


def cross_attention(c, name, ctx_t, wq, wk, wv, wo, bq, bk, bv, bo, kscratch):
    nc = c.nc
    KB = 1024
    NKB = SK // KB
    ITEMS = B * NKB
    DH = D // H
    STACK = 6 * DH
    ROWS = STACK + 3
    Q_PART = (0, 1, 0, 1, 2, 0)
    K_PART = (0, 0, 1, 1, 0, 2)
    KT = KB // P
    QUADS = H // 4
    SLOTS = QUADS * KT
    VW = DH + 1
    NU = 5
    NV = 3
    c.stage(name)
    pe, act, dve, pool, sp = c.lanes
    with ExitStack() as long:
        def sb(n, shape, dt=F32, ctx=long):
            return ctx.enter_context(nc.sbuf_tensor(f"{name}_{n}", shape, dt))

        def ps(n, shape, dt=F32, ctx=long):
            return ctx.enter_context(nc.psum_tensor(f"{name}_{n}", shape, dt))

        att = sb("att", [P, NT, D])
        q_base = sb("q_base", [P, H, N], BF16)
        wk_sb, wv_sb = sb("wk", [P, KC, D]), sb("wv", [P, KC, D])
        w_slot = c.slot(f"{name}_w")
        w_mark = sp.dma(w_slot, wk_sb[:, :, :], wk.rearrange("(k p) n -> p k n", p=P))
        w_mark = sp.dma(w_slot, wv_sb[:, :, :], wv.rearrange("(k p) n -> p k n", p=P))
        if bk is not None:
            bk_sb = sb("bk", [P, KC])
            w_mark = sp.dma(w_slot, bk_sb[:, :], bk)
        ks = [sb(f"ks{u}", [P, 8, KB], BF16) for u in range(2)]
        vs = sb("vs", [P, NV, KT, H, VW])
        cx = sb("cx", [P, 2, KC, KB])
        kp = sb("kp", [P, 2, 3, 512], BF16)
        kr = sb("kr", [P, 512])
        pj = ps("pj", [P, 512])
        pj_bf = pj[:, :].bitcast(BF16)
        pj_ring, ks_ring, vs_ring, cx_ring, kp_ring = Ring(1), Ring(NU), Ring(NV), Ring(2), Ring(2)
        ks_slot = [c.slot(f"{name}_ks{i}") for i in range(NU)]
        cx_slot = [c.slot(f"{name}_cx{i}") for i in range(2)]
        kd_slot = [c.slot(f"{name}_kd{i}") for i in range(4)]
        ones_k = pool.do(lambda e: e.memset(ks[0][STACK:ROWS, :, :], 1.0))
        init = [pool.do(lambda e: e.memset(vs[:, :, :, :, DH:VW], 1.0), ones_k)]
        ctx_r = ctx_t.rearrange("b (k p) s -> b p k s", p=P)
        item = [dict() for _ in range(ITEMS)]
        c.kr_users = []

        def load_ctx(i):
            b, kb = divmod(i, NKB)
            s, users = cx_ring.take()
            item[i]["cx"] = s
            item[i]["cx_ready"] = sp.dma(cx_slot[s], cx[:, s, :, :],
                                         ctx_r[b, :, :, kb * KB:(kb + 1) * KB], users)

        def project_keys(i, mt, ch):
            b, kb = divmod(i, NKB)
            s = item[i]["cx"]
            _, users = pj_ring.take()
            mm = matmuls(c, pj[:, :],
                         [(wk_sb[:, k, mt * P:(mt + 1) * P], cx[:, s, k, ch * 512:(ch + 1) * 512])
                          for k in range(KC)], item[i]["cx_ready"], w_mark, users)
            cx_ring.used(s, mm)
            p, pusers = kp_ring.take()
            bias = bk_sb[:, mt:mt + 1] if bk is not None else 0.0
            if bk is not None:
                a = act.do(lambda e: e.activation(kp[:, p, 0, :], pj[:, :], ACT.Identity, bias=bias),
                           mm, pusers)
            else:
                a = act.do(lambda e: e.activation(kp[:, p, 0, :], pj[:, :], ACT.Copy), mm, pusers)
            r = dve.do(lambda e: e.scalar_tensor_tensor(
                kr[:, :], pj[:, :], bias, kp[:, p, 0, :], ALU.add, ALU.subtract),
                a, c.kr_users)
            pj_ring.used(0, a, r)
            a2 = pool.do(lambda e: e.tensor_copy(kp[:, p, 1, :], kr[:, :]), r, pusers, init)
            a3 = pool.do(lambda e: e.tensor_tensor(
                kp[:, p, 2, :], kr[:, :], kp[:, p, 1, :], ALU.subtract), a2)
            c.kr_users = [a3]
            d = (2 * i + mt) % 2
            out = sp.dma(kd_slot[2 * d + ch], kscratch[2 * i + mt, :, :, ch * 512:(ch + 1) * 512]
                         .rearrange("c p n -> p c n"), kp[:, p, :, :], a, a2, a3)
            kp_ring.used(p, out)
            item[i].setdefault(("k", mt), []).append(out)

        def stack_keys(i, mt):
            u, users = ks_ring.take()
            item[i][("unit", mt)] = u
            for j, part in enumerate(K_PART):
                m = sp.dma(ks_slot[u], ks[u][DH * j:DH * (j + 1), :, :],
                           kscratch[2 * i + mt, part, :, :].rearrange("(h d) n -> d h n", d=DH),
                           users, item[i][("k", mt)])
            item[i][("ready", mt)] = m

        def project_values(i, t):
            s = item[i]["cx"]
            if t == 0:
                item[i]["vs"], item[i]["vs_users"] = vs_ring.take()
                item[i]["v_ready"] = []
            v = item[i]["vs"]
            _, users = pj_ring.take()
            mm = matmuls(c, pj[:, 0:D],
                         [(cx[:, s, k, t * P:(t + 1) * P], wv_sb[:, k, :]) for k in range(KC)],
                         item[i]["cx_ready"], w_mark, users)
            cx_ring.used(s, mm)
            a = act.do(lambda e: e.activation(
                vs[:, v, t, :, 0:DH], pj[:, 0:D].rearrange("p (h d) -> p h d", d=DH), ACT.Copy),
                mm, item[i]["vs_users"], init)
            pj_ring.used(0, a)
            item[i]["v_ready"].append(a)

        KEY_SLOTS, VALUE_SLOTS = ((0, 5), (16, 21)), (7, 9, 12, 14, 23, 25, 28, 30)

        def fill_step(i, s):
            for mt, slots in enumerate(KEY_SLOTS):
                if s in slots:
                    project_keys(i, mt, slots.index(s))
                if s == slots[-1] + 1:
                    stack_keys(i, mt)
            if s in VALUE_SLOTS:
                project_values(i, VALUE_SLOTS.index(s))
            if s == 1 and i + 1 < ITEMS:
                load_ctx(i + 1)

        load_ctx(0)

        with ExitStack() as short:
            xn = sb("xn", [P, NT, D], ctx=short)
            xt = sb("xt", [P, KC, N], ctx=short)
            wq_sb = sb("wq", [P, KC, D], ctx=short)
            qf = sb("qf", [P, 2, 4, D], ctx=short)
            qr = sb("qr", [P, 2, 4, D], ctx=short)
            qtm = sb("qtm", [P, 2, 4 * H, STACK], BF16, ctx=short)
            bq_sb = sb("bq", [P, D], ctx=short)
            banks = [ps(f"bank{i}", [P, 512], ctx=short) for i in range(4)]
            tbank = [ps(f"tbank{i}", [P, 8, P], BF16, ctx=short) for i in range(3)]
            ring, tring = Ring(4), Ring(3)
            q_slot = c.slot(f"{name}_wq")
            wq_mark = sp.dma(q_slot, wq_sb[:, :, :], wq.rearrange("(k p) n -> p k n", p=P))
            if bq is not None:
                wq_mark = sp.dma(q_slot, bq_sb[:, :], bq)
            def queries():
                normed = layernorm(c, xn)
                yield
                yield
                xt_ready = to_features(c, xn, xt, normed, banks, ring)
                turned = []
                for grp in range(NT // 4):
                    got = []
                    for pair in range(2):
                        b, users = ring.take()
                        for j in range(2):
                            t = 4 * grp + 2 * pair + j
                            mm = matmuls(c, banks[b][:, j * D:(j + 1) * D],
                                         [(xt[:, k, t * P:(t + 1) * P], wq_sb[:, k, :]) for k in range(KC)],
                                         xt_ready[grp], wq_mark, users)
                        f2 = qf[:, grp, 2 * pair:2 * pair + 2, :]
                        p2 = banks[b][:, :].rearrange("p (j n) -> p j n", j=2)
                        if bq is not None:
                            bqb = bq_sb[:, :].rearrange("p (o n) -> p o n", o=1).to_broadcast([P, 2, D])
                            a = dve.do(lambda e, f2=f2, p2=p2, bqb=bqb: e.tensor_tensor(
                            f2, p2, bqb, ALU.add), mm)
                        else:
                            a = dve.do(lambda e, f2=f2, p2=p2: e.tensor_copy(f2, p2), mm)
                        ring.used(b, a)
                        got.append(a)
                        yield

                    def part(j, grp=grp):
                        return qtm[:, grp, :, j * DH:(j + 1) * DH]
                    f3 = qf[:, grp, :, :].rearrange("p t (h d) -> p (t h) d", d=DH)
                    r3 = qr[:, grp, :, :].rearrange("p t (h d) -> p (t h) d", d=DH)
                    a0 = act.do(lambda e, o=part(0), f3=f3: e.activation(o, f3, ACT.Copy, scale=0.25), got)
                    a = dve.do(lambda e, r3=r3, f3=f3, o=part(0): e.scalar_tensor_tensor(
                        r3, f3, 0.25, o, ALU.mult, ALU.subtract), a0)
                    a1 = act.do(lambda e, o=part(1), r3=r3: e.activation(o, r3, ACT.Copy), a)
                    a2 = dve.do(lambda e, r3=r3, o=part(4), s=part(1): e.tensor_tensor(
                        o, r3, s, ALU.subtract), a1)
                    done = [a2, pool.do(lambda e, o=part(2), s=part(0): e.tensor_copy(o, s), a0),
                            act.do(lambda e, o=part(5), s=part(0): e.activation(o, s, ACT.Copy), a0),
                            dve.do(lambda e, o=part(3), s=part(1): e.tensor_copy(o, s), a1)]
                    turned.append(done)
                for grp, done in enumerate(turned):
                    for g in range(H // 2):
                        tb, tusers = tring.take()
                        for j in range(8):
                            hh, t = divmod(j, 4)
                            tr = pe.do(lambda e, tb=tb, j=j, hh=hh, t=t, g=g, grp=grp: e.transpose(
                                tbank[tb][0:STACK, j, :], qtm[:, grp, t * H + 2 * g + hh, :],
                                c.ident_bf[:, :]),
                                done, tusers, c.ident_ready, count=(j == 7))
                        src = tbank[tb][0:STACK, :, :].rearrange("p (h t) n -> p h (t n)", h=2)
                        dst = q_base[0:STACK, 2 * g:2 * g + 2, grp * 512:(grp + 1) * 512]
                        if g % 2:
                            ev = act.do(lambda e, dst=dst, src=src: e.activation(dst, src, ACT.Copy), tr)
                        else:
                            ev = dve.do(lambda e, dst=dst, src=src: e.tensor_copy(dst, src), tr)
                        tring.used(tb, ev)
                        yield

            def first_block():
                for s in range(SLOTS):
                    fill_step(0, s)
                    if s in KEY_SLOTS[0] + KEY_SLOTS[1] + VALUE_SLOTS:
                        yield
            run_even((queries(), 23, 0), (first_block(), 16, 0))
        c.stage(f"{name}_blocks")
        ks += [sb(f"ks{u}", [P, 8, KB], BF16) for u in range(2, NU)]
        ex = sb("ex", [P, 2, 4, S])
        o_sb = sb("o_sb", [P, 2, S])
        o_all = sb("o_all", [P, NKB, 2, H, VW])
        m_part = sb("m_part", [P, 2, 2, H, 2])
        m_blk2 = sb("m_blk", [P, 2, 2, H, NKB])
        m_spl = sb("m_spl", [P, 2, 8, 4])
        mt_bf = sb("mt_bf", [P, 2, 8, 3], BF16)
        w_blk = sb("w_blk", [P, 2, H, NKB])
        m_all = sb("m_all", [P, 2, H])
        acc = sb("acc", [P, 2, H, VW])
        sc = [ps(f"sc{i}", [P, 4, S]) for i in range(2)]
        mx = [ps(f"mx{i}", [P, 512]) for i in range(2)]
        pv = ps("pv", [P, S])
        sc_ring, mx_ring, pv_ring = Ring(2), Ring(2), Ring(1)
        ex_ring, o_ring, ms_ring = Ring(2), Ring(2), Ring(2)
        for u in range(1, NU):
            init.append(sp.dma(ks_slot[u], ks[u][STACK:ROWS, :, :], ks[0][STACK:ROWS, :, :], ones_k))
        init.append(dve.do(lambda e: e.memset(pv[:, :], 0.0)))

        q_m_users = [[] for _ in range(QUADS)]
        blk_users = []
        m_blk_users = [[], []]
        att_ready = {}

        def block_max(i, h, qt):
            b, kb = divmod(i, NKB)
            mt, hl = divmod(h, 8)
            u = item[i][("unit", mt)]
            par = i % 2
            if h == 0 and qt == 0:
                item[i]["mx"] = []
            for ch in range(2):
                s, users = mx_ring.take()
                mm = pe.do(lambda e, s=s, ch=ch: e.matmul(
                    mx[s][:, :], q_base[0:STACK, h, b * S + qt * P:b * S + (qt + 1) * P],
                    ks[u][0:STACK, hl, ch * 512:(ch + 1) * 512], start=True, stop=True),
                    item[i][("ready", mt)], users)
                r = dve.do(lambda e, s=s, ch=ch: e.tensor_reduce(
                    m_part[:, par, qt, h, ch:ch + 1], mx[s][:, :], AX.X, ALU.max), mm,
                    c.m_part_users.get((par, h)))
                mx_ring.used(s, r)
                item[i]["mx"].append(r)

        def place_max(i, g):
            b, kb = divmod(i, NKB)
            par = i % 2
            hs = slice(4 * g, 4 * g + 4)
            s, users = ms_ring.take()
            m_blk = m_blk2[:, b % 2, :, :, :]
            a = dve.do(lambda e: e.tensor_reduce(m_blk[:, :, hs, kb:kb + 1], m_part[:, par, :, hs, :],
                                                 AX.X, ALU.max), item[i]["mx"], m_blk_users[b % 2])
            c.m_part_users.update({(par, h): [a] for h in range(4 * g, 4 * g + 4)})
            item[i].setdefault("blk", []).append(a)
            m8 = m_spl[:, s, :, :]
            neg = m8[:, :, 0].rearrange("p (q h) -> p q h", q=2)
            a = dve.do(lambda e: e.tensor_scalar(neg, m_blk[:, :, hs, kb], -1.0, None, ALU.mult), a, users)
            a = dve.do(lambda e: e.tensor_copy(mt_bf[:, s, :, 0], m8[:, :, 0]), a)
            a = dve.do(lambda e: e.tensor_tensor(m8[:, :, 1], m8[:, :, 0], mt_bf[:, s, :, 0],
                                                 ALU.subtract), a)
            a = dve.do(lambda e: e.tensor_copy(mt_bf[:, s, :, 1], m8[:, :, 1]), a)
            a = dve.do(lambda e: e.tensor_tensor(mt_bf[:, s, :, 2], m8[:, :, 1], mt_bf[:, s, :, 1],
                                                 ALU.subtract), a)
            item[i]["spl", g] = (s, a)

        def place_max_rows(i, g):
            b = i // NKB
            hs = slice(4 * g, 4 * g + 4)
            s, a = item[i]["spl", g]
            _, pusers = pj_ring.take()
            for j in range(8):
                tr = pe.do(lambda e, j=j: e.transpose(
                    pj_bf[96:99, j * P:(j + 1) * P], mt_bf[:, s, j, :], c.ident_bf[:, :]),
                    a, pusers, count=(j == 7))
            ms_ring.used(s, tr)
            a = act.do(lambda e: e.activation(
                q_base[96:99, hs, b * S:(b + 1) * S].rearrange("p h (q t) -> p q h t", q=2),
                pj_bf[96:99, :].rearrange("p (q h t) -> p q h t", q=2, h=4), ACT.Copy),
                tr, q_m_users[g])
            q_m_users[g] = []
            pj_ring.used(0, a)
            item[i][("m", g)] = a

        def scores(i, g, kt):
            b = i // NKB
            s, users = sc_ring.take()
            for j in range(4):
                h = 4 * g + j
                mt, hl = divmod(h, 8)
                u = item[i][("unit", mt)]
                mm = pe.do(lambda e, s=s, j=j, h=h, u=u, hl=hl: e.matmul(
                    sc[s][:, j, :], ks[u][0:ROWS, hl, kt * P:(kt + 1) * P],
                    q_base[0:ROWS, h, b * S:(b + 1) * S], start=True, stop=True),
                    users, item[i][("m", g)], item[i][("ready", mt)], init, count=(j == 3))
            ks_ring.used(u, mm)
            q_m_users[g].append(mm)
            x, xusers = ex_ring.take()
            a = act.do(lambda e: e.activation(ex[:, x, :, :], sc[s][:, :, :], ACT.Exp), mm, xusers)
            sc_ring.used(s, a)
            return (i, g, kt, x, a)

        def weigh(unit):
            i, g, kt, x, a = unit
            v = item[i]["vs"]
            if kt == 0:
                _, c.pv_users = pv_ring.take()
            for j in range(4):
                mm = pe.do(lambda e, j=j: e.matmul(
                    pv[32 * j:32 * j + VW, :], vs[:, v, kt, 4 * g + j, :], ex[:, x, j, :],
                    start=(kt == 0), stop=(kt == KT - 1)),
                    a, item[i]["v_ready"], c.pv_users, init, count=(j == 3))
            ex_ring.used(x, mm)
            vs_ring.used(v, mm)
            if kt < KT - 1:
                return
            o, ousers = o_ring.take()
            ev = dve.do(lambda e: e.tensor_copy(o_sb[:, o, :], pv[:, :]), mm, ousers)
            pv_ring.used(0, ev)
            item[i][("o", g)] = (o, ev)

        def gather(i, g):
            kb = i % NKB
            o, ev = item[i][("o", g)]
            _, users = pj_ring.take()
            for q in range(2):
                tr = pe.do(lambda e, q=q: e.transpose(pj[:, q * P:(q + 1) * P],
                                                      o_sb[:, o, q * P:(q + 1) * P], c.ident[:, :]),
                           ev, users, count=(q == 1))
            o_ring.used(o, tr)
            a = dve.do(lambda e: e.tensor_copy(
                o_all[:, kb, :, 4 * g:4 * g + 4, :],
                pj[:, 0:S].rearrange("p (q h v) -> p q h v", q=2, h=4)[:, :, :, 0:VW]), tr, blk_users)
            pj_ring.used(0, a)
            item[i].setdefault("o", []).append(a)

        def combine(b):
            m_blk = m_blk2[:, b % 2, :, :, :]
            marks = [item[i][k] for i in range(b * NKB, (b + 1) * NKB) for k in ("o", "blk")]
            a = dve.do(lambda e: e.tensor_reduce(m_all[:, :, :].rearrange("p q (h o) -> p q h o", o=1),
                                                 m_blk[:, :, :, :], AX.X, ALU.max), marks)
            for kb in range(NKB):
                a2 = dve.do(lambda e, kb=kb: e.tensor_tensor(w_blk[:, :, :, kb], m_blk[:, :, :, kb],
                                                             m_all[:, :, :], ALU.subtract), a)
            a = act.do(lambda e: e.activation(w_blk[:, :, :, :], w_blk[:, :, :, :], ACT.Exp), a2)
            for kb in range(NKB):
                yield
                ob = o_all[:, kb, :, :, :].rearrange("p q h v -> p (q h) v")
                wb = (w_blk[:, :, :, kb:kb + 1].rearrange("p q h o -> p (q h) o")
                      .to_broadcast([P, 2 * H, VW]))
                a3 = dve.do(lambda e, ob=ob, wb=wb: e.tensor_tensor(ob, ob, wb, ALU.mult), a)
                ac = acc[:, :, :, :].rearrange("p q h v -> p (q h) v")
                if kb == 0:
                    a4 = dve.do(lambda e, ob=ob, ac=ac: e.tensor_copy(ac, ob), a3)
                else:
                    a4 = dve.do(lambda e, ob=ob, ac=ac: e.tensor_tensor(ac, ac, ob, ALU.add), a3, a4)
            blk_users[:] = [a4]
            m_blk_users[b % 2] = [a2]
            yield
            a = dve.do(lambda e: e.reciprocal(m_all[:, :, :], acc[:, :, :, DH]), a4)
            rb = m_all[:, :, :].rearrange("p q (h o) -> p (q h) o", o=1).to_broadcast([P, 2 * H, DH])
            av = acc[:, :, :, 0:DH].rearrange("p q h v -> p (q h) v")
            ov = att[:, 2 * b:2 * b + 2, :].rearrange("p q (h v) -> p (q h) v", v=DH)
            a = dve.do(lambda e: e.tensor_tensor(ov, av, rb, ALU.mult), a)
            att_ready[b] = a

        wo_sb, bo_sb, bv_sb = cx[:, 0, :, 0:D], cx[:, 0, 0, D:2 * D], cx[:, 0, 1, D:2 * D]
        at = cx[:, 1, :, :]
        wo_slot = c.slot(f"{name}_wo")

        def load_out():
            free = cx_ring.users[0] + cx_ring.users[1]
            sp.dma(wo_slot, wo_sb, wo.rearrange("(k p) n -> p k n", p=P), free)
            if bv is not None:
                sp.dma(wo_slot, bv_sb, bv)
            c.wo_ready = [sp.dma(wo_slot, bo_sb, bo), free]

        def turn_out(b):
            a = att_ready[b]
            if bv is not None:
                bvb = bv_sb.rearrange("p (o n) -> p o n", o=1).to_broadcast([P, 2, D])
                a = dve.do(lambda e: e.tensor_tensor(att[:, 2 * b:2 * b + 2, :],
                                                     att[:, 2 * b:2 * b + 2, :], bvb, ALU.add),
                           a, c.wo_ready)
            _, users = pj_ring.take()
            for k in range(KC):
                for q in range(2):
                    j = 2 * k + q
                    tr = pe.do(lambda e, j=j, k=k, q=q: e.transpose(
                        pj[:, j * P:(j + 1) * P], att[:, 2 * b + q, k * P:(k + 1) * P],
                        c.ident[:, :]), a, users, count=(j == 3))
            a = act.do(lambda e: e.activation(
                at[:, :, b * S:(b + 1) * S], pj[:, :].rearrange("p (k s) -> p k s", k=KC), ACT.Copy),
                tr, c.wo_ready)
            pj_ring.used(0, a)
            att_ready[b] = a

        def project_out(b):
            _, users = pj_ring.take()
            for q in range(2):
                t = 2 * b + q
                mm = matmuls(c, pj[:, q * D:(q + 1) * D],
                             [(at[:, k, t * P:(t + 1) * P], wo_sb[:, k, :]) for k in range(KC)],
                             att_ready[b], c.wo_ready, users)
            x2 = c.x[:, 2 * b:2 * b + 2, :]
            bob = bo_sb.rearrange("p (o n) -> p o n", o=1).to_broadcast([P, 2, D])
            a = dve.do(lambda e: e.tensor_tensor(x2, x2, pj[:, :].rearrange("p (q n) -> p q n", q=2),
                                                 ALU.add), mm)
            pj_ring.used(0, a)
            a = dve.do(lambda e: e.tensor_tensor(x2, x2, bob, ALU.add), a, c.wo_ready)
            token_stats(c, (2 * b, 2 * b + 1), a)
            return a

        c.m_part_users, c.pv_users = {}, []
        combining = iter(())
        for w in range(-1, ITEMS):
            fill, top, run = w + 2, w + 1, w
            pending = None
            if fill == ITEMS:
                load_out()
            for s in range(SLOTS):
                g, kt = divmod(s, KT)
                unit = None
                if run == ITEMS - 1 and s % 8 == 5 and s // 8 < B - 1:
                    turn_out(s // 8)
                elif run == ITEMS - 1 and s % 8 == 7 and s // 8 < B - 1:
                    project_out(s // 8)
                if run >= 0:
                    unit = scores(run, g, kt)
                if 0 <= top < ITEMS:
                    block_max(top, s // 2, s % 2)
                if fill < ITEMS:
                    fill_step(fill, s)
                if run >= 0 and pending is not None:
                    weigh(pending)
                pending = unit
                if kt == 2 and 0 <= QUADS * run + g - 1:
                    gather(*divmod(QUADS * run + g - 1, QUADS))
                if kt == 3 and 0 <= QUADS * top + g - 1 < QUADS * ITEMS:
                    place_max_rows(*divmod(QUADS * top + g - 1, QUADS))
                if kt == KT - 1 and 0 <= top < ITEMS:
                    place_max(top, g)
                if s == 3 and run > 0 and run % NKB == 0:
                    combining = combine(run // NKB - 1)
                next(combining, None)
            if run >= 0:
                weigh(pending)
        gather(ITEMS - 1, QUADS - 1)
        for _ in combine(B - 1):
            pass
        turn_out(B - 1)
        c.x_ready = project_out(B - 1)


def self_attention(c, name, sb, ps_s, ps_t, ps_o, rings, q_of, k_of, v_of, mask, scale, at_once,
                   emit, ready, v_ready, extra, batches=range(B), scale_of=None, rounds=1, skip=0):
    pe, act, dve, pool, sp = c.lanes
    s_ring, t_ring, o_ring, p_ring, pt_ring, st_ring = rings
    p_sb, pt_sb, stat = sb
    KEYS = (P, 2 * P - skip)
    FIRST = (0, skip)
    OFF = (0, P)
    width = sum(KEYS)
    BLOCKS = ((slice(0, P), slice(0, P), slice(0, P)),
              (slice(P, 2 * P - skip), slice(skip, P), slice(P, 2 * P)),
              (slice(2 * P - skip, width), slice(0, P), slice(2 * P, 3 * P)))
    step = P // at_once
    o = None

    def front(b, h):
        p, pusers = p_ring.take()
        st, stusers = st_ring.take()
        t3 = stat[:, st, :, :]
        s, susers = s_ring.take()
        pe.do(lambda e: e.matmul(ps_s[s][:, 0:width], c.ident_bf[:, :], mask[:, :], start=True,
                                 stop=False), extra, susers, count=False)
        for q in range(2):
            ql, kr = q_of(b, h, q), k_of(b, h, FIRST[q], KEYS[q])
            mm = pe.do(lambda e, q=q, ql=ql, kr=kr: e.matmul(
                ps_s[s][:, OFF[q]:OFF[q] + KEYS[q]], ql, kr, start=False, stop=(q == 1)),
                ready, count=(q == 1))
        sv = p_sb[:, p, 0:width]
        for q in range(2):
            m = dve.do(lambda e, q=q: e.tensor_reduce(
                t3[:, 0, q:q + 1], ps_s[s][:, OFF[q]:OFF[q] + KEYS[q]], AX.X, ALU.max), mm, stusers)
        if scale_of is not None:
            m = dve.do(lambda e: e.scalar_tensor_tensor(
                t3[:, 1, :], t3[:, 0, :], -1.0, scale_of(h, slice(0, 2)), ALU.mult, ALU.mult), m)
        else:
            m = dve.do(lambda e: e.tensor_scalar(t3[:, 1, :], t3[:, 0, :], -scale, None, ALU.mult), m)
        for q in range(2):
            x = act.do(lambda e, q=q: e.activation(
                sv[:, OFF[q]:OFF[q] + KEYS[q]], ps_s[s][:, OFF[q]:OFF[q] + KEYS[q]], ACT.Exp,
                bias=t3[:, 1, q:q + 1],
                scale=scale if scale_of is None else scale_of(h, slice(q, q + 1)),
                accum_out=t3[:, 2, q:q + 1]), m, pusers)
        s_ring.used(s, x)
        return p, st, x

    def divide(p, st, x):
        sv, t3 = p_sb[:, p, :], stat[:, st, :, :]
        m = dve.do(lambda e: e.reciprocal(t3[:, 3, :], t3[:, 2, :]), x)
        n = [lane.do(lambda e, q=q: e.tensor_scalar(
            sv[:, OFF[q]:OFF[q] + KEYS[q]], sv[:, OFF[q]:OFF[q] + KEYS[q]],
            t3[:, 3, q:q + 1], None, ALU.mult), m) for q, lane in ((0, dve), (1, pool))]
        st_ring.used(st, n)
        return p, n

    def back(b, h, p, n):
        t, tusers = t_ring.take()
        for j, (cols, rows, to) in enumerate(BLOCKS):
            tr = pe.do(lambda e, cols=cols, rows=rows, to=to: (
                e.matmul(ps_t[t][rows, to], p_sb[:, p, cols], c.ident[:, :], start=True, stop=True)
                if rows.start else e.transpose(ps_t[t][rows, to], p_sb[:, p, cols], c.ident[:, :])),
                n, tusers, count=(j == 2))
        p_ring.used(p, tr)
        pt, ptusers = pt_ring.take()
        ev = act.do(lambda e: e.activation(pt_sb[:, pt, :], ps_t[t][:, 0:3 * P], ACT.Copy), tr, ptusers)
        t_ring.used(t, ev)
        return pt, ev

    def apply(b, heads, round_):
        nonlocal o
        g = heads[0][0] // (at_once * rounds)
        if round_ == 0:
            o = o_ring.take()
        bank, users = o
        for first, cols, keys, n in ((True, slice(0, 2 * P), slice(0, 2 * P), 0),
                                     (False, slice(P, 2 * P), slice(2 * P, 3 * P), 1)):
            for j, (h, pt, ev) in enumerate(heads):
                rows = slice(step * j, step * j + step)
                mm = pe.do(lambda e, rows=rows, pt=pt, h=h, first=first, cols=cols, keys=keys, n=n:
                           e.matmul(ps_o[bank][rows, cols], v_of(b, n, h), pt_sb[:, pt, keys],
                                    start=first and round_ == 0, stop=not first and round_ == rounds - 1),
                           ev, v_ready, users, count=(not first and j == at_once - 1))
        for h, pt, ev in heads:
            pt_ring.used(pt, mm)
        if round_ == rounds - 1:
            o_ring.used(bank, emit(b, g, ps_o[bank], mm))

    todo = [(b, h) for b in batches for h in range(H)]
    fronts, full = {}, []
    LAG = 3

    def apply_full(heads):
        apply(heads[0][0], [x[1:] for x in heads], heads[0][1] // at_once % rounds)
    for i in range(len(todo) + LAG + 1):
        if i < len(todo):
            fronts[i] = front(*todo[i])
        if 0 <= i - 1 < len(todo):
            fronts[i - 1] = divide(*fronts[i - 1])
        if 0 <= i - LAG < len(todo):
            if len(full) == at_once + 1:
                apply_full(full[:-1])
                full = full[-1:]
            b, h = todo[i - LAG]
            full.append((b, h, *back(b, h, *fronts[i - LAG])))
        if i == len(todo) + LAG:
            apply_full(full)
        yield


def run(*jobs):
    jobs = list(jobs)
    while jobs:
        jobs = [j for j in jobs if next(j, "end") != "end"]


def alternate(*jobs):
    jobs = list(jobs)
    while jobs:
        for job in list(jobs):
            if next(job, "end") == "end":
                jobs.remove(job)
            else:
                yield


def run_even(*jobs):
    ticks = max(steps for _, steps, _ in jobs)
    taken = [0] * len(jobs)
    for tick in range(ticks):
        for n, (job, steps, late) in enumerate(jobs):
            start = late * ticks
            due = steps * (tick + 1 - start) / (ticks - start)
            while taken[n] < due:
                next(job, None)
                taken[n] += 1
    run(*[job for job, _, _ in jobs])


def load_mask(c, mask, src, asb, slot):
    stage = asb[0][:, 0, 0:mask.shape[1]]
    m = c.sp.dma(slot, stage, src)
    return [c.dve.do(lambda e: e.tensor_copy(mask[:, :], stage), m), c.ident_ready]


def attention_buffers(c, name, ctx, n_pt):
    nc = c.nc
    sb = (ctx.enter_context(nc.sbuf_tensor(f"{name}_p", [P, 5, 3 * P], F32)),
          ctx.enter_context(nc.sbuf_tensor(f"{name}_pt", [P, n_pt, 3 * P], F32)),
          ctx.enter_context(nc.sbuf_tensor(f"{name}_stat", [P, 5, 4, 2], F32)))
    return sb


def conv_attention(c, name, g):
    nc = c.nc
    c.stage(name)
    pe, act, dve, pool, sp = c.lanes
    GH = 8
    G = H // GH
    STRIPS = 4
    SW = P // STRIPS
    DH = D // H
    with ExitStack() as ctx:
        def sb(n, shape, dt=F32):
            return ctx.enter_context(nc.sbuf_tensor(f"{name}_{n}", shape, dt))
        wq, wk, wo = (sb(n, [P, KC, D]) for n in ("wq", "wk", "wo"))
        wv = sb("wv", [P, KC, H * SW])
        cw = sb("cw", [P, 3, G, D])
        cols = sb("cols", [P, 5, G])
        own = sb("own", [P, 2])
        bv, bo = sb("bv", [P, H * SW]), sb("bo", [P, D])
        mask = sb("mask", [P, 3 * P], BF16)
        xn, xt = sb("xn", [P, NT, D]), sb("xt", [P, KC, N])
        q, k = sb("q", [P, GH, G, N]), sb("k", [P, G, N])
        v = sb("v", [P, NT, H * SW])
        cc = sb("cc", [P, G, B, S + 2])
        asb = attention_buffers(c, name, ctx, 6)
        banks = [ctx.enter_context(nc.psum_tensor(f"{name}_bank{i}", [P, 512], F32)) for i in range(8)]
        slot = c.slot(f"{name}_w")
        for dst, src in ((wq, "ca_wq"), (wk, "ca_wk"), (wv, "ca_wv"), (wo, "ca_wo")):
            w = sp.dma(slot, dst[:, :, :], g(src).rearrange("(k p) n -> p k n", p=P))
        w = sp.dma(slot, cols[:, :, :], g("ca_cols").rearrange("p (a b) -> p a b", a=5))
        for dst, src in ((own, "ca_own"), (bv, "ca_bv"), (bo, "ca_bo")):
            w = sp.dma(slot, dst[:, :], g(src))
        slot2 = c.slot(f"{name}_cw")
        cw_mark = sp.dma(slot2, cw[:, :, :, :], g("ca_cw").rearrange("t (k p) n -> p t k n", p=P))
        zero = [pool.do(lambda e, b=b: e.memset(cc[:, :, :, b:b + 1], 0.0)) for b in (0, S + 1)]
        zero_src = (c.ident[:, :].rearrange("p (o n) -> p o n", o=1).to_broadcast([P, 6 * G * N // P, P]))
        q_zero = [pool.do(lambda e: e.memset(q[:, 0:2, :, :], 0.0), zero),
                  act.do(lambda e: e.activation(
                      q[:, 2:8, :, :].rearrange("p h g (a n) -> p (h g a) n", n=P), zero_src,
                      ACT.Copy, scale=0.0), c.ident_ready)]

        def spread(gr, b, cols_, bank_cols, bias, mm):
            marks = []
            for h in range(GH):
                second, j = divmod(h, STRIPS)
                rows = slice(SW * j, SW * j + SW)
                o, src = q[rows, h, gr, cols_], banks[b][rows, bank_cols]
                bi, ow = cols[rows, bias + second, gr:gr + 1], own[rows, second:second + 1]
                if j < 2:
                    marks.append(act.do(lambda e, o=o, src=src, bi=bi, ow=ow: e.activation(
                        o, src, ACT.Identity, bias=bi, scale=ow), mm, q_zero))
                else:
                    marks.append(dve.do(lambda e, o=o, src=src, bi=bi, ow=ow: e.tensor_scalar(
                        o, src, ow, bi, ALU.mult, ALU.add), mm, q_zero))
            return marks
        ring = Ring(8)
        normed = layernorm(c, xn)
        xr = to_features(c, xn, xt, normed, banks, ring)
        masked = load_mask(c, mask, g("causal"), asb, c.slot(f"{name}_mask"))

        q_ready, k_ready, v_ready = [], [], []
        for gr in range(G):
            for half in range(2):
                tokens = slice(half * 512, (half + 1) * 512)
                b, users = ring.take()
                mm = matmuls(c, banks[b][:, :], [
                    (wq[:, i, gr * P:(gr + 1) * P], xt[:, i, tokens]) for i in range(KC)], xr, w, users)
                a = spread(gr, b, tokens, slice(0, 512), 1, mm)
                ring.used(b, a)
                q_ready += a
                b, users = ring.take()
                mm = matmuls(c, banks[b][:, :], [
                    (wk[:, i, gr * P:(gr + 1) * P], xt[:, i, tokens]) for i in range(KC)], users)
                a = dve.do(lambda e, b=b, gr=gr, tokens=tokens: e.tensor_scalar(
                    k[:, gr, tokens], banks[b][:, :], cols[:, 0, gr:gr + 1], None, ALU.add), mm)
                ring.used(b, a)
                k_ready.append(a)
        for t in range(NT):
            b, users = ring.take()
            mm = matmuls(c, banks[b][:, :], [(xt[:, i, t * P:(t + 1) * P], wv[:, i, :])
                                             for i in range(KC)], users)
            a = dve.do(lambda e, t=t, b=b: e.tensor_tensor(v[:, t, :], banks[b][:, :], bv[:, :],
                                                           ALU.add), mm)
            ring.used(b, a)
            v_ready.append(a)

        free = [Ring(3), Ring(2), Ring(1), Ring(5), Ring(6), Ring(5)]
        s_banks, t_banks, o_banks = (0, 1, 4), (2, 3), (5,)
        for r, numbers in ((free[0], s_banks), (free[1], t_banks), (free[2], o_banks)):
            for i, number in enumerate(numbers):
                r.used(i, ring.users[number])
        ring.users[0:6] = [[] for _ in range(6)]

        def q_of(b, h, qt):
            gr, j = divmod(h, GH)
            return q[:, j, gr, b * S + qt * P:b * S + (qt + 1) * P]

        def k_of(b, h, first, n):
            return k[:, h // GH, b * S + first:b * S + first + n]

        def v_of(b, kt, h):
            return v[:, 2 * b + kt, SW * h:SW * (h + 1)]

        def attend(emitted, queries, *waits):
            def keep(b, gr, bank, mm):
                a = act.do(lambda e: e.activation(cc[:, gr, b, 1:S + 1], bank[:, 0:S], ACT.Copy),
                           mm, waits)
                emitted.append(a)
                return a
            s, t, o = ([banks[i] for i in numbers] for numbers in (s_banks, t_banks, o_banks))
            run(self_attention(c, name, asb, s, t, o, free, q_of, k_of,
                               v_of, mask, 1.0 / float(np.sqrt(DH)), STRIPS, keep,
                               [queries, k_ready], v_ready, masked, rounds=GH // STRIPS))
        conv_in = []
        attend(conv_in, q_ready)
        q2 = []
        for gr in range(G):
            for b in range(B):
                i = 6 + b % 2
                users, ring.users[i] = ring.users[i], []
                pairs = [(cw[:, t, kk, gr * P:(gr + 1) * P], cc[:, kk, b, t:t + S])
                         for t in range(3) for kk in range(G)]
                mm = matmuls(c, banks[i][:, 0:S], pairs, conv_in, zero, cw_mark, users)
                a = spread(gr, i, slice(b * S, (b + 1) * S), slice(0, S), 3, mm)
                ring.users[i] = a
                q2 += a
        ctx2 = []
        attend(ctx2, q2, q2)
        for t in range(NT):
            b, qt = divmod(t, 2)
            i = 6 + t % 2
            users, ring.users[i] = ring.users[i], []
            mm = matmuls(c, banks[i][:, 0:D],
                         [(cc[:, kk, b, 1 + qt * P:1 + (qt + 1) * P], wo[:, kk, :]) for kk in range(G)],
                         ctx2, users)
            a = dve.do(lambda e, t=t, i=i: e.tensor_tensor(c.x[:, t, :], c.x[:, t, :],
                                                           banks[i][:, 0:D], ALU.add), mm)
            ring.users[i] = [a]
            last = dve.do(lambda e, t=t: e.tensor_tensor(c.x[:, t, :], c.x[:, t, :], bo[:, :],
                                                         ALU.add), a)
            token_stats(c, (t,), last)
        c.x_ready = last


DEPTH = 6
WINDOW = 64
LH = 64
INNER = H * LH
FF = int(D * 4 * 2 / 3)
FC = -(-FF // P)
FFP = FC * P


def local_transformer(c, name, g):
    nc = c.nc
    c.stage(name)
    pe, act, dve, pool, sp = c.lanes
    HP = H // 2
    with ExitStack() as ctx:
        def sb(n, shape, dt=F32):
            return ctx.enter_context(nc.sbuf_tensor(f"{name}_{n}", shape, dt))
        y = c.x
        parked = []
        for b in range(B):
            tiles = slice(2 * b, 2 * b + 2)
            parked.append(sp.dma(c.slot(f"{name}_park{b}"), c.parked[:, tiles, :], c.x[:, tiles, :],
                                 c.x_ready))
        wqk = sb("wqk", [P, 2, KC, 2 * INNER])
        wval = sb("wval", [P, KC, INNER])
        wo, w1, w2 = sb("wo", [P, HP, D]), sb("w1", [P, KC, 2 * FFP]), sb("w2", [P, FC, D])
        scl = sb("scl", [P, 2, 4, LH])
        rot = sb("rot", [P, 4, 2, LH])
        tab = sb("tab", [P, 2, 4, 2, LH])
        b2, ffc, lnc = sb("b2", [P, 2, D]), sb("ffc", [P, DEPTH, 2, FC]), sb("lnc", [P, DEPTH, 2, KC])
        mask = sb("mask", [P, 3 * P - WINDOW], BF16)
        xs, xt = sb("xs", [P, 2, 2, P]), sb("xt", [P, 2, KC, S])
        r_qk = sb("r_qk", [P, 2, INNER])
        t_sq = sb("t_sq", [P, 2, 512])
        t_rot = sb("t_rot", [P, 2, 512])
        nrm = sb("nrm", [P, 2, 3, H])
        rq = sb("rq", [P, 2, 2, H])
        q_even, q_odd = sb("q_even", [P, 2, HP, S]), sb("q_odd", [P, 2, HP, S])
        kt = sb("kt", [P, 2, HP, S])
        v = sb("v", [P, 2, 2, INNER])
        ot = sb("ot", [P, HP, S])
        fs, ft = sb("fs", [P, 2, D]), sb("ft", [P, KC, S])
        fst, fmv, frs = sb("fst", [P, 2, 6]), sb("fmv", [P, 2, 2]), sb("frs", [P, 2, 2])
        gl, u = sb("gl", [P, 2, S]), sb("u", [P, FC, S])
        asb = attention_buffers(c, name, ctx, 4)
        banks = [ctx.enter_context(nc.psum_tensor(f"{name}_bank{i}", [P, 512], F32)) for i in range(8)]
        arings = [Ring(2), Ring(2), Ring(1), Ring(5), Ring(4), Ring(5)]
        gen = Ring(3)
        r_ring, t_ring, n_ring = Ring(2), Ring(2), Ring(2)
        gl_ring = Ring(2)

        slot = c.slot(f"{name}_small")
        small = sp.dma(slot, rot[:, :, :, :], g("lt_rot").rearrange("p (a b c) -> p a b c", a=4, b=2))
        small = sp.dma(slot, ffc[:, :, :, :], g("lt_ffc").rearrange("p (a b c) -> p a b c", a=DEPTH, b=2))
        small = sp.dma(slot, lnc[:, :, :, :], g("lt_lnc").rearrange("p (a b c) -> p a b c", a=DEPTH, b=2))
        zeros = [pool.do(lambda e: e.memset(xs[0:1, :, 0, :], 0.0))]
        zeros.append(pool.do(lambda e: e.memset(q_even[64:128, :, :, :], 0.0), zeros[0]))
        zeros.append(pool.do(lambda e: e.memset(q_odd[0:64, :, :, :], 0.0), zeros[1]))
        normed = layernorm(c, y, by_tile=[parked[t // 2] for t in range(NT)])
        y_ready = {b: [normed[2 * b], normed[2 * b + 1]] for b in range(B)}

        wq_slot = [c.slot(f"{name}_wqkv{i}") for i in range(2)]
        wb_slot = [c.slot(f"{name}_w{n}") for n in ("o", "1", "2")]
        xs_slot = [c.slot(f"{name}_xs{i}") for i in range(2)]
        fs_slot = c.slot(f"{name}_fs")
        wv_slot = c.slot(f"{name}_wval")
        wval_ready, wval_users = {}, {l: [] for l in range(-1, DEPTH)}
        wqkv_ready, wqkv_users = {}, {l: [] for l in range(-2, DEPTH)}
        wb_ready, wb_users = {}, {l: [[], [], []] for l in range(-1, DEPTH)}
        tab_ready, tab_users = {}, {l: [] for l in range(-2, DEPTH)}
        b2_users = {l: [] for l in range(-2, DEPTH)}
        par_users = {}
        ot_users, fs_users, ft_users, u_users = [[]], [[]], [[]], [[]]

        def load_values(l):
            w = g("lt_wqkv")[l].rearrange("(k p) n -> p k n", p=P)
            wval_ready[l] = sp.dma(wv_slot, wval[:, :, :], w[:, :, 2 * INNER:], wval_users[l - 1])

        def load_front(l):
            i = l % 2
            w = g("lt_wqkv")[l].rearrange("(k p) n -> p k n", p=P)
            sp.dma(wq_slot[i], scl[:, i, :, :], g("lt_scl")[l].rearrange("p (a b) -> p a b", a=4),
                   tab_users[l - 2])
            sp.dma(wq_slot[i], b2[:, i, :], g("lt_b2")[l], b2_users[l - 2])
            wqkv_ready[l] = sp.dma(wq_slot[i], wqk[:, i, :, :], w[:, :, 0:2 * INNER], wqkv_users[l - 2])

        def tables(l):
            i = l % 2
            for tile in range(2):
                a = dve.do(lambda e, tile=tile: e.tensor_tensor(
                    tab[:, i, :, tile, :], rot[:, :, tile, :], scl[:, i, :, :], ALU.mult),
                    wqkv_ready[l], small, tab_users[l - 2])
            tab_ready[l] = a

        def load_back(l, n):
            dst = (wo, w1, w2)[n]
            src = (g("lt_wo"), g("lt_w1"), g("lt_w2"))[n]
            wb_ready[l, n] = sp.dma(wb_slot[n], dst[:, :, :], src[l].rearrange("(k p) n -> p k n", p=P),
                                    wb_users[l - 1][n])

        def shift(dst, slot_, b, cols, *waits):
            sp.dma(slot_, dst[1:P, :, cols], y[0:P - 1, 2 * b:2 * b + 2, P:D], waits)
            return sp.dma(slot_, dst[0:1, 1, cols], y[P - 1:P, 2 * b, P:D])

        def shift_ahead(l, b):
            par = (l * B + b) % 2
            xs_ready[l, b] = shift(xs[:, par, :, :], xs_slot[par], b, slice(0, P), y_ready[b],
                                   zeros, xs_users[par])

        def features(l, b):
            par = (l * B + b) % 2
            i, users = gen.take()
            for k in range(KC):
                for q in range(2):
                    src = y[:, 2 * b + q, 0:P] if k == 0 else xs[:, par, q, :]
                    tr = pe.do(lambda e, k=k, q=q, src=src: e.transpose(
                        banks[5 + i][:, (2 * k + q) * P:(2 * k + q + 1) * P], src, c.ident[:, :]),
                        xs_ready[l, b], y_ready[b], users, count=(k + q == 2))
            a = act.do(lambda e: e.activation(
                xt[:, par, :, :], banks[5 + i][:, :].rearrange("p (k s) -> p k s", k=KC), ACT.Copy), tr)
            gen.used(i, a)
            xs_users[par] = tr
            xt_ready[l, b] = a
            if l == 0 and b + 2 < B:
                shift_ahead(0, b + 2)

        def front(l, b):
            par, lp = (l * B + b) % 2, l % 2
            prev = par_users.get((l * B + b) - 2, [])
            if b == 2 and l + 1 < DEPTH:
                load_front(l + 1)
            if b == 3 and l + 1 < DEPTH:
                tables(l + 1)
            x_mark = xt_ready[l, b]
            done_k, done_q, done_v = [], [], []
            yield

            def project(tile, sec):
                r, rusers = r_ring.take()
                n, nusers = n_ring.take()
                parts = []
                for half in range(2):
                    i, users = gen.take()
                    col = sec * INNER + half * 512
                    mm = matmuls(c, banks[5 + i][:, :], [
                        (xt[:, par, k, tile * P:(tile + 1) * P], wqk[:, lp, k, col:col + 512])
                        for k in range(KC)], x_mark, wqkv_ready[l], users)
                    wqkv_users[l].append(mm)
                    t, tusers = t_ring.take()
                    p3 = banks[5 + i][:, :].rearrange("p (h d) -> p h d", d=LH)
                    sq3 = t_sq[:, t, :].rearrange("p (h d) -> p h d", d=LH)
                    ro3 = t_rot[:, t, :].rearrange("p (h d) -> p h d", d=LH)
                    out3 = r_qk[:, r, half * 512:(half + 1) * 512].rearrange("p (h d) -> p h d", d=LH)

                    def table(j, lo, hi):
                        return (tab[:, lp, 2 * sec + j, tile:tile + 1, lo:hi]
                                .to_broadcast([P, 8, hi - lo]))
                    c1 = dve.do(lambda e, out3=out3, p3=p3, tb=table(0, 0, LH): e.tensor_tensor(
                        out3, p3, tb, ALU.mult), mm, rusers, tab_ready[l])
                    dve.do(lambda e, ro3=ro3, p3=p3, tb=table(1, 0, 32): e.tensor_tensor(
                        ro3[:, :, 0:32], p3[:, :, 32:64], tb, ALU.mult), tusers)
                    c2 = dve.do(lambda e, ro3=ro3, p3=p3, tb=table(1, 32, 64): e.tensor_tensor(
                        ro3[:, :, 32:64], p3[:, :, 0:32], tb, ALU.mult))
                    a = act.do(lambda e, sq3=sq3, p3=p3: e.activation(sq3, p3, ACT.Square), c2, tusers)
                    gen.used(i, a)
                    c3 = pool.do(lambda e, out3=out3, ro3=ro3: e.tensor_tensor(
                        out3, out3, ro3, ALU.add), c1, c2)
                    parts.append(c3)
                    yield
                    s_ = dve.do(lambda e, half=half, sq3=sq3: e.tensor_reduce(
                        nrm[:, n, 0, half * 8:half * 8 + 8], sq3, AX.X, ALU.add), a, nusers)
                    parts.append(s_)
                    t_ring.used(t, s_, c3)
                f = dve.do(lambda e: e.tensor_scalar(nrm[:, n, 1, :], nrm[:, n, 0, :], 1e-24,
                                                     None, ALU.max), parts)
                f = rsqrt(c, nrm[:, n, 2, :], nrm[:, n, 1, :], H, f)
                if sec == 0:
                    f = pool.do(lambda e: e.tensor_scalar(
                        rq[:, par, tile, :], nrm[:, n, 2, :], 8.0, None, ALU.mult), f, prev)
                    done_q.append(f)
                    n_ring.used(n, f)
                projected[tile, sec] = r, n, f, parts

            def normalise(tile):
                r, n, f, parts = projected[tile, 1]
                full = r_qk[:, r, :].rearrange("p (h d) -> p h d", d=LH)
                nb = nrm[:, n, 2, :].rearrange("p (h o) -> p h o", o=1).to_broadcast([P, H, LH])
                f = dve.do(lambda e: e.tensor_tensor(full, full, nb, ALU.mult), f)
                n_ring.used(n, f)
                parts.append(f)

            def turn(tile, sec):
                r, _, _, parts = projected[tile, sec]
                for half in range(2):
                    i, users = gen.take()
                    for j in range(4):
                        hp = 4 * half + j
                        tr = pe.do(lambda e, i=i, j=j, hp=hp: e.transpose(
                            banks[5 + i][:, j * P:(j + 1) * P], r_qk[:, r, hp * P:(hp + 1) * P],
                            c.ident[:, :]), parts, users, count=(j == 3))
                    src = banks[5 + i][:, :].rearrange("p (j t) -> p j t", j=4)
                    hs, ts = slice(4 * half, 4 * half + 4), slice(tile * P, (tile + 1) * P)
                    if sec == 0:
                        a = act.do(lambda e, src=src, hs=hs, ts=ts: e.activation(
                            q_even[0:64, par, hs, ts], src[0:64, :, :], ACT.Copy), tr, prev)
                        a2 = act.do(lambda e, src=src, hs=hs, ts=ts: e.activation(
                            q_odd[64:128, par, hs, ts], src[64:128, :, :], ACT.Copy), tr, prev)
                        done_q.extend([a, a2])
                        gen.used(i, a, a2)
                    else:
                        a = act.do(lambda e, src=src, hs=hs, ts=ts: e.activation(
                            kt[:, par, hs, ts], src, ACT.Copy), tr, prev)
                        done_k.append(a)
                        gen.used(i, a)
                    r_ring.used(r, tr)
                    yield

            def values(tile):
                for half in range(2):
                    i, users = gen.take()
                    col = half * 512
                    mm = matmuls(c, banks[5 + i][:, :], [
                        (xt[:, par, k, tile * P:(tile + 1) * P], wval[:, k, col:col + 512])
                        for k in range(KC)], x_mark, wval_ready[l], users)
                    wval_users[l].append(mm)
                    a = act.do(lambda e, i=i, half=half: e.activation(
                        v[:, par, tile, half * 512:(half + 1) * 512], banks[5 + i][:, :], ACT.Copy),
                        mm, prev)
                    gen.used(i, a)
                    done_v.append(a)
                    yield
            projected = {}
            yield from project(0, 0)
            yield from alternate(project(0, 1), values(0))
            yield from turn(0, 0)
            normalise(0)
            yield from alternate(project(1, 0), turn(0, 1))
            yield from project(1, 1)
            yield from alternate(turn(1, 0), values(1))
            if b == B - 1 and l + 1 < DEPTH:
                load_values(l + 1)
            normalise(1)
            yield
            if (l, b) != jobs[-1]:
                features(*jobs[l * B + b + 1])
            yield from turn(1, 1)
            parts = projected[1, 1][3]
            tab_users[l].append(done_k[-1])
            tab_users[l] += parts
            ready[l * B + b] = ([done_q, done_k], done_v)

        def back(l, b):
            par = (l * B + b) % 2
            qk_ready, v_ready = ready[l * B + b]
            emitted = []

            def keep(b_, gr, bank, mm):
                a = act.do(lambda e: e.activation(ot[:, gr, :], bank[:, 0:S], ACT.Copy), mm, ot_users[0])
                emitted.append(a)
                return a

            def q_of(b_, h, qt):
                q = q_odd if h % 2 else q_even
                return q[:, par, h // 2, qt * P:(qt + 1) * P]
            yield from self_attention(
                c, name, asb, banks[0:2], banks[2:4], banks[4:5], arings, q_of,
                lambda b_, h, first, n: kt[:, par, h // 2, first:first + n],
                lambda b_, t, h: v[:, par, t, h * LH:(h + 1) * LH],
                mask, 8.0, 2, keep, [qk_ready, zeros], v_ready, masked, batches=[b],
                scale_of=lambda h, q: rq[:, par, q, h], skip=WINDOW)
            par_users[l * B + b] = [emitted, pe.last(), dve.last(), act.last()]
            m = []
            for tile in range(2):
                t = 2 * b + tile
                i, users = gen.take()
                mm = matmuls(c, banks[5 + i][:, 0:D], [
                    (ot[:, k, tile * P:(tile + 1) * P], wo[:, k, :]) for k in range(HP)],
                    emitted, wb_ready[l, 0], users)
                a = dve.do(lambda e, t=t, i=i: e.tensor_tensor(y[:, t, :], y[:, t, :],
                                                               banks[5 + i][:, 0:D], ALU.add), mm)
                gen.used(i, a)
                m.append(a)
                yield
            ot_users[0] = [mm]
            wb_users[l][0] = [mm]
            if b == B - 1 and l + 1 < DEPTH:
                load_back(l + 1, 0)
            y_ready[b] = m

        def gated(l, b):
            sp.dma(fs_slot, fs[:, :, 0:P], y[:, 2 * b:2 * b + 2, 0:P], y_ready[b], fs_users[0])
            f = [shift(fs, fs_slot, b, slice(P, D)),
                 dve.do(lambda e: e.memset(fs[0:1, 0, P:D], 0.0), fs_users[0])]
            yield
            yield
            yield
            for q in range(2):
                a = dve.do(lambda e, q=q: e.bn_stats(fst[:, q, :], fs[:, q, :]), f)
                a = dve.do(lambda e, q=q: e.bn_aggr(fmv[:, q, :], fst[:, q, :]), a)
            a = dve.do(lambda e: e.tensor_scalar(frs[:, 0, :], fmv[:, :, 1], LN_EPS, None, ALU.add), a)
            a = rsqrt(c, frs[:, 1, :], frs[:, 0, :], 2, a)
            yield
            yield
            n = []
            for q in range(2):
                n.append(dve.do(lambda e, q=q: e.tensor_scalar(
                    fs[:, q, :], fs[:, q, :], fmv[:, q, 0:1], frs[:, 1, q:q + 1],
                    ALU.subtract, ALU.mult), a))
            yield
            i, users = gen.take()
            for k in range(KC):
                for q in range(2):
                    tr = pe.do(lambda e, k=k, q=q, i=i: e.transpose(
                        banks[5 + i][:, (2 * k + q) * P:(2 * k + q + 1) * P],
                        fs[:, q, k * P:(k + 1) * P], c.ident[:, :]), n, users, count=(k + q == 2))
            fs_users[0] = [tr]
            fx = []
            for k in range(KC):
                fx.append(dve.do(lambda e, k=k, i=i: e.tensor_scalar(
                    ft[:, k, :], banks[5 + i][:, k * S:(k + 1) * S], lnc[:, l, 0, k:k + 1],
                    lnc[:, l, 1, k:k + 1], ALU.mult, ALU.add), tr, small, ft_users[0]))
            gen.used(i, fx)
            yield
            ud = []
            for mc in range(0, FC, 2):
                got = []
                for m_ in (mc, mc + 1):
                    i, users = gen.take()
                    matmuls(c, banks[5 + i][:, S:2 * S], [
                        (w1[:, k, FFP + m_ * P:FFP + (m_ + 1) * P], ft[:, k, :]) for k in range(KC)],
                        fx, wb_ready[l, 1], users)
                    mm = matmuls(c, banks[5 + i][:, 0:S], [
                        (w1[:, k, m_ * P:(m_ + 1) * P], ft[:, k, :]) for k in range(KC)])
                    got.append((m_, i, mm))
                for n_, (m_, i, mm) in enumerate(got):
                    j, jusers = gl_ring.take()
                    a = act.do(lambda e, i=i, j=j, m_=m_: e.activation(
                        gl[:, j, :], banks[5 + i][:, S:2 * S], ACT.Gelu, bias=ffc[:, l, 1, m_:m_ + 1]),
                        got[-1][2], jusers)
                    got[n_] = m_, i, j, a
                for m_, i, j, a in got:
                    a = dve.do(lambda e, i=i, j=j, m_=m_: e.scalar_tensor_tensor(
                        u[:, m_, :], banks[5 + i][:, 0:S], ffc[:, l, 0, m_:m_ + 1], gl[:, j, :],
                        ALU.add, ALU.mult), a, u_users[0])
                    gen.used(i, a)
                    gl_ring.used(j, a)
                    ud.append(a)
                yield
            ft_users[0] = [mm]
            wb_users[l][1] = [mm]
            if b == B - 1 and l + 1 < DEPTH:
                load_back(l + 1, 1)
            fin = []
            for tile in range(2):
                t = 2 * b + tile
                i, users = gen.take()
                mm = matmuls(c, banks[5 + i][:, 0:D], [
                    (u[:, k, tile * P:(tile + 1) * P], w2[:, k, :]) for k in range(FC)],
                    ud, wb_ready[l, 2], users)
                a = dve.do(lambda e, t=t, i=i: e.tensor_tensor(y[:, t, :], y[:, t, :],
                                                               banks[5 + i][:, 0:D], ALU.add), mm)
                gen.used(i, a)
                a = dve.do(lambda e, t=t: e.tensor_tensor(y[:, t, :], y[:, t, :], b2[:, l % 2, :],
                                                          ALU.add), a)
                fin.append(a)
                yield
            b2_users[l] = fin
            u_users[0] = [mm]
            wb_users[l][2] = [mm]
            if b == B - 1 and l + 1 < DEPTH:
                load_back(l + 1, 2)
            y_ready[b] = fin
            if l + 1 < DEPTH:
                shift_ahead(l + 1, b)

        ready, xt_ready, xs_ready, xs_users = {}, {}, {}, [None, None]
        jobs = [(l, b) for l in range(DEPTH) for b in range(B)]
        load_front(0)
        for b in range(2):
            shift_ahead(0, b)
        masked = load_mask(c, mask, g("band"), asb, c.slot(f"{name}_mask"))
        load_values(0)
        tables(0)
        zeros += [dve.do(lambda e, i=i: e.memset(banks[i][:, :], 0.0)) for i in (2, 3)]
        for n in range(3):
            load_back(0, n)
        features(0, 0)
        for n in range(len(jobs) + 2):
            run_even(*[(part(*jobs[n - lag]), steps, late) for lag, (part, steps, late) in
                       enumerate(((front, 24, 0), (back, 23, 0), (gated, 17, 0.1)))
                       if 0 <= n - lag < len(jobs)])
        back_in = sp.dma(c.slot(f"{name}_return"), ot[:, :, :], c.parked,
                         par_users[len(jobs) - 1], ot_users[0])
        for t in range(NT):
            last = dve.do(lambda e, t=t: e.tensor_tensor(y[:, t, :], y[:, t, :], ot[:, t, :],
                                                         ALU.add), y_ready[t // 2], back_in)
            token_stats(c, (t,), last)
        c.x_ready = last


DK = D // 2 // H
DV = D // H
TAPS = 4


def gated_linear_attention(c, name, g):
    nc = c.nc
    c.stage(name)
    pe, act, dve, pool, sp = c.lanes
    with ExitStack() as ctx:
        def sb(n, shape, dt=F32):
            return ctx.enter_context(nc.sbuf_tensor(f"{name}_{n}", shape, dt))
        taps = sb("taps", [P, KC, TAPS])
        w_in, w_out = sb("w_in", [P, KC, 3 * D]), sb("w_out", [P, KC, D])
        bg, aug = sb("bg", [P, D]), sb("aug", [P, P])
        xn, xt = sb("xn", [P, NT, D]), sb("xt", [P, KC, N])
        yc = sb("yc", [P, KC, N])
        q, kg, eg, kk = (sb(n, [P, NT, P]) for n in ("q", "kg", "eg", "kk"))
        v, gt = sb("v", [P, NT, D]), sb("gt", [P, NT, D])
        t1, t2 = sb("t1", [P, NT, P]), sb("t2", [P, NT, P])
        kd = sb("kd", [P, NT, P])
        cf = sb("cf", [P, NT, H])
        tv = sb("tv", [P, NT, D])
        o = sb("o", [P, NT, D])
        mu, var = sb("mu", [P, NT * H]), sb("var", [P, NT * H])
        ot = sb("ot", [P, KC, N])
        banks = [ctx.enter_context(nc.psum_tensor(f"{name}_bank{i}", [P, 512], F32)) for i in range(8)]
        ring = Ring(8)
        slot = c.slot(f"{name}_w")
        sp.dma(slot, taps[:, :, :], g("gla_taps").rearrange("p (k t) -> p k t", k=KC))
        sp.dma(slot, w_in[:, :, :], g("gla_win").rearrange("(k p) n -> p k n", p=P))
        sp.dma(slot, w_out[:, :, :], g("gla_wout").rearrange("(k p) n -> p k n", p=P))
        sp.dma(slot, bg[:, :], g("gla_bg"))
        w = sp.dma(slot, aug[:, :], g("gla_aug"))
        normed = layernorm(c, xn)
        xr = to_features(c, xn, xt, normed, banks, ring)

        yr = []
        for k in range(KC):
            a = dve.do(lambda e, k=k: e.tensor_scalar(yc[:, k, :], xt[:, k, :],
                                                      taps[:, k, TAPS - 1:TAPS], None, ALU.mult), xr, w)
            for back in range(1, TAPS):
                a = dve.do(lambda e, k=k, back=back: e.scalar_tensor_tensor(
                    yc[:, k, back * S:N], xt[:, k, 0:N - back * S], taps[:, k, TAPS - 1 - back:TAPS - back],
                    yc[:, k, back * S:N], ALU.mult, ALU.add), a)
            yr.append(act.do(lambda e, k=k: e.activation(xt[:, k, :], yc[:, k, :], ACT.Silu), a))

        qr, kr, vr, gr = [], [], [], []
        for t in range(NT):
            b, users = ring.take()
            mm = matmuls(c, banks[b][:, :], [(xt[:, k, t * P:(t + 1) * P], w_in[:, k, 0:512])
                                             for k in range(KC)], yr, users)
            a1 = dve.do(lambda e, t=t, b=b: e.tensor_copy(q[:, t, :], banks[b][:, 0:P]), mm)
            a2 = dve.do(lambda e, t=t, b=b: e.tensor_copy(kg[:, t, :], banks[b][:, P:2 * P]), mm)
            a3 = act.do(lambda e, t=t, b=b: e.activation(v[:, t, :], banks[b][:, 2 * P:], ACT.Copy), a2)
            ring.used(b, a1, a2, a3)
            b, users = ring.take()
            mm = matmuls(c, banks[b][:, 0:D], [(xt[:, k, t * P:(t + 1) * P], w_in[:, k, 512:768])
                                               for k in range(KC)], users)
            a4 = dve.do(lambda e, t=t, b=b: e.tensor_tensor(gt[:, t, :], banks[b][:, 0:D], bg[:, :],
                                                            ALU.add), mm)
            ring.used(b, a4)
            qr.append(a1), kr.append(a2), vr.append(a3), gr.append(a4)

        sg = act.do(lambda e: e.activation(gt[:, :, :], gt[:, :, :], ACT.Silu), gr)
        a = act.do(lambda e: e.activation(t1[:, :, :], kg[:, :, :], ACT.Abs), kr)
        a = act.do(lambda e: e.activation(t1[:, :, :], t1[:, :, :], ACT.Exp, scale=-1.0), a)
        a = dve.do(lambda e: e.tensor_scalar(t1[:, :, :], t1[:, :, :], 1.0, None, ALU.add), a)
        a = act.do(lambda e: e.activation(t2[:, :, :], t1[:, :, :], ACT.Ln), a)
        a = dve.do(lambda e: e.scalar_tensor_tensor(t1[:, :, :], kg[:, :, :], 0.0, t2[:, :, :],
                                                    ALU.min, ALU.subtract), a)
        er = act.do(lambda e: e.activation(eg[:, :, :], t1[:, :, :], ACT.Exp, scale=1.0 / 16.0), a)
        kr = dve.do(lambda e: e.tensor_scalar(kk[:, :, :], eg[:, :, :], -1.0, 1.0, ALU.mult, ALU.add), er)

        def steps(x, s, n):
            return x[:, 2 * s:2 * (s + n), :]

        def heads(x, width):
            return x.rearrange("p t (h d) -> p (t h) d", d=width)

        a = dve.do(lambda e: e.tensor_tensor(t2[:, :, :], q[:, :, :], kk[:, :, :], ALU.mult), qr, kr)
        augb = aug[:, :].rearrange("p (o n) -> p o n", o=1).to_broadcast([P, NT, P])
        a = dve.do(lambda e: e.tensor_tensor(t2[:, :, :], t2[:, :, :], augb, ALU.mult), a)
        a = dve.do(lambda e: e.tensor_reduce(cf[:, :, :].rearrange("p t (h o) -> p (t h) o", o=1),
                                             heads(t2[:, :, :], DK), AX.X, ALU.add), a)
        cb = cf[:, :, :].rearrange("p t (h o) -> p (t h) o", o=1).to_broadcast([P, NT * H, DV])
        a = dve.do(lambda e: e.tensor_tensor(heads(o[:, :, :], DV), heads(v[:, :, :], DV), cb, ALU.mult),
                   a, vr)
        oa = act.do(lambda e: e.activation(o[:, :, :], o[:, :, :], ACT.Sigmoid), a)
        qs = dve.do(lambda e: e.tensor_scalar(q[:, :, :], q[:, :, :], float(DK) ** -0.5, None, ALU.mult), a)
        for s in range(B):
            if s:
                dec = (steps(eg, s, 1).rearrange("p t d -> p (t d)").rearrange("p (o n) -> p o n", o=1)
                       .to_broadcast([P, s, 2 * P]))
                kds = steps(kd, 0, s).rearrange("p (s t) d -> p s (t d)", t=2)
                a = dve.do(lambda e, kds=kds, dec=dec: e.tensor_tensor(kds, kds, dec, ALU.mult), a)
            a = dve.do(lambda e, s=s: e.tensor_copy(steps(kd, s, 1), steps(kk, s, 1)), a)
            qb = (steps(q, s, 1).rearrange("p t d -> p (t d)").rearrange("p (o n) -> p o n", o=1)
                  .to_broadcast([P, s + 1, 2 * P]))
            a = dve.do(lambda e, s=s, qb=qb: e.tensor_tensor(
                steps(t1, 0, s + 1).rearrange("p (s t) d -> p s (t d)", t=2),
                steps(kd, 0, s + 1).rearrange("p (s t) d -> p s (t d)", t=2), qb, ALU.mult), a, qs)
            a = dve.do(lambda e, s=s: e.tensor_reduce(
                steps(cf, 0, s + 1).rearrange("p t (h o) -> p (t h) o", o=1),
                heads(steps(t1, 0, s + 1), DK), AX.X, ALU.add), a)
            cbs = (steps(cf, 0, s + 1).rearrange("p t (h o) -> p (t h) o", o=1)
                   .to_broadcast([P, 2 * (s + 1) * H, DV]))
            a = dve.do(lambda e, s=s, cbs=cbs: e.tensor_tensor(
                heads(steps(tv, 0, s + 1), DV), heads(steps(v, 0, s + 1), DV), cbs, ALU.mult), a)
            for j in range(s + 1):
                a = dve.do(lambda e, s=s, j=j: e.tensor_tensor(
                    steps(o, s, 1), steps(o, s, 1), steps(tv, j, 1), ALU.add), a, oa)
        oh = heads(o[:, :, :], DV)
        th = heads(tv[:, :, :], DV)

        def col(x):
            return x[:, :].rearrange("p (n o) -> p n o", o=1)
        a = dve.do(lambda e: e.tensor_reduce(col(mu), oh, AX.X, ALU.add), a)
        a = dve.do(lambda e: e.tensor_scalar(mu[:, :], mu[:, :], 1.0 / DV, None, ALU.mult), a)
        a = dve.do(lambda e: e.tensor_tensor(oh, oh, col(mu).to_broadcast([P, NT * H, DV]), ALU.subtract), a)
        a2 = act.do(lambda e: e.activation(tv[:, :, :], o[:, :, :], ACT.Square), a)
        a = dve.do(lambda e: e.tensor_reduce(col(var), th, AX.X, ALU.add), a2)
        a = dve.do(lambda e: e.tensor_scalar(var[:, :], var[:, :], 1.0 / DV, LN_EPS, ALU.mult, ALU.add), a)
        a = act.do(lambda e: e.activation(mu[:, :], var[:, :], ACT.Sqrt), a)
        a = dve.do(lambda e: e.reciprocal(var[:, :], mu[:, :]), a)
        a = dve.do(lambda e: e.tensor_tensor(oh, oh, col(var).to_broadcast([P, NT * H, DV]), ALU.mult), a)
        fin = []
        for t in range(NT):
            fin.append(dve.do(lambda e, t=t: e.tensor_tensor(o[:, t, :], o[:, t, :], gt[:, t, :],
                                                             ALU.mult), a, sg))
        orr = to_features(c, o, ot, fin, banks, ring)
        for t in range(NT):
            b, users = ring.take()
            mm = matmuls(c, banks[b][:, 0:D], [(ot[:, k, t * P:(t + 1) * P], w_out[:, k, :])
                                               for k in range(KC)], orr[t // 4], users)
            last = dve.do(lambda e, t=t, b=b: e.tensor_tensor(c.x[:, t, :], c.x[:, t, :],
                                                              banks[b][:, 0:D], ALU.add), mm)
            ring.used(b, last)
            token_stats(c, (t,), last)
        c.x_ready = last


EXPERTS, GROUPS, TOP_GROUPS, TOP = 64, 8, 4, 8
GE = EXPERTS // GROUPS
FI = 128
CAP = 256
ROUTE_SCALE = 2.5
OUT = -1e30
TAKEN = -3e38


def experts(c, name, g):
    nc = c.nc
    c.stage(name)
    pe, act, dve, pool, sp = c.lanes
    AHEAD = 9
    NW = 8
    with ExitStack() as ctx:
        def sb(n, shape, dt=F32):
            return ctx.enter_context(nc.sbuf_tensor(f"{name}_{n}", shape, dt))
        gw, gb = sb("gw", [P, KC, EXPERTS]), sb("gb", [P, EXPERTS])
        upper, ones = sb("upper", [P, P]), sb("ones", [P, P])
        xn, xt = sb("xn", [P, NT, D]), sb("xt", [P, KC, N])
        sc, sf, pick = (sb(n, [P, NT, EXPERTS]) for n in ("sc", "sf", "pick"))
        srt = sb("srt", [P, NT, GROUPS, 8])
        gs, gm, g8, v8 = (sb(n, [P, NT, 8]) for n in ("gs", "gm", "g8", "v8"))
        wt, den = sb("wt", [P, NT, EXPERTS]), sb("den", [P, 2, NT])
        wg, wu, wd = sb("wg", [P, NW, KC, FI]), sb("wu", [P, NW, KC, FI]), sb("wd", [P, NW, D])
        sg, hh = sb("sg", [P, 2, 512]), sb("hh", [P, AHEAD + 1, 512])
        banks = [ctx.enter_context(nc.psum_tensor(f"{name}_bank{i}", [P, 512], F32)) for i in range(8)]
        ring = Ring(8)
        slot = c.slot(f"{name}_w")
        w_slot = [c.slot(f"{name}_w{i}") for i in range(NW)]
        sp.dma(slot, gw[:, :, :], g("moe_gw").rearrange("(k p) n -> p k n", p=P))
        sp.dma(slot, gb[:, :], g("moe_gb"))
        w = sp.dma(slot, upper[:, :], g("upper"))
        w_ring = Ring(NW)

        def load(e_):
            i, users = w_ring.take()
            sp.dma(w_slot[i], wg[:, i, :, :], g("moe_wg")[e_].rearrange("(k p) n -> p k n", p=P), users)
            sp.dma(w_slot[i], wu[:, i, :, :], g("moe_wu")[e_].rearrange("(k p) n -> p k n", p=P))
            return i, sp.dma(w_slot[i], wd[:, i, :], g("moe_wd")[e_])
        loaded = {e_: load(e_) for e_ in range(NW)}
        one = dve.do(lambda e: e.memset(ones[:, :], 1.0))
        normed = layernorm(c, xn)
        xr = to_features(c, xn, xt, normed, banks, ring)
        sr = []
        for t in range(NT):
            b, users = ring.take()
            mm = matmuls(c, banks[b][:, 0:EXPERTS], [(xt[:, k, t * P:(t + 1) * P], gw[:, k, :])
                                                     for k in range(KC)], xr[t // 4], w, users)
            a = act.do(lambda e, t=t, b=b: e.activation(sc[:, t, :], banks[b][:, 0:EXPERTS],
                                                        ACT.Sigmoid), mm)
            ring.used(b, a)
            sr.append(dve.do(lambda e, t=t: e.tensor_tensor(sf[:, t, :], sc[:, t, :], gb[:, :], ALU.add), a))
        up_ring, y_ring, h_ring, sg_ring = Ring(2), Ring(4), Ring(AHEAD + 1), Ring(2)
        for i in range(8):
            (up_ring.used(i // 2, ring.users[i]) if i < 4 else y_ring.used(i - 4, ring.users[i]))
        w_done = []

        def choose():
            for t in range(NT):
                for gr in range(GROUPS):
                    a = dve.do(lambda e, t=t, gr=gr: e.max(
                        srt[:, t, gr, :], sf[:, t, gr * GE:(gr + 1) * GE]), sr[t])
                if t % 2:
                    yield
            a = dve.do(lambda e: e.tensor_tensor(gs[:, :, :], srt[:, :, :, 0], srt[:, :, :, 1], ALU.add), a)
            for t in range(NT):
                a1 = dve.do(lambda e, t=t: e.max(g8[:, t, :], gs[:, t, :]), a)
            a1 = dve.do(lambda e: e.memset(g8[:, :, TOP_GROUPS:], -OUT), a1)
            for t in range(NT):
                a2 = dve.do(lambda e, t=t: e.match_replace(
                    gm[:, t, :], g8[:, t, :], gs[:, t, :], TAKEN), a1)
            a2 = dve.do(lambda e: e.tensor_scalar(gm[:, :, :], gm[:, :, :], TAKEN / 2, OUT,
                                                  ALU.is_gt, ALU.mult), a2)
            gmb = gm[:, :, :].rearrange("p t (g o) -> p (t g) o", o=1).to_broadcast([P, NT * GROUPS, GE])
            a = dve.do(lambda e: e.tensor_tensor(
                sf[:, :, :].rearrange("p t (g j) -> p (t g) j", j=GE),
                sf[:, :, :].rearrange("p t (g j) -> p (t g) j", j=GE), gmb, ALU.add), a2)
            yield
            for t in range(NT):
                a1 = dve.do(lambda e, t=t: e.max(v8[:, t, :], sf[:, t, :]), a)
            for t in range(NT):
                a2 = dve.do(lambda e, t=t: e.match_replace(
                    pick[:, t, :], v8[:, t, :], sf[:, t, :], TAKEN), a1)
            yield
            pr = dve.do(lambda e: e.tensor_scalar(pick[:, :, :], pick[:, :, :], TAKEN / 2, None,
                                                  ALU.is_lt), a2)
            a = dve.do(lambda e: e.tensor_tensor(wt[:, :, :], sc[:, :, :], pick[:, :, :], ALU.mult), pr)
            a = dve.do(lambda e: e.tensor_reduce(den[:, 0, :].rearrange("p (t o) -> p t o", o=1),
                                                 wt[:, :, :], AX.X, ALU.add), a)
            a = dve.do(lambda e: e.tensor_scalar(den[:, 0, :], den[:, 0, :], 1e-20, None, ALU.add), a)
            a = dve.do(lambda e: e.reciprocal(den[:, 1, :], den[:, 0, :]), a)
            for t in range(NT):
                wr = dve.do(lambda e, t=t: e.tensor_scalar(wt[:, t, :], wt[:, t, :], den[:, 1, t:t + 1],
                                                          ROUTE_SCALE, ALU.mult, ALU.mult), a)
            yield
            for t in range(NT):
                b, users = y_ring.take()
                mm = matmuls(c, banks[4 + b][:, 0:EXPERTS],
                             [(ones[:, :], pick[:, j, :]) for j in range(t)] + [(upper[:, :], pick[:, t, :])],
                             pr, one, w, users)
                a = dve.do(lambda e, t=t, b=b: e.scalar_tensor_tensor(
                    wt[:, t, :], banks[4 + b][:, 0:EXPERTS], CAP + 0.5, wt[:, t, :], ALU.is_lt, ALU.mult),
                    mm, wr)
                y_ring.used(b, a)
                if t % 2:
                    yield
            w_done.append(a)
        def up(e_, half):
            i, m = loaded[e_]
            b, users = up_ring.take()
            pairs = [(wg[:, i, k, :], xt[:, k, half * 512:(half + 1) * 512]) for k in range(KC)]
            m1 = matmuls(c, banks[2 * b][:, :], pairs, m, xr, users)
            pairs = [(wu[:, i, k, :], xt[:, k, half * 512:(half + 1) * 512]) for k in range(KC)]
            m2 = matmuls(c, banks[2 * b + 1][:, :], pairs)
            s, susers = sg_ring.take()
            h, husers = h_ring.take()
            a = act.do(lambda e: e.activation(sg[:, s, :], banks[2 * b][:, :], ACT.Silu), m1, susers)
            a = dve.do(lambda e: e.tensor_tensor(hh[:, h, :], sg[:, s, :], banks[2 * b + 1][:, :],
                                                 ALU.mult), a, m2, husers)
            up_ring.used(b, a)
            sg_ring.used(s, a)
            return e_, half, h, a

        def down(e_, half, h, a):
            i, _ = loaded[e_]
            for p in range(2):
                y, users = y_ring.take()
                for j in range(2):
                    t = 4 * half + 2 * p + j
                    mm = pe.do(lambda e, j=j, y=y, t=t: e.matmul(
                        banks[4 + y][:, j * D:(j + 1) * D], hh[:, h, (t % 4) * P:(t % 4 + 1) * P],
                        wd[:, i, :], start=True, stop=True), a, users, count=(j == 1))
                for j in range(2):
                    t = 4 * half + 2 * p + j
                    s = dve.do(lambda e, j=j, y=y, t=t: e.scalar_tensor_tensor(
                        c.x[:, t, :], banks[4 + y][:, j * D:(j + 1) * D], wt[:, t, e_:e_ + 1],
                        c.x[:, t, :], ALU.mult, ALU.add), mm, w_done, acc.get(t))
                    acc[t] = s
                y_ring.used(y, s)
            h_ring.used(h, mm)
            w_ring.used(i, mm)
            if half == 1 and e_ + NW < EXPERTS:
                loaded[e_ + NW] = load(e_ + NW)
            return s
        acc = {}
        units = [(e_, half) for e_ in range(EXPERTS) for half in range(2)]
        ready = []

        def first_units():
            for unit in units[:AHEAD]:
                ready.append(up(*unit))
                yield
        run_even((choose(), 12, 0), (first_units(), AHEAD, 0))
        for unit in units[AHEAD:]:
            ready.append(up(*unit))
            down(*ready.pop(0))
        for unit in ready:
            last = down(*unit)
        c.x_ready = last


def scratch_tensors(nc):
    return {"keys": nc.dram_tensor("keys", (2 * B * (SK // 1024), 3, P, 1024), BF16, kind="Internal").ap(),
            "parked": nc.dram_tensor("parked", (P, NT, D), F32, kind="Internal").ap()}


def strip_order():
    group, strip, second, d = np.indices((2, 4, 2, 16))
    return (16 * (8 * group + strip + 4 * second) + d).reshape(-1)


def value_columns(w):
    w = np.asarray(w)
    z = np.zeros(w.shape[:-1] + (2, 2, 4, 2, 16), w.dtype)
    heads = w.reshape(w.shape[:-1] + (2, 2, 4, 16))
    for second in range(2):
        z[..., second, :, second, :] = heads[..., second, :, :]
    return np.ascontiguousarray(z.reshape(w.shape[:-1] + (2 * D,)))


def more_layout(a, o, rows, cols):
    w, b = a["L0_attn_Wqkv_w"], a["L0_attn_Wqkv_b"]
    order = strip_order()
    second = np.arange(P) // 16 % 2
    o["ca_wq"], o["ca_wk"] = (np.ascontiguousarray(w[i * D:(i + 1) * D].T[:, order]) for i in range(2))
    o["ca_wv"], o["ca_bv"] = value_columns(w[2 * D:].T), rows(value_columns(b[2 * D:]))
    o["ca_own"] = np.stack([second == 0, second == 1], 1).astype(np.float32)
    columns = [cols(b[D:2 * D][order])]
    for bias in (b[0:D], a["L0_attn_conv_b"]):
        for which in range(2):
            column = np.zeros((P, KC), bias.dtype)
            column[second == which] = cols(bias[order])[second == which]
            columns.append(column)
    o["ca_cols"] = np.ascontiguousarray(np.concatenate(columns, 1))
    cw = a["L0_attn_conv_w"].transpose(2, 1, 0)
    o["ca_cw"] = np.ascontiguousarray(cw[:, order][:, :, order])
    o["ca_wo"] = np.ascontiguousarray(a["L0_attn_out_w"].T[order])
    o["ca_bo"] = rows(a["L0_attn_out_b"])
    i, j = np.arange(P)[:, None], np.arange(2 * P)[None, :]
    o["causal"] = np.where(np.concatenate([j[:, :P] <= i, j <= i + P], 1), 0, NEG).astype(np.float32)
    f = np.float32
    o["lt_wqkv"] = a["L0_ffn_Wqkv"]
    o["lt_wo"] = a["L0_ffn_Wo"]
    w1 = np.zeros((DEPTH, D, 2, FFP), f)
    w1[..., :FF] = a["L0_ffn_W1"].reshape(DEPTH, D, 2, FF)
    o["lt_w1"] = w1.reshape(DEPTH, D, 2 * FFP)
    w2 = np.zeros((DEPTH, FFP, D), f)
    w2[:, :FF] = a["L0_ffn_W2"]
    o["lt_w2"] = w2
    b1 = np.zeros((DEPTH, 2, FFP), f)
    b1[..., :FF] = a["L0_ffn_b1"].reshape(DEPTH, 2, FF)
    o["lt_ffc"] = np.ascontiguousarray(b1.reshape(-1, P).T)
    ln = np.stack([a["L0_ffn_ln_g"], a["L0_ffn_ln_b"]], 1)
    o["lt_lnc"] = np.ascontiguousarray(ln.reshape(-1, P).T)
    o["lt_b2"] = np.ascontiguousarray(np.broadcast_to(a["L0_ffn_b2"][:, None], (DEPTH, P, D)))
    qs, ks = a["L0_ffn_q_scale"], a["L0_ffn_k_scale"]
    scl = np.stack([qs, np.roll(qs, 32, 1), ks, np.roll(ks, 32, 1)], 1).reshape(DEPTH, 1, 4 * LH)
    o["lt_scl"] = np.ascontiguousarray(np.broadcast_to(scl, (DEPTH, P, 4 * LH)))
    half = np.arange(0, LH, 2, dtype=f)
    t = np.arange(S, dtype=f)
    freqs = t[:, None] * (f(1) / f(10000) ** (half / f(LH)))[None, :]
    base = (half + f(0.4 * LH)) / f(1.4 * LH)
    scale = base[None, :] ** ((t - S // 2) / f(32))[:, None]
    cos, sin = np.cos(freqs), np.sin(freqs)
    two = lambda p, q: np.concatenate([p, q], 1)
    rot = np.stack([two(cos * scale, cos * scale), two(-sin * scale, sin * scale),
                    two(cos / scale, cos / scale), two(-sin / scale, sin / scale)])
    o["lt_rot"] = np.ascontiguousarray(
        rot.reshape(4, 2, P, LH).transpose(2, 0, 1, 3).reshape(P, -1).astype(f))
    band = np.concatenate([(j[:, :P] <= i) & (j[:, :P] >= i - WINDOW),
                           ((j <= i + P) & (j >= i + P - WINDOW))[:, WINDOW:]], 1)
    o["band"] = np.where(band, 0, NEG).astype(f)
    o["gla_taps"] = np.ascontiguousarray(
        a["L1_attn_conv_w"].reshape(KC, P, TAPS).transpose(1, 0, 2).reshape(P, -1))
    o["gla_win"] = np.ascontiguousarray(np.concatenate(
        [a[f"L1_attn_W{n}"] for n in ("q", "kg", "v", "g")], 1))
    o["gla_wout"] = a["L1_attn_Wout"]
    o["gla_bg"] = rows(a["L1_attn_bg"])
    o["gla_aug"] = rows(a["L1_attn_aug_balance"])
    o["moe_gw"] = np.ascontiguousarray(a["L1_ffn_gate_w"].T)
    o["moe_gb"] = rows(a["L1_ffn_gate_bias"])
    o["moe_wg"], o["moe_wu"], o["moe_wd"] = (a[f"L1_ffn_w_{n}"] for n in ("gate", "up", "down"))
    o["upper"] = np.triu(np.ones((P, P), np.float32))


def build(nc, ins, out, scratch, first=0, last=5):
    with ExitStack() as ctx:
        c = Core(nc, ctx)
        sb = lambda n, shape, dt=F32: ctx.enter_context(nc.sbuf_tensor(n, shape, dt))
        c.x = sb("x_sb", [P, NT, D])
        c.parked = scratch["parked"]
        c.minus_half = sb("minus_half", [P, 64])
        c.ident = sb("ident", [P, P])
        c.ident_bf = sb("ident_bf", [P, P], BF16)
        c.stage("load")
        s = c.slot("load")
        c.sp.dma(s, c.x[:, :, :], ins["x"].rearrange("b (q p) d -> p (b q) d", p=P))
        m = c.sp.dma(s, c.ident[:, :], ins["ident"])
        half = c.dve.do(lambda e: e.memset(c.minus_half[:, :], -0.5))
        c.stats, c.mean_var = sb("stats", [P, NT, 6]), sb("mean_var", [P, NT, 2])
        c.rstd = sb("rstd", [P, 2, NT])
        c.x_ready = [m, half]
        token_stats(c, range(NT), c.x_ready)
        c.ident_ready = c.dve.do(lambda e: e.tensor_copy(c.ident_bf[:, :], c.ident[:, :]), m)
        g = ins.get
        for i in range(first, last + 1):
            STAGES[i](c, g, scratch)
        c.stage("store")
        s = c.slot("store")
        m = c.sp.dma(s, out.rearrange("b (q p) d -> p (b q) d", p=P), c.x[:, :, :])
        c.sp.hold(m)
        with nc.Block() as block:
            block.sync(lambda e: c.sp.replay(e))
            block.gpsimd(lambda e: c.pool.replay(e))
            block.scalar(lambda e: c.act.replay(e))
            block.vector(lambda e: c.dve.replay(e))
            block.tensor(lambda e: c.pe.replay(e))


STAGES = [
    lambda c, g, d: cross_attention(c, "xa0", g("ctx_t"), g("xa0_wq"), g("xa0_wk"), g("xa0_wv"), g("xa0_wo"),
                                 g("xa0_bq"), g("xa0_bk"), g("xa0_bv"), g("xa0_bo"), d["keys"]),
    lambda c, g, d: conv_attention(c, "ca", g),
    lambda c, g, d: local_transformer(c, "lt", g),
    lambda c, g, d: cross_attention(c, "xa1", g("ctx_t"), g("xa1_wq"), g("xa1_wk"), g("xa1_wv"), g("xa1_wo"),
                                 None, None, None, g("xa1_bo"), d["keys"]),
    lambda c, g, d: gated_linear_attention(c, "gla", g),
    lambda c, g, d: experts(c, "moe", g),
]


def layout(inputs):
    a = {k: np.asarray(v) for k, v in inputs.items()}

    def rows(v):
        return np.ascontiguousarray(np.broadcast_to(v, (P, v.shape[-1])))

    def cols(v):
        return np.ascontiguousarray(v.reshape(-1, P).T)

    o = {"x": a["x"], "ident": np.eye(P, dtype=np.float32)}
    o["ctx_t"] = np.ascontiguousarray(a["ctx_1024"].transpose(0, 2, 1))
    for n in "qkvo":
        o[f"xa0_w{n}"] = np.ascontiguousarray(a[f"L0_xattn_w_{n}"].T)
        o[f"xa1_w{n}"] = np.ascontiguousarray(a[f"L1_xattn_W{n}"].T)
    for n in "qvo":
        o[f"xa0_b{n}"] = rows(a[f"L0_xattn_b_{n}"])
    o["xa0_bk"] = cols(a["L0_xattn_b_k"])
    o["xa1_bo"] = rows(a["L1_xattn_bo"])
    more_layout(a, o, rows, cols)
    return o


def kernel(**inputs):
    import concourse.bacc as bacc
    from concourse.bass_utils import run_bass_kernel_spmd

    nc = bacc.Bacc("TRN2", target_bir_lowering=False, num_devices=1)
    arrays = layout(inputs)
    ins = {k: nc.dram_tensor(f"in_{k}", v.shape, mybir.dt.from_np(v.dtype), kind="ExternalInput").ap()
           for k, v in arrays.items()}
    out = nc.dram_tensor("result", (B, S, D), F32, kind="ExternalOutput").ap()
    build(nc, ins, out, scratch_tensors(nc))
    r = run_bass_kernel_spmd(nc, [{f"in_{k}": v for k, v in arrays.items()}], core_ids=[0])
    return r.results[0]["result"]
```
